# Optimizing a Trainium2 kernel written in Bass

```python
import numpy as np
import jax
import jax.numpy as jnp

def _softmax(x, axis=-1):
    return jax.nn.softmax(x, axis=axis)

def _gelu(x):
    return jax.nn.gelu(x, approximate=True)

def _silu(x):
    return jax.nn.silu(x)

def _sigmoid(x):
    return jax.nn.sigmoid(x)

def _layernorm(x, axis=-1, eps=1e-05):
    m = jnp.mean(x, axis=axis, keepdims=True)
    v = jnp.var(x, axis=axis, keepdims=True)
    return (x - m) / jnp.sqrt(v + eps)

def _scatter_add(tgt, idx, src, axis=0):
    return tgt.at[idx].add(src)

def _segment_sum(src, seg, n):
    return jax.ops.segment_sum(src, seg, n)
kernel_name = 'mk_xattn_ffn_d4_seqx_r8_d6fe4b'

def setup_inputs(seed: int=0):
    np.random.seed(seed)
    _w = jnp.asarray

    def _rec_inputs():
        import jax
        import jax.numpy as jnp
        _rk = jax.random.key(seed)
        x = 2.818e-05 + 1 * jax.random.normal(jax.random.fold_in(_rk, 1), (16, 56, 128), jnp.float32)
        _lenS = 56 - jax.random.randint(jax.random.fold_in(_rk, 7), (16,), 0, max(1, 56 // 4) + 1, jnp.int32)
        _lenS2 = 1500 - jax.random.randint(jax.random.fold_in(_rk, 8), (16,), 0, max(1, 1500 // 4) + 1, jnp.int32)
        _ctx_1024P = jax.random.normal(jax.random.fold_in(_rk, 11), (16, 16, 128), jnp.float32)
        _ctx_1024c = jax.random.dirichlet(jax.random.fold_in(_rk, 511), 0.3 * jnp.ones((16,), jnp.float32), (16, 1500))
        _ctx_1024t = jnp.einsum('bsk,bkd->bsd', _ctx_1024c, _ctx_1024P)
        _ctx_1024t = _ctx_1024t * jax.lax.rsqrt(jnp.mean(jnp.square(_ctx_1024t)) + 1e-12) * 0.953939
        ctx_1024 = -0.000392918 + 0.999932 * (_ctx_1024t + 0.3 * jax.random.normal(jax.random.fold_in(_rk, 611), (16, 1500, 128), jnp.float32))
        _validS = jnp.arange(56)[None, :] < _lenS[:, None]
        _validS2 = jnp.arange(1500)[None, :] < _lenS2[:, None]
        _causal = jnp.tril(jnp.ones((56, 56), dtype=bool))
        mask_BxS2_bk0 = jnp.logical_not(jnp.broadcast_to(_validS2[:, :], (16, 1500)))
        return (x, ctx_1024, mask_BxS2_bk0)
    x, ctx_1024, mask_BxS2_bk0 = _rec_inputs()

    def _L0_xattn_setup():
        import jax, jax.numpy as jnp
        import numpy as np
        B, L, D = (8, 256, 128)
        key = jax.random.key(seed)
        k1, k2, k3 = jax.random.split(key, 3)
        enc_outputs = jax.random.normal(k1, (B, L, D), dtype=jnp.float32)
        x = jax.random.normal(k2, (B, L, D), dtype=jnp.float32)
        Wq = jax.random.normal(k3, (D, D), dtype=jnp.float32) * (1.0 / np.sqrt(D))
        return {'enc_outputs': enc_outputs, 'x': x, 'Wq': Wq}
    _L0_xattn_all = _L0_xattn_setup()
    _L0_xattn_in = {k: v for k, v in _L0_xattn_all.items() if k in ('Wq',)}
    del _L0_xattn_all

    def _L0_ffn_setup():
        import jax, jax.numpy as jnp
        import numpy as np
        B, T, D, F, E, K = (2, 256, 128, 512, 8, 2)
        key = jax.random.key(seed)
        ks = jax.random.split(key, 7)
        s_d = 1.0 / np.sqrt(D)
        s_f = 1.0 / np.sqrt(F)
        return {'x': jax.random.normal(ks[0], (B, T, D), dtype=jnp.float32), 'Wg': jax.random.uniform(ks[1], (D, E), jnp.float32, -s_d, s_d), 'bg': jnp.zeros((E,), jnp.float32), 'W1': jax.random.uniform(ks[2], (E, D, F), jnp.float32, -s_d, s_d), 'b1': jax.random.uniform(ks[3], (E, F), jnp.float32, -s_d, s_d), 'W2': jax.random.uniform(ks[4], (E, F, D), jnp.float32, -s_f, s_f), 'b2': jax.random.uniform(ks[5], (E, D), jnp.float32, -s_f, s_f)}
    _L0_ffn_all = _L0_ffn_setup()
    _L0_ffn_in = {k: v for k, v in _L0_ffn_all.items() if k in ('Wg', 'bg', 'W1', 'b1', 'W2', 'b2')}
    del _L0_ffn_all

    def _L1_xattn_setup():
        import jax, jax.numpy as jnp
        import numpy as np
        E = 128
        NUM_HEADS = 16
        DK = E // NUM_HEADS
        EPS = 1e-05
        NEG_INF = -jnp.inf

        def layer_norm(x, g, b):
            mu = jnp.mean(x, axis=-1, keepdims=True)
            var = jnp.var(x, axis=-1, keepdims=True)
            return (x - mu) * jax.lax.rsqrt(var + EPS) * g + b

        def self_attn(x, Wq, Wk, Wv):
            Q, K, V = (x @ Wq, x @ Wk, x @ Wv)
            energy = jnp.einsum('bqd,bkd->bqk', Q, K)
            S = energy.shape[-1]
            lengths = jnp.sum(energy[:, 0] != 0, axis=-1)
            kidx = jnp.arange(S)
            pad = kidx[None, None, :] >= lengths[:, None, None]
            causal = kidx[None, :] < kidx[:, None]
            causal = (kidx[None, :] > kidx[:, None])[None]
            energy = jnp.where(pad | causal, NEG_INF, energy)
            score = jax.nn.softmax(energy / np.sqrt(DK), axis=-1)
            return jnp.einsum('bqk,bkd->bqd', score, V)

        def cross_attn(x, context, Wq, Wk, Wv):
            Q = x @ Wq
            K, V = (context @ Wk, context @ Wv)
            energy = jnp.einsum('bqd,bkd->bqk', Q, K)
            Sk = energy.shape[-1]
            lengths = jnp.sum(energy[:, 0] != 0, axis=-1)
            kidx = jnp.arange(Sk)
            pad = kidx[None, None, :] >= lengths[:, None, None]
            energy = jnp.where(pad, NEG_INF, energy)
            score = jax.nn.softmax(energy / np.sqrt(DK), axis=-1)
            return jnp.einsum('bqk,bkd->bqd', score, V)
        key = jax.random.key(seed)
        ks = jax.random.split(key, 12)
        B, S = (8, 256)
        s = 1.0 / np.sqrt(E)
        inp = {'x': jax.random.normal(ks[0], (B, S, E), jnp.float32), 'context': jax.random.normal(ks[1], (B, S, E), jnp.float32), 'Wq1': jax.random.normal(ks[2], (E, E), jnp.float32) * s, 'Wk1': jax.random.normal(ks[3], (E, E), jnp.float32) * s, 'Wv1': jax.random.normal(ks[4], (E, E), jnp.float32) * s, 'Wq2': jax.random.normal(ks[5], (E, E), jnp.float32) * s, 'Wk2': jax.random.normal(ks[6], (E, E), jnp.float32) * s, 'Wv2': jax.random.normal(ks[7], (E, E), jnp.float32) * s, 'fc1_w': jax.random.normal(ks[8], (E, E), jnp.float32) * s, 'fc1_b': jnp.zeros((E,), jnp.float32), 'fc2_w': jax.random.normal(ks[9], (E, E), jnp.float32) * s, 'fc2_b': jnp.zeros((E,), jnp.float32), 'ln1_g': jnp.ones((E,), jnp.float32), 'ln1_b': jnp.zeros((E,), jnp.float32), 'ln2_g': jnp.ones((E,), jnp.float32), 'ln2_b': jnp.zeros((E,), jnp.float32), 'ln3_g': jnp.ones((E,), jnp.float32), 'ln3_b': jnp.zeros((E,), jnp.float32)}
        return inp
    _L1_xattn_all = _L1_xattn_setup()
    _L1_xattn_in = {k: v for k, v in _L1_xattn_all.items() if k in ('Wq1', 'Wk1', 'Wv1', 'Wq2', 'Wk2', 'Wv2', 'fc1_w', 'fc1_b', 'fc2_w', 'fc2_b', 'ln1_g', 'ln1_b', 'ln2_g', 'ln2_b', 'ln3_g', 'ln3_b')}
    del _L1_xattn_all

    def _L1_ffn_setup():
        import jax, jax.numpy as jnp
        import numpy as np
        BLOCK = 32
        W_BITS = 4
        ACT_BITS = 16

        def act_qdq(x):
            qmax = 2.0 ** (ACT_BITS - 1) - 1.0
            scale = jnp.maximum(jnp.max(jnp.abs(x)) / qmax, 1e-12)
            return jnp.clip(jnp.round(x / scale), -qmax - 1.0, qmax) * scale

        def fixed_qdq_u16(x):
            scale = 1.0 / 65536.0
            return jnp.clip(jnp.round(x / scale), 0.0, 65535.0) * scale

        def lpbq_dequant(w):
            O, I = w.shape
            qmax = 2.0 ** (W_BITS - 1) - 1.0
            wb = w.reshape(O, I // BLOCK, BLOCK)
            s = jnp.maximum(jnp.max(jnp.abs(wb), axis=-1, keepdims=True) / qmax, 1e-12)
            wq = jnp.clip(jnp.round(wb / s), -qmax - 1.0, qmax) * s
            return wq.reshape(O, I)
        key = jax.random.key(seed)
        k1, k2, k3, k4 = jax.random.split(key, 4)
        B, S, H, I = (2, 512, 128, 384)
        x = jax.random.normal(k1, (B, S, H), jnp.float32)
        w_gate = jax.random.normal(k2, (I, H), jnp.float32) * 0.02
        w_up = jax.random.normal(k3, (I, H), jnp.float32) * 0.02
        w_down = jax.random.normal(k4, (H, I), jnp.float32) * 0.02
        return {'x': x, 'w_gate': w_gate, 'w_up': w_up, 'w_down': w_down}
    _L1_ffn_all = _L1_ffn_setup()
    _L1_ffn_in = {k: v for k, v in _L1_ffn_all.items() if k in ('w_gate', 'w_up', 'w_down')}
    del _L1_ffn_all

    def _L2_xattn_setup():
        import jax, jax.numpy as jnp
        import numpy as np
        IN_FEATURES = 128
        NUM_HEAD = 16
        DIM = 64
        B, S = (2, 256)
        EPS = 1e-05
        key = jax.random.key(seed)
        ks = jax.random.split(key, 10)
        hd = NUM_HEAD * DIM
        scale_in = 1.0 / np.sqrt(IN_FEATURES)
        scale_cat = 1.0 / np.sqrt(IN_FEATURES + hd)
        return {'query': jax.random.normal(ks[0], (B, S, IN_FEATURES), jnp.float32), 'value': jax.random.normal(ks[1], (B, S, IN_FEATURES), jnp.float32), 'Wq': jax.random.uniform(ks[2], (IN_FEATURES, hd), jnp.float32, -scale_in, scale_in), 'bq': jax.random.uniform(ks[3], (hd,), jnp.float32, -scale_in, scale_in), 'Wv': jax.random.uniform(ks[4], (IN_FEATURES, hd), jnp.float32, -scale_in, scale_in), 'bv': jax.random.uniform(ks[5], (hd,), jnp.float32, -scale_in, scale_in), 'Wfc': jax.random.uniform(ks[6], (IN_FEATURES + hd, IN_FEATURES), jnp.float32, -scale_cat, scale_cat), 'bfc': jax.random.uniform(ks[7], (IN_FEATURES,), jnp.float32, -scale_cat, scale_cat), 'gamma': jnp.ones((IN_FEATURES,), jnp.float32), 'beta': jnp.zeros((IN_FEATURES,), jnp.float32)}
    _L2_xattn_all = _L2_xattn_setup()
    _L2_xattn_in = {k: v for k, v in _L2_xattn_all.items() if k in ('Wq', 'bq', 'Wv', 'bv', 'Wfc', 'bfc', 'gamma', 'beta')}
    del _L2_xattn_all

    def _L2_ffn_setup():
        import jax, jax.numpy as jnp
        import numpy as np
        D_MODEL = 128
        M = 64
        INNER = 16
        key = jax.random.key(seed)
        ks = jax.random.split(key, 9)

        def init(k, shape, fan_in):
            bound = 1.0 / np.sqrt(fan_in)
            return jax.random.uniform(k, shape, jnp.float32, -bound, bound)
        x = jax.random.normal(ks[0], (16, 512, D_MODEL), dtype=jnp.float32)
        Win = init(ks[1], (D_MODEL, M), D_MODEL)
        bin_ = init(ks[2], (M,), D_MODEL)
        W1 = init(ks[3], (M, INNER), 1)
        b1 = init(ks[4], (M, INNER), 1)
        W2 = init(ks[5], (M, INNER), INNER)
        b2 = init(ks[6], (M,), INNER)
        Wout = init(ks[7], (M, D_MODEL), M)
        bout = init(ks[8], (D_MODEL,), M)
        return {'x': x, 'Win': Win, 'bin_': bin_, 'W1': W1, 'b1': b1, 'W2': W2, 'b2': b2, 'Wout': Wout, 'bout': bout}
    _L2_ffn_all = _L2_ffn_setup()
    _L2_ffn_in = {k: v for k, v in _L2_ffn_all.items() if k in ('Win', 'bin_', 'W1', 'b1', 'W2', 'b2', 'Wout', 'bout')}
    del _L2_ffn_all

    def _L3_xattn_setup():
        import jax, jax.numpy as jnp
        import numpy as np
        D_MODEL = 128
        N_HEAD = 16
        D_H = D_MODEL // N_HEAD
        key = jax.random.key(seed)
        ks = jax.random.split(key, 12)
        B, LQ, LK = (4, 128, 256)
        s = 1.0 / np.sqrt(D_MODEL)
        inp = {'q_input': jax.random.normal(ks[0], (B, LQ, D_MODEL), jnp.float32), 'kv_input': jax.random.normal(ks[1], (B, LK, D_MODEL), jnp.float32), 'key_padding_mask': jax.random.randint(ks[2], (B, LK), 0, 2) > 0, 'W_Q': jax.random.normal(ks[3], (D_MODEL, D_MODEL), jnp.float32) * s, 'b_Q': jnp.zeros((D_MODEL,), jnp.float32), 'W_K': jax.random.normal(ks[4], (D_MODEL, D_MODEL), jnp.float32) * s, 'b_K': jnp.zeros((D_MODEL,), jnp.float32), 'W_V': jax.random.normal(ks[5], (D_MODEL, D_MODEL), jnp.float32) * s, 'b_V': jnp.zeros((D_MODEL,), jnp.float32), 'W_O': jax.random.normal(ks[6], (D_MODEL, D_MODEL), jnp.float32) * s, 'b_O': jnp.zeros((D_MODEL,), jnp.float32)}
        return inp
    _L3_xattn_all = _L3_xattn_setup()
    _L3_xattn_in = {k: v for k, v in _L3_xattn_all.items() if k in ('W_Q', 'b_Q', 'W_K', 'b_K', 'W_V', 'b_V', 'W_O', 'b_O')}
    del _L3_xattn_all

    def _L3_ffn_setup():
        import jax, jax.numpy as jnp
        import numpy as np
        D_MODEL = 128
        D_FF = 512
        N_EXPERTS = 8
        TOP_K = 2
        LN_EPS = 1e-06

        def _moe(x, router_w, w1, b1, w2, b2, gamma, beta):
            B, S, D = x.shape
            x_flat = x.reshape(-1, D)
            N = x_flat.shape[0]
            logits = x_flat @ router_w
            gate_vals, gate_idx = jax.lax.top_k(logits, TOP_K)
            gate_w = jax.nn.softmax(gate_vals, axis=-1)
            gates = jnp.zeros_like(logits).at[jnp.arange(N)[:, None], gate_idx].set(gate_w)
            h = jax.nn.gelu(jnp.einsum('nd,edf->enf', x_flat, w1) + b1[:, None, :], approximate=False)
            out = jnp.einsum('enf,efd->end', h, w2) + b2[:, None, :]
            res = x_flat[None, :, :] + out
            mu = jnp.mean(res, axis=-1, keepdims=True)
            var = jnp.mean(jnp.square(res - mu), axis=-1, keepdims=True)
            normed = (res - mu) * jax.lax.rsqrt(var + LN_EPS)
            expert_out = normed * gamma[:, None, :] + beta[:, None, :]
            y = jnp.einsum('end,ne->nd', expert_out, gates)
            return y.reshape(B, S, D)
        key = jax.random.key(seed)
        ks = jax.random.split(key, 8)
        x = jax.random.normal(ks[0], (2, 256, D_MODEL), dtype=jnp.float32)
        router_w = jax.random.normal(ks[1], (D_MODEL, N_EXPERTS), dtype=jnp.float32) * 0.02
        w1 = jax.random.normal(ks[2], (N_EXPERTS, D_MODEL, D_FF), dtype=jnp.float32) * 0.02
        b1 = jnp.zeros((N_EXPERTS, D_FF), dtype=jnp.float32)
        w2 = jax.random.normal(ks[3], (N_EXPERTS, D_FF, D_MODEL), dtype=jnp.float32) * 0.02
        b2 = jnp.zeros((N_EXPERTS, D_MODEL), dtype=jnp.float32)
        gamma = jnp.ones((N_EXPERTS, D_MODEL), dtype=jnp.float32)
        beta = jnp.zeros((N_EXPERTS, D_MODEL), dtype=jnp.float32)
        return {'x': x, 'router_w': router_w, 'w1': w1, 'b1': b1, 'w2': w2, 'b2': b2, 'gamma': gamma, 'beta': beta}
    _L3_ffn_all = _L3_ffn_setup()
    _L3_ffn_in = {k: v for k, v in _L3_ffn_all.items() if k in ('router_w', 'w1', 'b1', 'w2', 'b2', 'gamma', 'beta')}
    del _L3_ffn_all
    return {'x': x, 'ctx_1024': ctx_1024, 'mask_BxS2_bk0': mask_BxS2_bk0, 'L0_xattn_Wq': _L0_xattn_in['Wq'], 'L0_ffn_Wg': _L0_ffn_in['Wg'], 'L0_ffn_bg': _L0_ffn_in['bg'], 'L0_ffn_W1': _L0_ffn_in['W1'], 'L0_ffn_b1': _L0_ffn_in['b1'], 'L0_ffn_W2': _L0_ffn_in['W2'], 'L0_ffn_b2': _L0_ffn_in['b2'], 'L1_xattn_Wq1': _L1_xattn_in['Wq1'], 'L1_xattn_Wk1': _L1_xattn_in['Wk1'], 'L1_xattn_Wv1': _L1_xattn_in['Wv1'], 'L1_xattn_Wq2': _L1_xattn_in['Wq2'], 'L1_xattn_Wk2': _L1_xattn_in['Wk2'], 'L1_xattn_Wv2': _L1_xattn_in['Wv2'], 'L1_xattn_fc1_w': _L1_xattn_in['fc1_w'], 'L1_xattn_fc1_b': _L1_xattn_in['fc1_b'], 'L1_xattn_fc2_w': _L1_xattn_in['fc2_w'], 'L1_xattn_fc2_b': _L1_xattn_in['fc2_b'], 'L1_xattn_ln1_g': _L1_xattn_in['ln1_g'], 'L1_xattn_ln1_b': _L1_xattn_in['ln1_b'], 'L1_xattn_ln2_g': _L1_xattn_in['ln2_g'], 'L1_xattn_ln2_b': _L1_xattn_in['ln2_b'], 'L1_xattn_ln3_g': _L1_xattn_in['ln3_g'], 'L1_xattn_ln3_b': _L1_xattn_in['ln3_b'], 'L1_ffn_w_gate': _L1_ffn_in['w_gate'], 'L1_ffn_w_up': _L1_ffn_in['w_up'], 'L1_ffn_w_down': _L1_ffn_in['w_down'], 'L2_xattn_Wq': _L2_xattn_in['Wq'], 'L2_xattn_bq': _L2_xattn_in['bq'], 'L2_xattn_Wv': _L2_xattn_in['Wv'], 'L2_xattn_bv': _L2_xattn_in['bv'], 'L2_xattn_Wfc': _L2_xattn_in['Wfc'], 'L2_xattn_bfc': _L2_xattn_in['bfc'], 'L2_xattn_gamma': _L2_xattn_in['gamma'], 'L2_xattn_beta': _L2_xattn_in['beta'], 'L2_ffn_Win': _L2_ffn_in['Win'], 'L2_ffn_bin_': _L2_ffn_in['bin_'], 'L2_ffn_W1': _L2_ffn_in['W1'], 'L2_ffn_b1': _L2_ffn_in['b1'], 'L2_ffn_W2': _L2_ffn_in['W2'], 'L2_ffn_b2': _L2_ffn_in['b2'], 'L2_ffn_Wout': _L2_ffn_in['Wout'], 'L2_ffn_bout': _L2_ffn_in['bout'], 'L3_xattn_W_Q': _L3_xattn_in['W_Q'], 'L3_xattn_b_Q': _L3_xattn_in['b_Q'], 'L3_xattn_W_K': _L3_xattn_in['W_K'], 'L3_xattn_b_K': _L3_xattn_in['b_K'], 'L3_xattn_W_V': _L3_xattn_in['W_V'], 'L3_xattn_b_V': _L3_xattn_in['b_V'], 'L3_xattn_W_O': _L3_xattn_in['W_O'], 'L3_xattn_b_O': _L3_xattn_in['b_O'], 'L3_ffn_router_w': _L3_ffn_in['router_w'], 'L3_ffn_w1': _L3_ffn_in['w1'], 'L3_ffn_b1': _L3_ffn_in['b1'], 'L3_ffn_w2': _L3_ffn_in['w2'], 'L3_ffn_b2': _L3_ffn_in['b2'], 'L3_ffn_gamma': _L3_ffn_in['gamma'], 'L3_ffn_beta': _L3_ffn_in['beta']}

def reference(x, ctx_1024, mask_BxS2_bk0, L0_xattn_Wq, L0_ffn_Wg, L0_ffn_bg, L0_ffn_W1, L0_ffn_b1, L0_ffn_W2, L0_ffn_b2, L1_xattn_Wq1, L1_xattn_Wk1, L1_xattn_Wv1, L1_xattn_Wq2, L1_xattn_Wk2, L1_xattn_Wv2, L1_xattn_fc1_w, L1_xattn_fc1_b, L1_xattn_fc2_w, L1_xattn_fc2_b, L1_xattn_ln1_g, L1_xattn_ln1_b, L1_xattn_ln2_g, L1_xattn_ln2_b, L1_xattn_ln3_g, L1_xattn_ln3_b, L1_ffn_w_gate, L1_ffn_w_up, L1_ffn_w_down, L2_xattn_Wq, L2_xattn_bq, L2_xattn_Wv, L2_xattn_bv, L2_xattn_Wfc, L2_xattn_bfc, L2_xattn_gamma, L2_xattn_beta, L2_ffn_Win, L2_ffn_bin_, L2_ffn_W1, L2_ffn_b1, L2_ffn_W2, L2_ffn_b2, L2_ffn_Wout, L2_ffn_bout, L3_xattn_W_Q, L3_xattn_b_Q, L3_xattn_W_K, L3_xattn_b_K, L3_xattn_W_V, L3_xattn_b_V, L3_xattn_W_O, L3_xattn_b_O, L3_ffn_router_w, L3_ffn_w1, L3_ffn_b1, L3_ffn_w2, L3_ffn_b2, L3_ffn_gamma, L3_ffn_beta):
    import jax
    import jax.numpy as jnp

    def _L0_xattn_ref(enc_outputs, x, Wq):
        import jax, jax.numpy as jnp
        import numpy as np
        B, L, D = (8, 256, 128)
        d_k = x.shape[-1]
        q = jnp.einsum('bld,hd->blh', x, Wq)
        k = jnp.einsum('bld,hd->blh', enc_outputs, Wq)
        v = k
        scores = jnp.einsum('bqh,bkh->bqk', q, k) / jnp.sqrt(jnp.float32(d_k))
        Lq, Lk = (scores.shape[1], scores.shape[2])
        causal = jnp.tril(jnp.ones((Lq, Lk), dtype=bool))
        scores = jnp.where(causal, scores, -jnp.inf)
        attn = jax.nn.softmax(scores, axis=-1)
        return jnp.einsum('bqk,bkh->bqh', attn, v)

    def _L0_ffn_ref(x, Wg, bg, W1, b1, W2, b2):
        import jax, jax.numpy as jnp
        import numpy as np
        B, T, D, F, E, K = (2, 256, 128, 512, 8, 2)
        logits = jnp.einsum('btd,de->bte', x, Wg) + bg
        scores = jax.nn.softmax(logits, axis=-1)
        topk_vals, topk_idx = jax.lax.top_k(scores, K)
        w = jnp.sum(jax.nn.one_hot(topk_idx, E, dtype=x.dtype) * topk_vals[..., None], axis=-2)
        out = jnp.zeros_like(x)
        for e in range(E):
            h = jax.nn.gelu(jnp.einsum('btd,df->btf', x, W1[e]) + b1[e], approximate=False)
            y = jnp.einsum('btf,fd->btd', h, W2[e]) + b2[e]
            out = out + y * w[..., e, None]
        return out

    def _L1_xattn_ref(x, context, Wq1, Wk1, Wv1, Wq2, Wk2, Wv2, fc1_w, fc1_b, fc2_w, fc2_b, ln1_g, ln1_b, ln2_g, ln2_b, ln3_g, ln3_b):
        import jax, jax.numpy as jnp
        import numpy as np
        E = 128
        NUM_HEADS = 16
        DK = E // NUM_HEADS
        EPS = 1e-05
        NEG_INF = -jnp.inf

        def layer_norm(x, g, b):
            mu = jnp.mean(x, axis=-1, keepdims=True)
            var = jnp.var(x, axis=-1, keepdims=True)
            return (x - mu) * jax.lax.rsqrt(var + EPS) * g + b

        def self_attn(x, Wq, Wk, Wv):
            Q, K, V = (x @ Wq, x @ Wk, x @ Wv)
            energy = jnp.einsum('bqd,bkd->bqk', Q, K)
            S = energy.shape[-1]
            lengths = jnp.sum(energy[:, 0] != 0, axis=-1)
            kidx = jnp.arange(S)
            pad = kidx[None, None, :] >= lengths[:, None, None]
            causal = kidx[None, :] < kidx[:, None]
            causal = (kidx[None, :] > kidx[:, None])[None]
            energy = jnp.where(pad | causal, NEG_INF, energy)
            score = jax.nn.softmax(energy / np.sqrt(DK), axis=-1)
            return jnp.einsum('bqk,bkd->bqd', score, V)

        def cross_attn(x, context, Wq, Wk, Wv):
            Q = x @ Wq
            K, V = (context @ Wk, context @ Wv)
            energy = jnp.einsum('bqd,bkd->bqk', Q, K)
            Sk = energy.shape[-1]
            lengths = jnp.sum(energy[:, 0] != 0, axis=-1)
            kidx = jnp.arange(Sk)
            pad = kidx[None, None, :] >= lengths[:, None, None]
            energy = jnp.where(pad, NEG_INF, energy)
            score = jax.nn.softmax(energy / np.sqrt(DK), axis=-1)
            return jnp.einsum('bqk,bkd->bqd', score, V)
        z = self_attn(x, Wq1, Wk1, Wv1)
        x = layer_norm(x + z, ln1_g, ln1_b)
        z = cross_attn(x, context, Wq2, Wk2, Wv2)
        x = layer_norm(x + z, ln2_g, ln2_b)
        z = jax.nn.relu(x @ fc1_w + fc1_b)
        z = z @ fc2_w + fc2_b
        return layer_norm(x + z, ln3_g, ln3_b)

    def _L1_ffn_ref(x, w_gate, w_up, w_down):
        import jax, jax.numpy as jnp
        import numpy as np
        BLOCK = 32
        W_BITS = 4
        ACT_BITS = 16

        def act_qdq(x):
            qmax = 2.0 ** (ACT_BITS - 1) - 1.0
            scale = jnp.maximum(jnp.max(jnp.abs(x)) / qmax, 1e-12)
            return jnp.clip(jnp.round(x / scale), -qmax - 1.0, qmax) * scale

        def fixed_qdq_u16(x):
            scale = 1.0 / 65536.0
            return jnp.clip(jnp.round(x / scale), 0.0, 65535.0) * scale

        def lpbq_dequant(w):
            O, I = w.shape
            qmax = 2.0 ** (W_BITS - 1) - 1.0
            wb = w.reshape(O, I // BLOCK, BLOCK)
            s = jnp.maximum(jnp.max(jnp.abs(wb), axis=-1, keepdims=True) / qmax, 1e-12)
            wq = jnp.clip(jnp.round(wb / s), -qmax - 1.0, qmax) * s
            return wq.reshape(O, I)
        x = act_qdq(x)
        up = act_qdq(x @ lpbq_dequant(w_up).T)
        gate = act_qdq(x @ lpbq_dequant(w_gate).T)
        sig = fixed_qdq_u16(jax.nn.sigmoid(gate))
        gate = act_qdq(gate * sig)
        o = act_qdq(gate * up)
        return o @ lpbq_dequant(w_down).T

    def _L2_xattn_ref(query, value, Wq, bq, Wv, bv, Wfc, bfc, gamma, beta):
        import jax, jax.numpy as jnp
        import numpy as np
        IN_FEATURES = 128
        NUM_HEAD = 16
        DIM = 64
        B, S = (2, 256)
        EPS = 1e-05
        Bq, Sq, _ = query.shape
        q = (query @ Wq + bq).reshape(Bq, Sq, NUM_HEAD, DIM)
        v = (value @ Wv + bv).reshape(value.shape[0], value.shape[1], NUM_HEAD, DIM)
        score = jnp.einsum('bqhd,bkhd->bhqk', q, v) / np.sqrt(DIM)
        align = jax.nn.softmax(score, axis=-1)
        context = jnp.einsum('bhqk,bkhd->bqhd', align, v)
        context = context.reshape(Bq, Sq, NUM_HEAD * DIM)
        combined = jnp.concatenate([context, query], axis=2)
        out = combined @ Wfc + bfc
        mu = jnp.mean(out, axis=-1, keepdims=True)
        var = jnp.var(out, axis=-1, keepdims=True)
        out = (out - mu) / jnp.sqrt(var + EPS) * gamma + beta
        return out

    def _L2_ffn_ref(x, Win, bin_, W1, b1, W2, b2, Wout, bout):
        import jax, jax.numpy as jnp
        import numpy as np
        D_MODEL = 128
        M = 64
        INNER = 16
        s = jnp.einsum('btd,dm->btm', x, Win) + bin_
        h = jax.nn.relu(s[..., None] * W1 + b1)
        g = jnp.einsum('btmh,mh->btm', h, W2) + b2
        out = jnp.einsum('btm,md->btd', g, Wout) + bout
        return out

    def _L3_xattn_ref(q_input, kv_input, key_padding_mask, W_Q, b_Q, W_K, b_K, W_V, b_V, W_O, b_O):
        import jax, jax.numpy as jnp
        import numpy as np
        D_MODEL = 128
        N_HEAD = 16
        D_H = D_MODEL // N_HEAD
        B, LQ, _ = q_input.shape
        LK = kv_input.shape[1]
        q = q_input @ W_Q + b_Q
        k = kv_input @ W_K + b_K
        v = kv_input @ W_V + b_V
        q = q.reshape(B, LQ, N_HEAD, D_H).transpose(0, 2, 1, 3)
        k = k.reshape(B, LK, N_HEAD, D_H).transpose(0, 2, 1, 3)
        v = v.reshape(B, LK, N_HEAD, D_H).transpose(0, 2, 1, 3)
        sim = jnp.einsum('bhqd,bhkd->bhqk', q, k) / jnp.sqrt(jnp.float32(D_H))
        neg_inf = jnp.finfo(sim.dtype).min
        mask = key_padding_mask[:, None, None, :]
        sim = jnp.where(mask, neg_inf, sim)
        attn = jax.nn.softmax(sim, axis=-1)
        out = jnp.einsum('bhqk,bhkd->bhqd', attn, v)
        out = out.transpose(0, 2, 1, 3).reshape(B, LQ, D_MODEL)
        return out @ W_O + b_O

    def _L3_ffn_ref(x, router_w, w1, b1, w2, b2, gamma, beta):
        import jax, jax.numpy as jnp
        import numpy as np
        D_MODEL = 128
        D_FF = 512
        N_EXPERTS = 8
        TOP_K = 2
        LN_EPS = 1e-06

        def _moe(x, router_w, w1, b1, w2, b2, gamma, beta):
            B, S, D = x.shape
            x_flat = x.reshape(-1, D)
            N = x_flat.shape[0]
            logits = x_flat @ router_w
            gate_vals, gate_idx = jax.lax.top_k(logits, TOP_K)
            gate_w = jax.nn.softmax(gate_vals, axis=-1)
            gates = jnp.zeros_like(logits).at[jnp.arange(N)[:, None], gate_idx].set(gate_w)
            h = jax.nn.gelu(jnp.einsum('nd,edf->enf', x_flat, w1) + b1[:, None, :], approximate=False)
            out = jnp.einsum('enf,efd->end', h, w2) + b2[:, None, :]
            res = x_flat[None, :, :] + out
            mu = jnp.mean(res, axis=-1, keepdims=True)
            var = jnp.mean(jnp.square(res - mu), axis=-1, keepdims=True)
            normed = (res - mu) * jax.lax.rsqrt(var + LN_EPS)
            expert_out = normed * gamma[:, None, :] + beta[:, None, :]
            y = jnp.einsum('end,ne->nd', expert_out, gates)
            return y.reshape(B, S, D)
        return _moe(x, router_w, w1, b1, w2, b2, gamma, beta)
    x = x + _L0_xattn_ref(ctx_1024, _layernorm(x, axis=-1), L0_xattn_Wq)
    x = x + _L0_ffn_ref(_layernorm(x, axis=-1), L0_ffn_Wg, L0_ffn_bg, L0_ffn_W1, L0_ffn_b1, L0_ffn_W2, L0_ffn_b2)
    x = x + _L1_xattn_ref(_layernorm(x, axis=-1), ctx_1024, L1_xattn_Wq1, L1_xattn_Wk1, L1_xattn_Wv1, L1_xattn_Wq2, L1_xattn_Wk2, L1_xattn_Wv2, L1_xattn_fc1_w, L1_xattn_fc1_b, L1_xattn_fc2_w, L1_xattn_fc2_b, L1_xattn_ln1_g, L1_xattn_ln1_b, L1_xattn_ln2_g, L1_xattn_ln2_b, L1_xattn_ln3_g, L1_xattn_ln3_b)
    x = x + _L1_ffn_ref(_layernorm(x, axis=-1), L1_ffn_w_gate, L1_ffn_w_up, L1_ffn_w_down)
    x = x + _L2_xattn_ref(_layernorm(x, axis=-1), ctx_1024, L2_xattn_Wq, L2_xattn_bq, L2_xattn_Wv, L2_xattn_bv, L2_xattn_Wfc, L2_xattn_bfc, L2_xattn_gamma, L2_xattn_beta)
    x = x + _L2_ffn_ref(_layernorm(x, axis=-1), L2_ffn_Win, L2_ffn_bin_, L2_ffn_W1, L2_ffn_b1, L2_ffn_W2, L2_ffn_b2, L2_ffn_Wout, L2_ffn_bout)
    x = x + _L3_xattn_ref(_layernorm(x, axis=-1), ctx_1024, mask_BxS2_bk0, L3_xattn_W_Q, L3_xattn_b_Q, L3_xattn_W_K, L3_xattn_b_K, L3_xattn_W_V, L3_xattn_b_V, L3_xattn_W_O, L3_xattn_b_O)
    x = x + _L3_ffn_ref(_layernorm(x, axis=-1), L3_ffn_router_w, L3_ffn_w1, L3_ffn_b1, L3_ffn_w2, L3_ffn_b2, L3_ffn_gamma, L3_ffn_beta)
    return x

_drawn_inputs = setup_inputs


def setup_inputs(seed=0):
    import zlib

    import numpy as np

    out = dict(_drawn_inputs(seed))
    spreads = {'L0_ffn_bg': (0.0, 0.407),
     'L1_xattn_fc1_b': (0.0, 0.1),
     'L1_xattn_fc2_b': (0.0, 0.1),
     'L1_xattn_ln1_g': (1.0, 0.2),
     'L1_xattn_ln1_b': (0.0, 0.1),
     'L1_xattn_ln2_g': (1.0, 0.2),
     'L1_xattn_ln2_b': (0.0, 0.1),
     'L1_xattn_ln3_g': (1.0, 0.2),
     'L1_xattn_ln3_b': (0.0, 0.1),
     'L2_xattn_gamma': (1.0, 0.543),
     'L2_xattn_beta': (0.0, 0.481),
     'L3_xattn_b_Q': (0.0, 2.0),
     'L3_xattn_b_K': (0.0, 2.0),
     'L3_xattn_b_V': (0.0, 0.538),
     'L3_xattn_b_O': (0.0, 0.487),
     'L3_ffn_b1': (0.0, 0.8),
     'L3_ffn_b2': (0.0, 1.849),
     'L3_ffn_gamma': (1.0, 0.6),
     'L3_ffn_beta': (0.0, 0.996)}
    factors = {'L0_ffn_b1': 7.649,
     'L0_ffn_b2': 5.75,
     'L1_ffn_w_gate': 8.0,
     'L1_ffn_w_up': 8.0,
     'L1_ffn_w_down': 8.0,
     'L2_xattn_bq': 43.256,
     'L2_ffn_bin_': 55.903,
     'L3_ffn_w1': 4.703,
     'L3_ffn_w2': 4.294,
     'L2_xattn_Wq': 3.912,
     'L2_xattn_bv': 3.234,
     'L2_xattn_bfc': 4.401,
     'L2_ffn_Win': 4.566,
     'L2_ffn_W1': 4.284,
     'L2_ffn_b1': 3.169,
     'L2_ffn_b2': 3.816,
     'L2_ffn_bout': 5.123}
    for name, (base, spread) in spreads.items():
        noise = np.random.default_rng([zlib.crc32(name.encode()), seed]).standard_normal(out[name].shape)
        drawn = base * np.exp(spread * noise) if base else spread * noise
        out[name] = jnp.asarray(drawn.astype(out[name].dtype))
    for name, factor in factors.items():
        out[name] = (out[name] * factor).astype(out[name].dtype)
    return out
```

```python
from contextlib import ExitStack

import numpy as np

import concourse.bass as bass
from concourse import mybir

F32 = mybir.dt.float32
F32R = mybir.dt.float32r
I32 = mybir.dt.int32
U8 = mybir.dt.uint8
ALU = mybir.AluOpType
ACT = mybir.ActivationFunctionType
X_AXIS = mybir.AxisListType.X
XY_AXES = mybir.AxisListType.XY

BATCH, TOK, D = 16, 56, 128
PAIRS = BATCH // 2
HALF = 64
KEYS = 1500
CHUNK = 125
CHUNKS = KEYS // CHUNK
BANKS = 3
BANK_KEYS = KEYS // BANKS
HEADS = 16
ROWS = HEADS * TOK
TILES = BATCH * ROWS // 128
BATCH_TILES = ROWS // 128
EXPERTS, FF = 8, 512
FCHUNKS = FF // 128
FFN1 = 384
GCHUNKS = FFN1 // 128
M2, INNER = 64, 16
NEG = -3.0e38
HALF_TOK = BATCH // 2 * TOK


class Chain:

    def __init__(self, eng, sem):
        self.eng, self.sem, self.n, self.base = eng, sem, 0, 0

    def __call__(self, ins):
        self.n += 1
        ins.then_inc(self.sem, 1)
        self.eng.wait_ge(self.sem, self.base + self.n)


def settle(eng, passed):
    eng.sem_inc(passed, 1)


def run_steps(eng, total, lag, unroll, step):
    first = -(-lag // unroll) * unroll
    loops = (total - first) // unroll
    for n in range(first):
        step(n, n % unroll, n)
    if loops > 0:
        with eng.Fori(first // unroll, first // unroll + loops) as i:
            for u in range(unroll):
                step(i * unroll + u, u, None)
    for n in range(first + max(loops, 0) * unroll, total + lag):
        step(n, n % unroll, n)


def live(known, lag, total):
    return known is None or lag <= known < total + lag


class Stack:

    def __init__(self, nc, t, out):
        self.nc, self.t, self.out = nc, t, out
        self.used = []

    def sem(self, ctx, name):
        sem = ctx.enter_context(self.nc.semaphore(f"{self.stage}_{name}"))
        if self.stage != "all":
            self.used.append(sem.num)
        return sem

    def clear_used(self):
        runs = []
        for num in sorted(set(self.used)):
            if runs and runs[-1][-1] == num - 1:
                runs[-1].append(num)
            else:
                runs.append([num])
        self.used = []
        with self.nc.Block() as block:

            @block.gpsimd
            def _(g):
                for run in runs:
                    g.sem_clear(range(run[0], run[-1] + 1))

    def sb(self, ctx, name, shape, dt=F32):
        return ctx.enter_context(self.nc.sbuf_tensor(f"{self.stage}_{name}", shape, dt))




def rsqrt(v, chain, out, var, eps, w):
    ve, half, y2, tt = w[0], w[1], w[2], w[3]
    chain(v.tensor_scalar(ve, var, eps, None, ALU.add))
    chain(v.tensor_scalar(half, ve, -0.5, None, ALU.mult))
    chain(v.tensor_scalar(tt.bitcast(I32), ve.bitcast(I32), 1, None, ALU.logical_shift_right))
    chain(v.tensor_scalar(out.bitcast(I32), tt.bitcast(I32), -1.0, float(0x5F3759DF), ALU.mult, ALU.add))
    for _ in range(3):
        chain(v.tensor_tensor(y2, out, out, ALU.mult))
        chain(v.tensor_tensor(tt, y2, half, ALU.mult))
        chain(v.scalar_tensor_tensor(out=out, in0=tt, scalar=1.5, in1=out, op0=ALU.add, op1=ALU.mult))


def layer_norm(v, chain, dst, src, w, eps):
    stats, mv, rstd, work = w
    for t in range(PAIRS):
        last = v.bn_stats(stats[:, t, :], src[:, t, :])
    chain(last)
    for t in range(PAIRS):
        last = v.bn_aggr(mv[:, t, :], stats[:, t, :])
    chain(last)
    rsqrt(v, chain, rstd[:, :], mv[:, :, 1], eps, [work[:, k, :] for k in range(4)])
    for t in range(PAIRS):
        last = v.tensor_scalar(dst[:, t, :], src[:, t, :], mv[:, t, 0:1], rstd[:, t:t + 1],
                               ALU.subtract, ALU.mult)
    chain(last)


class Kernel(Stack):
    def norm_scratch(self, ctx):
        return (self.sb(ctx, "stats", [128, PAIRS, 6]), self.sb(ctx, "mv", [128, PAIRS, 2]),
                self.sb(ctx, "rstd", [128, PAIRS]), self.sb(ctx, "nwork", [128, 4, PAIRS]))

    def setup(self):
        nc, t = self.nc, self.t
        self.stage = "init"
        with ExitStack() as ctx:
            zeroed, marked, x_in, step = (self.sem(ctx, n) for n in ("zeroed", "marked", "x_in", "step"))
            X, ident, blockm, valid, pick, rowmask, kidx, e_idx, ones = (
                self.X, self.ident, self.blockm, self.valid, self.pick, self.rowmask, self.kidx,
                self.e_idx, self.ones)
            block = ctx.enter_context(nc.Block())

            @block.vector
            def _(v):
                chain = Chain(v, step)
                v.memset(ident[:, :], 0.0)
                v.memset(blockm[:, :], NEG)
                v.memset(valid[:, :], 0.0)
                v.memset(pick[:, :], 0.0)
                v.memset(ones[:, :], 1.0)
                v.memset(rowmask[:, :], 1.0)
                chain(v.memset(X[:, :, :], 0.0))
                v.memset(blockm[0:HALF, 0:HALF], 0.0)
                v.memset(blockm[HALF:128, HALF:128], 0.0)
                v.memset(valid[0:HALF, 0:TOK], 1.0)
                v.memset(valid[HALF:128, HALF:HALF + TOK], 1.0)
                v.memset(pick[0:1, 0:HALF], 1.0)
                v.memset(pick[HALF:HALF + 1, HALF:128], 1.0).then_inc(zeroed, 1)

            @block.gpsimd
            def _(g):
                chain = Chain(g, marked)
                g.iota(kidx[:, :], [[1, KEYS]], base=0, channel_multiplier=0,
                       allow_small_or_imprecise_dtypes=True)
                chain(g.iota(e_idx[:, :, :], [[0, PAIRS], [1, EXPERTS]], base=-EXPERTS, channel_multiplier=0,
                             allow_small_or_imprecise_dtypes=True))
                g.wait_ge(zeroed, 1)
                chain(g.affine_select(out=ident[:, :], in_=ident[:, :], compare_op=ALU.not_equal, fill=1.0,
                                      base=0, pattern=[[-1, 128]], channel_multiplier=1))
                chain(g.affine_select(out=blockm[:, :], in_=blockm[:, :], compare_op=ALU.is_ge, fill=NEG,
                                      base=0, pattern=[[-1, 128]], channel_multiplier=1))
                for p in (0, HALF):
                    chain(g.affine_select(out=rowmask[p:p + HALF, :], in_=rowmask[p:p + HALF, :],
                                          compare_op=ALU.is_ge, fill=0.0, base=TOK - 1, pattern=[[0, 1]],
                                          channel_multiplier=-1))

            @block.sync
            def _(sp):
                xv = t["x"].rearrange("(t two) q d -> two q t d", two=2)
                sp.wait_ge(zeroed, 1)
                for par in range(2):
                    sp.dma_start(X[HALF * par:HALF * par + TOK, :, :], xv[par]).then_inc(x_in, 16)
                sp.wait_ge(x_in, 32)

    def local_attention(self, stage, self_keys):
        nc, t = self.nc, self.t
        self.stage = stage
        X, XN, ident, blockm, PS = self.X, self.XN, self.ident, self.blockm, self.PS
        scale = 1.0 / np.sqrt(8.0) if self_keys else 1.0 / np.sqrt(float(D))
        with ExitStack() as ctx:
            XT = self.sb(ctx, "XT", [128, PAIRS, 128])
            QT = self.sb(ctx, "QT", [128, PAIRS, 128])
            KT = XT if self_keys else self.sb(ctx, "KT", [128, PAIRS, 2, HALF])
            C = XN if self_keys else self.sb(ctx, "C", [128, PAIRS, D])
            S = self.sb(ctx, "S", [128, PAIRS, 128])
            PT = self.sb(ctx, "PT", [128, PAIRS, 128])
            OT = self.sb(ctx, "OT", [128, PAIRS, 128])
            w_q = self.sb(ctx, "w_q", [128, 128])
            w_k = self.sb(ctx, "w_k", [128, 128])
            w_v = self.sb(ctx, "w_v", [128, 128])
            fold = self.sb(ctx, "fold", [128, 128])
            red = self.sb(ctx, "red", [128, 4, PAIRS])
            ln = self.norm_scratch(ctx)
            gb = self.sb(ctx, "gb", [128, 2, D])
            (w_in, c_in, c_zero, fold_ps, fold_in, xn_ready, xt_ps, xt_in, qt_ps, qt_in, e_ps, s_ready,
             p_ready, p_done, pt_ps, pt_in, o_ps, o_in, z_ps, step, cnt_in, len_ps) = (
                self.sem(ctx, n) for n in (
                    "w_in", "c_in", "c_zero", "fold_ps", "fold_in", "xn_ready", "xt_ps", "xt_in",
                    "qt_ps", "qt_in", "e_ps", "s_ready", "p_ready", "p_done", "pt_ps", "pt_in", "o_ps",
                    "o_in", "z_ps", "step", "cnt_in", "len_ps"))
            block = ctx.enter_context(nc.Block())
            flat = lambda a: a[:, :, :].rearrange("p t m -> p (t m)")

            @block.sync
            def _(sp):
                if self_keys:
                    sp.dma_start(w_q[:, :], t["Wq1T"]).then_inc(w_in, 16)
                    sp.dma_start(w_k[:, :], t["Wk1T"]).then_inc(w_in, 16)
                    sp.dma_start(w_v[:, :], t["L1_xattn_Wv1"]).then_inc(w_in, 16)
                    sp.dma_start(gb[:, 0, :], t["L1_xattn_ln1_g"].partition_broadcast(128)).then_inc(w_in, 16)
                    sp.dma_start(gb[:, 1, :], t["L1_xattn_ln1_b"].partition_broadcast(128)).then_inc(w_in, 16)
                else:
                    sp.dma_start(w_q[:, :], t["L0_xattn_Wq"]).then_inc(w_in, 16)
                    sp.dma_start(w_v[:, :], t["WqT0"]).then_inc(w_in, 16)
                    sp.wait_ge(c_zero, 1)
                    cv = t["ctx_1024"].rearrange("(t two) k d -> two k t d", two=2)
                    tv = t["ctxT"].rearrange("(t two) d k -> two d t k", two=2)
                    for par in range(2):
                        sp.dma_start(C[HALF * par:HALF * par + TOK, :, :], cv[par, 0:TOK]).then_inc(c_in, 16)
                        sp.dma_start(KT[:, :, par, 0:TOK], tv[par, :, :, 0:TOK]).then_inc(c_in, 16)

            @block.tensor
            def _(pe):
                pe.wait_ge(w_in, 80 if self_keys else 32)
                pe.matmul(PS[:, 7, 0:128], w_q[:, :], w_k[:, :] if self_keys else w_q[:, :],
                          start=True, stop=True).then_inc(fold_ps, 1)
                pe.wait_ge(xn_ready, 1)
                for k in range(2):
                    for j in range(4):
                        mm = pe.transpose(PS[:, k, 128 * j:128 * j + 128], XN[:, 4 * k + j, :], ident[:, :])
                    mm.then_inc(xt_ps, 1)
                pe.wait_ge(fold_in, 1)
                for k in range(2):
                    pe.wait_ge(xt_in, k + 1)
                    pe.matmul(PS[:, 2 + k, :], fold[:, :], flat(XT)[:, 512 * k:512 * k + 512],
                              start=True, stop=True).then_inc(qt_ps, 1)
                if not self_keys:
                    pe.wait_ge(c_in, 64)
                for k in range(2):
                    pe.wait_ge(qt_in, k + 1)
                    for j in range(4):
                        keys = (XT[:, 4 * k + j, :] if self_keys
                                else KT[:, 4 * k + j, :, :].rearrange("p a k -> p (a k)"))
                        mm = pe.matmul(PS[:, 4 + k, 128 * j:128 * j + 128], QT[:, 4 * k + j, :], keys,
                                       start=True, stop=True)
                    mm.then_inc(e_ps, 1)
                if self_keys:
                    pe.wait_ge(cnt_in, 1)
                    pe.matmul(PS[:, 6, 0:PAIRS], self.pick[:, :], red[:, 3, :], start=True,
                              stop=True).then_inc(len_ps, 1)
                pe.wait_ge(p_done, 1)
                for k in range(2):
                    for j in range(4):
                        mm = pe.transpose(PS[:, k, 128 * j:128 * j + 128], S[:, 4 * k + j, :], ident[:, :])
                    mm.then_inc(pt_ps, 1)
                for k in range(2):
                    pe.wait_ge(pt_in, k + 1)
                    for j in range(4):
                        mm = pe.matmul(PS[:, 2 + k, 128 * j:128 * j + 128], C[:, 4 * k + j, :],
                                       PT[:, 4 * k + j, :], start=True, stop=True)
                    mm.then_inc(o_ps, 1)
                for k in range(2):
                    pe.wait_ge(o_in, k + 1)
                    for j in range(4):
                        mm = pe.matmul(PS[:, 4 + k, 128 * j:128 * j + 128], OT[:, 4 * k + j, :], w_v[:, :],
                                       start=True, stop=True)
                    mm.then_inc(z_ps, 1)

            @block.scalar
            def _(act):
                act.wait_ge(fold_ps, 1)
                act.copy(fold[:, :], PS[:, 7, 0:128]).then_inc(fold_in, 1)
                for k in range(2):
                    act.wait_ge(xt_ps, k + 1)
                    act.copy(flat(XT)[:, 512 * k:512 * k + 512], PS[:, k, :]).then_inc(xt_in, 1)
                for k in range(2):
                    act.wait_ge(qt_ps, k + 1)
                    act.mul(flat(QT)[:, 512 * k:512 * k + 512], PS[:, 2 + k, :], 1.0).then_inc(qt_in, 1)
                act.wait_ge(s_ready, 1)
                act.activation(S[:, :, :], S[:, :, :], ACT.Exp, scale=scale).then_inc(p_ready, 1)
                for k in range(2):
                    act.wait_ge(pt_ps, k + 1)
                    act.copy(flat(PT)[:, 512 * k:512 * k + 512], PS[:, k, :]).then_inc(pt_in, 1)
                for k in range(2):
                    act.wait_ge(o_ps, k + 1)
                    act.copy(flat(OT)[:, 512 * k:512 * k + 512], PS[:, 2 + k, :]).then_inc(o_in, 1)

            @block.vector
            def _(v):
                chain = Chain(v, step)
                if not self_keys:
                    chain(v.memset(C[:, :, :], 0.0))
                    v.memset(KT[:, :, :, :], 0.0).then_inc(c_zero, 1)
                layer_norm(v, chain, XN, X, ln, 1e-5)
                v.sem_inc(xn_ready, 1)
                E = PS[:, 4:6, :].rearrange("p a (j m) -> p (a j) m", m=128)
                v.wait_ge(e_ps, 2)
                if self_keys:
                    chain(v.tensor_scalar(S[:, :, :], E, 0.0, None, ALU.not_equal))
                    chain(v.tensor_tensor(S[:, :, :], S[:, :, :],
                                          self.valid[:, :].unsqueeze(1).to_broadcast([128, PAIRS, 128]), ALU.mult))
                    v.tensor_reduce(red[:, 3, :], S[:, :, :], X_AXIS, ALU.add).then_inc(cnt_in, 1)
                    v.wait_ge(len_ps, 1)
                    chain(v.tensor_copy(red[:, 3, :], PS[:, 6, 0:PAIRS]))
                    for p in (0, HALF):
                        chain(v.tensor_tensor(
                            S[p:p + HALF, :, p:p + HALF],
                            self.kidx[p:p + HALF, 0:HALF].unsqueeze(1).to_broadcast([HALF, PAIRS, HALF]),
                            red[p:p + HALF, 3, :].unsqueeze(2).to_broadcast([HALF, PAIRS, HALF]), ALU.is_ge))
                        chain(v.memset(S[p:p + HALF, :, HALF - p:128 - p], 0.0))
                    chain(v.tensor_scalar(S[:, :, :], S[:, :, :], NEG, None, ALU.mult))
                    chain(v.tensor_tensor(S[:, :, :], S[:, :, :],
                                          blockm[:, :].unsqueeze(1).to_broadcast([128, PAIRS, 128]), ALU.min))
                    chain(v.tensor_tensor(S[:, :, :], E, S[:, :, :], ALU.add))
                else:
                    chain(v.tensor_tensor(S[:, :, :], E,
                                          blockm[:, :].unsqueeze(1).to_broadcast([128, PAIRS, 128]), ALU.add))
                chain(v.tensor_reduce(red[:, 0, :], S[:, :, :], X_AXIS, ALU.max))
                v.tensor_tensor(S[:, :, :], S[:, :, :], red[:, 0, :].unsqueeze(2).to_broadcast([128, PAIRS, 128]),
                                ALU.subtract).then_inc(s_ready, 1)
                v.wait_ge(p_ready, 1)
                chain(v.tensor_reduce(red[:, 1, :], S[:, :, :], X_AXIS, ALU.add))
                chain(v.reciprocal(red[:, 2, :], red[:, 1, :]))
                v.tensor_tensor(S[:, :, :], S[:, :, :], red[:, 2, :].unsqueeze(2).to_broadcast([128, PAIRS, 128]),
                                ALU.mult).then_inc(p_done, 1)
                v.wait_ge(z_ps, 2)
                Z = PS[:, 4:6, :].rearrange("p a (j m) -> p (a j) m", m=128)
                if self_keys:
                    v.wait_ge(w_in, 80)
                    chain(v.tensor_tensor(S[:, :, :], Z, XN[:, :, :], ALU.add))
                    layer_norm(v, chain, XN, S, ln, 1e-5)
                    self.affine(v, chain, XN, gb)
                else:
                    chain(v.tensor_tensor(X[:, :, :], Z, X[:, :, :], ALU.add))

    def affine(self, v, chain, dst, gb):
        for k, op in ((0, ALU.mult), (1, ALU.add)):
            chain(v.tensor_tensor(dst[:, :, :], dst[:, :, :],
                                  gb[:, k, :].unsqueeze(1).to_broadcast([128, PAIRS, D]), op))

    def moe(self, stage, final):
        nc, t = self.nc, self.t
        self.stage = stage
        X, XN, ident, PS = self.X, self.XN, self.ident, self.PS
        W1, W2 = (t["L3_ffn_w1"], t["L3_ffn_w2"]) if final else (t["L0_ffn_W1"], t["L0_ffn_W2"])
        B1 = t["b1T3"] if final else t["b1T0"]
        with ExitStack() as ctx:
            XT = self.sb(ctx, "XT", [128, PAIRS, 128])
            HT = self.sb(ctx, "HT", [128, FCHUNKS, PAIRS, 2, HALF])
            w1 = [self.sb(ctx, f"w1_{s}", [128, FF]) for s in range(2)]
            w2 = [self.sb(ctx, f"w2_{s}", [128, FCHUNKS, D]) for s in range(2)]
            b1 = self.sb(ctx, "b1", [128, EXPERTS, FCHUNKS])
            wg = self.sb(ctx, "wg", [128, EXPERTS])
            bg = self.sb(ctx, "bg", [1, EXPERTS])
            add = self.sb(ctx, "add", [EXPERTS, D])
            G = self.sb(ctx, "G", [128, PAIRS, EXPERTS])
            GT = self.sb(ctx, "GT", [EXPERTS, PAIRS, 128])
            lg = self.sb(ctx, "lg", [128, 6, PAIRS, EXPERTS])
            red = self.sb(ctx, "red", [128, 6, PAIRS])
            ln = self.norm_scratch(ctx)
            if final:
                b2 = self.sb(ctx, "b2", [128, EXPERTS, D])
                gamma = self.sb(ctx, "gamma", [128, EXPERTS, D])
                XB = [self.sb(ctx, f"XB{s}", [128, PAIRS, D]) for s in range(2)]
                R = self.sb(ctx, "R", [128, PAIRS, D])
                gscale = self.sb(ctx, "gscale", [128, PAIRS])
            (w_in, g_in, h_zero, xn_ready, xt_ps, xt_in, lg_ps, l_ready, p_ready, g_ready, gt_ps, gt_in,
             add_ps, step) = (self.sem(ctx, n) for n in (
                 "w_in", "g_in", "h_zero", "xn_ready", "xt_ps", "xt_in", "lg_ps", "l_ready", "p_ready",
                 "g_ready", "gt_ps", "gt_in", "add_ps", "step"))
            w_slot = [self.sem(ctx, f"w_slot{s}") for s in range(2)]
            w_used = [self.sem(ctx, f"w_used{s}") for s in range(2)]
            h_ps, h_in = self.sem(ctx, "h_ps"), [self.sem(ctx, f"h_in{k}") for k in range(4)]
            y_ps = [self.sem(ctx, f"y_ps{s}") for s in range(2)]
            y_used = [self.sem(ctx, f"y_used{s}") for s in range(2)]
            xb_in = [self.sem(ctx, f"xb_in{s}") for s in range(2)]
            block = ctx.enter_context(nc.Block())
            flat = lambda a: a[:, :, :].rearrange("p t m -> p (t m)")
            SETUP_DMAS = 6 if final else 4

            @block.sync
            def _(sp):
                sp.dma_start(b1[:, :, :], B1).then_inc(w_in, 16)
                if final:
                    sp.dma_start(wg[:, :], t["L3_ffn_router_w"]).then_inc(w_in, 16)
                    sp.dma_start(add[:, :], t["L3_ffn_beta"]).then_inc(w_in, 16)
                    sp.dma_start(b2[:, :, :], t["L3_ffn_b2"].partition_broadcast(128)).then_inc(w_in, 16)
                    sp.dma_start(gamma[:, :, :], t["L3_ffn_gamma"].partition_broadcast(128)).then_inc(w_in, 16)
                    sp.dma_start(bg[:, :], t["L3_ffn_gamma"][0:1, 0:EXPERTS]).then_inc(w_in, 16)
                else:
                    sp.dma_start(wg[:, :], t["L0_ffn_Wg"]).then_inc(w_in, 16)
                    sp.dma_start(add[:, :], t["L0_ffn_b2"]).then_inc(w_in, 16)
                    sp.dma_start(bg[:, :], t["L0_ffn_bg"].unsqueeze(0)).then_inc(w_in, 16)
                with sp.Fori(0, EXPERTS // 2) as i:
                    for s in range(2):
                        sp.wait_ge(w_used[s], i)
                        sp.dma_start(w1[s][:, :], W1[bass.ds(2 * i + s, 1)].rearrange("a d f -> d (a f)")
                                     ).then_inc(w_slot[s], 16)
                        sp.dma_start(w2[s][:, :, :], W2[bass.ds(2 * i + s, 1)].rearrange(
                            "a (c f) d -> f (a c) d", f=128)).then_inc(w_slot[s], 16)

            @block.tensor
            def _(pe):
                pe.wait_ge(w_in, 16 * SETUP_DMAS)
                pe.wait_ge(xn_ready, 1)
                for k in range(2):
                    for j in range(4):
                        mm = pe.transpose(PS[:, k, 128 * j:128 * j + 128], XN[:, 4 * k + j, :], ident[:, :])
                    mm.then_inc(xt_ps, 1)
                pe.wait_ge(xt_in, 2)
                for p in range(PAIRS):
                    mm = pe.matmul(PS[:, 2, 8 * p:8 * p + 8], XT[:, p, :], wg[:, :], start=True, stop=final)
                    if not final:
                        mm = pe.matmul(PS[:, 2, 8 * p:8 * p + 8], self.ones[0:1, :], bg[0:1, :], start=False,
                                       stop=True)
                mm.then_inc(lg_ps, 1)
                pe.wait_ge(g_ready, 1)
                for k in range(2):
                    for j in range(4):
                        mm = pe.transpose(PS[0:EXPERTS, k, 128 * j:128 * j + 128], G[:, 4 * k + j, :],
                                          ident[:, :])
                    mm.then_inc(gt_ps, 1)
                pe.wait_ge(gt_in, 2)
                for k in range(2):
                    for j in range(4):
                        mm = pe.matmul(PS[:, 2 + k, 128 * j:128 * j + 128], GT[:, 4 * k + j, :], add[:, :],
                                       start=True, stop=True)
                    mm.then_inc(add_ps, 1)
                pe.wait_ge(g_in, 1)
                with pe.Fori(0, EXPERTS // 2) as i:
                    for s in range(2):
                        pe.wait_ge(w_slot[s], 32 * i + 32)
                        for half in range(2):
                            for c in range(FCHUNKS):
                                pe.wait_ge(h_in[c], 4 * i + (2 * s + half))
                                rhs = XT[:, 4 * half:4 * half + 4, :].rearrange(
                                    "p t (a q) -> p (t a) q", a=2)[:, :, 0:TOK]
                                pe.matmul(PS[:, c, 0:HALF_TOK], w1[s][:, 128 * c:128 * c + 128], rhs,
                                          start=True, stop=True).then_inc(h_ps, 1)
                        pe.wait_ge(y_used[s], i)
                        for half in range(2):
                            for c in range(FCHUNKS):
                                pe.wait_ge(h_in[c], 4 * i + 2 * s + half + 1)
                            for j in range(4):
                                p = 4 * half + j
                                for c in range(FCHUNKS):
                                    mm = pe.matmul(PS[:, 4 + 2 * s + half, 128 * j:128 * j + 128],
                                                   HT[:, c, p, :, :].rearrange("p a q -> p (a q)"),
                                                   w2[s][:, c, :], start=(c == 0), stop=(c == FCHUNKS - 1))
                            mm.then_inc(y_ps[s], 1)
                        pe.wait_ge(y_ps[s], 2 * i + 2)
                        pe.nop().then_inc(w_used[s], 1)

            @block.scalar
            def _(act):
                for k in range(2):
                    act.wait_ge(xt_ps, k + 1)
                    act.copy(flat(XT)[:, 512 * k:512 * k + 512], PS[:, k, :]).then_inc(xt_in, 1)
                act.wait_ge(l_ready, 1)
                act.activation(lg[:, 4, :, :], lg[:, 5, :, :], ACT.Exp).then_inc(p_ready, 1)
                for k in range(2):
                    act.wait_ge(gt_ps, k + 1)
                    act.copy(GT[:, 4 * k:4 * k + 4, :].rearrange("p t m -> p (t m)"),
                             PS[0:EXPERTS, k, :]).then_inc(gt_in, 1)
                act.wait_ge(h_zero, 1)
                act.wait_ge(w_in, 16 * SETUP_DMAS)
                with act.Fori(0, EXPERTS // 2) as i:
                    for s in range(2):
                        for half in range(2):
                            if half == 0:
                                act.wait_ge(w_used[1 - s], i + s)
                            for c in range(FCHUNKS):
                                act.wait_ge(h_ps, 16 * i + 8 * s + 4 * half + c + 1)
                                settle(act, self.passed)
                                act.activation(
                                    HT[:, c, 4 * half:4 * half + 4, :, 0:TOK].rearrange("p t a q -> p (t a) q"),
                                    PS[:, c, 0:HALF_TOK].rearrange("p (t q) -> p t q", q=TOK), ACT.Gelu,
                                    bias=b1[:, bass.ds(2 * i + s, 1), c]).then_inc(h_in[c], 1)

            @block.gpsimd
            def _(g):
                g.memset(HT[:, :, :, :, TOK:HALF], 0.0).then_inc(h_zero, 1)
                if final:
                    g.wait_ge(w_in, 16 * SETUP_DMAS)
                    g.wait_ge(xn_ready, 1)
                    with g.Fori(0, EXPERTS // 2) as i:
                        for s in range(2):
                            g.wait_ge(y_used[s], i)
                            g.tensor_tensor(XB[s][:, :, :], XN[:, :, :],
                                            b2[:, bass.ds(2 * i + s, 1), :].to_broadcast([128, PAIRS, D]),
                                            ALU.add).then_inc(xb_in[s], 1)

            @block.vector
            def _(v):
                chain = Chain(v, step)
                layer_norm(v, chain, XN, X, ln, 1e-5)
                v.sem_inc(xn_ready, 1)
                v.wait_ge(lg_ps, 1)
                self.gates(v, chain, PS[:, 2, 0:64].rearrange("p (t e) -> p t e", e=EXPERTS), lg, red, G,
                           l_ready, p_ready, final)
                v.sem_inc(g_ready, 1)
                v.wait_ge(add_ps, 2)
                chain(v.tensor_tensor(X[:, :, :], PS[:, 2:4, :].rearrange("p a (j m) -> p (a j) m", m=128),
                                      X[:, :, :], ALU.add))
                v.sem_inc(g_in, 1)
                per_expert = 20 if final else 1
                done = chain.n
                with v.Fori(0, EXPERTS // 2) as i:
                    for s in range(2):
                        chain.base, chain.n = done + 2 * per_expert * i + per_expert * s, 0
                        Y = PS[:, 4 + 2 * s:6 + 2 * s, :].rearrange("p a (j m) -> p (a j) m", m=128)
                        v.wait_ge(y_ps[s], 2 * i + 2)
                        if final:
                            v.wait_ge(xb_in[s], i + 1)
                            stats, mv, rstd, work = ln
                            chain(v.tensor_tensor(R[:, :, :], Y, XB[s][:, :, :], ALU.add))
                            v.sem_inc(y_used[s], 1)
                            for p in range(PAIRS):
                                last = v.bn_stats(stats[:, p, :], R[:, p, :])
                            chain(last)
                            settle(v, self.passed)
                            for p in range(PAIRS):
                                last = v.bn_aggr(mv[:, p, :], stats[:, p, :])
                            chain(last)
                            rsqrt(v, chain, rstd[:, :], mv[:, :, 1], 1e-6, [work[:, k, :] for k in range(4)])
                            chain(v.tensor_tensor(gscale[:, :], rstd[:, :],
                                                  G[:, :, bass.ds(2 * i + s, 1)].rearrange("p t a -> p (t a)"),
                                                  ALU.mult))
                            for p in range(PAIRS):
                                last = v.tensor_scalar(R[:, p, :], R[:, p, :], mv[:, p, 0:1],
                                                       gscale[:, p:p + 1], ALU.subtract, ALU.mult)
                            chain(last)
                            chain(v.tensor_tensor(
                                R[:, :, :], R[:, :, :],
                                gamma[:, bass.ds(2 * i + s, 1), :].to_broadcast([128, PAIRS, D]), ALU.mult))
                            chain(v.tensor_tensor(X[:, :, :], X[:, :, :], R[:, :, :], ALU.add))
                        else:
                            for p in range(PAIRS):
                                last = v.scalar_tensor_tensor(
                                    out=X[:, p, :], in0=Y[:, p, :], scalar=G[:, p, bass.ds(2 * i + s, 1)],
                                    in1=X[:, p, :], op0=ALU.mult, op1=ALU.add)
                            chain(last)
                            v.sem_inc(y_used[s], 1)
                        assert chain.n == per_expert, chain.n

    def gates(self, v, chain, logits, lg, red, G, l_ready, p_ready, final):
        shape = [128, PAIRS, EXPERTS]
        wide = lambda r: r.unsqueeze(2).to_broadcast(shape)
        L, cand, best, L2, P, less = (lg[:, k, :, :] for k in range(6))
        chain(v.tensor_copy(L, logits))
        chain(v.tensor_reduce(red[:, 0, :], L, X_AXIS, ALU.max))
        v.tensor_tensor(less, L, wide(red[:, 0, :]), ALU.subtract).then_inc(l_ready, 1)
        for k, (src, hit) in enumerate(((L, best), (L2, cand))):
            if k:
                chain(v.tensor_reduce(red[:, 0, :], src, X_AXIS, ALU.max))
            chain(v.tensor_tensor(cand, src, wide(red[:, 0, :]), ALU.is_equal))
            chain(v.tensor_tensor(cand, cand, self.e_idx[:, :, :], ALU.mult))
            chain(v.tensor_reduce(red[:, 1 + k, :], cand, X_AXIS, ALU.min))
            chain(v.tensor_tensor(hit, self.e_idx[:, :, :], wide(red[:, 1 + k, :]), ALU.is_equal))
            if not k:
                chain(v.scalar_tensor_tensor(out=L2.rearrange("p t e -> p (t e)"),
                                             in0=hit.rearrange("p t e -> p (t e)"), scalar=NEG,
                                             in1=L.rearrange("p t e -> p (t e)"), op0=ALU.mult, op1=ALU.add))
        chain(v.tensor_tensor(best, best, cand, ALU.add))
        v.wait_ge(p_ready, 1)
        chain(v.tensor_tensor(G[:, :, :], P, best, ALU.mult))
        chain(v.tensor_reduce(red[:, 3, :], G[:, :, :] if final else P, X_AXIS, ALU.add))
        chain(v.reciprocal(red[:, 4, :], red[:, 3, :]))
        chain(v.tensor_tensor(G[:, :, :], G[:, :, :], wide(red[:, 4, :]), ALU.mult))

    def cross_attention(self):
        nc, t = self.nc, self.t
        self.stage = "l1c"
        X, XN, ident, PS, kidx = self.X, self.XN, self.ident, self.PS, self.kidx
        scale = 1.0 / float(np.sqrt(8.0))
        with ExitStack() as ctx:
            XT = self.sb(ctx, "XT", [128, PAIRS, 128])
            QT = self.sb(ctx, "QT", [128, PAIRS, 128])
            ON = self.sb(ctx, "ON", [128, PAIRS, D])
            w = self.sb(ctx, "w", [128, 5, 128])
            fold = self.sb(ctx, "fold", [128, 128])
            col = self.sb(ctx, "col", [128, 1])
            row = self.sb(ctx, "row", [1, D])
            gb = self.sb(ctx, "gb", [128, 2, 2, D])
            q = [self.sb(ctx, f"q{s}", [128, 128]) for s in range(2)]
            cT = [self.sb(ctx, f"cT{s}", [128, 2, KEYS]) for s in range(2)]
            c = [self.sb(ctx, f"c{s}", [CHUNK, 2 * CHUNKS, D]) for s in range(2)]
            P = [self.sb(ctx, f"P{s}", [128, KEYS]) for s in range(2)]
            PT = [self.sb(ctx, f"PT{s}", [CHUNK, CHUNKS * 128]) for s in range(2)]
            pad = self.sb(ctx, "pad", [128, KEYS])
            small = self.sb(ctx, "small", [128, 6, 2])
            ln = self.norm_scratch(ctx)
            COUNT, LENGTH, TOP, BIAS, SUM, INV = range(6)
            (w_in, fold_ps, fold_in, xt_ps, xt_in, qt_ps, qt_in, q_in, e_ps, cnt_in, len_ps, len_in,
             pad_in, top_in, p_in, pt_ps, pt_in, o_ps, o_in, step, ot_ps, ot_in, z_ps,
             n2_ready, h_ps, h_in, y_ps) = (self.sem(ctx, n) for n in (
                 "w_in", "fold_ps", "fold_in", "xt_ps", "xt_in", "qt_ps", "qt_in", "q_in", "e_ps", "cnt_in",
                 "len_ps", "len_in", "pad_in", "top_in", "p_in", "pt_ps", "pt_in", "o_ps",
                 "o_in", "step", "ot_ps", "ot_in", "z_ps", "n2_ready", "h_ps", "h_in", "y_ps"))
            inv_in = self.sem(ctx, "inv_in")
            c_in = [self.sem(ctx, f"c_in{s}") for s in range(2)]
            cT_in = [self.sem(ctx, f"cT_in{s}") for s in range(2)]
            block = ctx.enter_context(nc.Block())
            flat = lambda a: a[:, :, :].rearrange("p t m -> p (t m)")

            @block.sync
            def _(sp):
                for k, src in enumerate((t["Wq2T"], t["Wk2T"], t["L1_xattn_Wv2"], t["L1_xattn_fc1_w"],
                                         t["L1_xattn_fc2_w"])):
                    sp.dma_start(w[:, k, :], src).then_inc(w_in, 16)
                sp.dma_start(col[:, :], t["L1_xattn_fc1_b"].unsqueeze(1)).then_inc(w_in, 16)
                sp.dma_start(row[:, :], t["L1_xattn_fc2_b"].unsqueeze(0)).then_inc(w_in, 16)
                for k, src in enumerate(("ln2_g", "ln2_b", "ln3_g", "ln3_b")):
                    sp.dma_start(gb[:, k // 2, k % 2, :], t["L1_xattn_" + src].partition_broadcast(128)
                                 ).then_inc(w_in, 16)

                def load(n, u, known):
                    two = bass.ds(2 * n, 2)
                    if known is None or known >= 2:
                        sp.wait_ge(e_ps, n - 1)
                    sp.dma_start(cT[u][:, :, :], t["ctxT"][two].rearrange("a d k -> d a k")
                                 ).then_inc(cT_in[u], 16)
                    if known is None or known >= 2:
                        sp.wait_ge(o_ps, n - 1)
                    sp.dma_start(c[u][:, :, :], t["ctx_1024"][two].rearrange(
                        "a (c k) d -> k (a c) d", k=CHUNK)).then_inc(c_in[u], 16)

                run_steps(sp, PAIRS, 2, 2, lambda n, u, known: load(n, u, known) if live(known, 0, PAIRS) else None)

            @block.gpsimd
            def _(g):
                g.wait_ge(qt_in, 2)

                def one(n, u, known):
                    if live(known, 0, PAIRS):
                        if known is None or known >= 2:
                            g.wait_ge(e_ps, n - 1)
                        g.tensor_copy(q[u][:, :], QT[:, bass.ds(n, 1), :].rearrange("p a m -> p (a m)")
                                      ).then_inc(q_in, 1)

                run_steps(g, PAIRS, 1, 2, one)

            @block.tensor
            def _(pe):
                pe.wait_ge(w_in, 16 * 11)
                pe.matmul(PS[:, 7, 0:128], w[:, 0, :], w[:, 1, :], start=True, stop=True).then_inc(fold_ps, 1)
                for k in range(2):
                    for j in range(4):
                        mm = pe.transpose(PS[:, k, 128 * j:128 * j + 128], XN[:, 4 * k + j, :], ident[:, :])
                    mm.then_inc(xt_ps, 1)
                pe.wait_ge(fold_in, 1)
                for k in range(2):
                    pe.wait_ge(xt_in, k + 1)
                    pe.matmul(PS[:, 2 + k, :], fold[:, :], flat(XT)[:, 512 * k:512 * k + 512],
                              start=True, stop=True).then_inc(qt_ps, 1)
                pe.wait_ge(qt_in, 2)

                def one(n, u, known):
                    if live(known, 0, PAIRS):
                        pe.wait_ge(cT_in[u], 8 * (n - u) + 16)
                        pe.wait_ge(q_in, n + 1)
                        for b in range(BANKS):
                            if known is None or known >= 2:
                                pe.wait_ge(pt_in, 3 * n - 5 + b)
                            for par in range(2):
                                mm = pe.matmul(PS[HALF * par:HALF * par + HALF, 3 * u + b, 0:BANK_KEYS],
                                               q[u][:, HALF * par:HALF * par + HALF],
                                               cT[u][:, par, BANK_KEYS * b:BANK_KEYS * b + BANK_KEYS],
                                               start=True, stop=True)
                        mm.then_inc(e_ps, 1)
                    if live(known, 1, PAIRS):
                        pe.wait_ge(p_in, n)
                        for b in range(BANKS):
                            for j in range(4):
                                at = CHUNK * (4 * b + j)
                                mm = pe.transpose(PS[0:CHUNK, 3 * (1 - u) + b, 128 * j:128 * j + 128],
                                                  P[1 - u][:, at:at + CHUNK], ident[:, :])
                            mm.then_inc(pt_ps, 1)
                    if live(known, 0, PAIRS):
                        pe.wait_ge(cnt_in, n + 1)
                        if known is None or known >= 2:
                            pe.wait_ge(o_in, n - 1)
                        pe.matmul(PS[:, 6 + u, 256:257], self.pick[:, :], small[:, COUNT, u:u + 1],
                                  start=True, stop=True).then_inc(len_ps, 1)
                    if live(known, 1, PAIRS):
                        pe.wait_ge(pt_in, 3 * n)
                        pe.wait_ge(c_in[1 - u], 8 * (n - 1 - (1 - u)) + 16)
                        for par in range(2):
                            for k in range(CHUNKS):
                                mm = pe.matmul(PS[HALF * par:HALF * par + HALF, 7 - u, 0:D],
                                               PT[1 - u][:, 128 * k + HALF * par:128 * k + HALF * par + HALF],
                                               c[1 - u][:, CHUNKS * par + k, :],
                                               start=(k == 0), stop=(k == CHUNKS - 1))
                        mm.then_inc(o_ps, 1)

                run_steps(pe, PAIRS, 1, 2, one)
                pe.wait_ge(o_in, PAIRS)
                for k in range(2):
                    for j in range(4):
                        mm = pe.transpose(PS[:, k, 128 * j:128 * j + 128], ON[:, 4 * k + j, :], ident[:, :])
                    mm.then_inc(ot_ps, 1)
                for k in range(2):
                    pe.wait_ge(ot_in, k + 1)
                    for j in range(4):
                        mm = pe.matmul(PS[:, 2 + k, 128 * j:128 * j + 128], QT[:, 4 * k + j, :], w[:, 2, :],
                                       start=True, stop=True)
                    mm.then_inc(z_ps, 1)
                pe.wait_ge(n2_ready, 1)
                for k in range(2):
                    for j in range(4):
                        mm = pe.transpose(PS[:, 4 + k, 128 * j:128 * j + 128], XN[:, 4 * k + j, :], ident[:, :])
                    mm.then_inc(xt_ps, 1)
                for k in range(2):
                    pe.wait_ge(xt_in, k + 3)
                    pe.matmul(PS[:, 6 + k, :], w[:, 3, :], flat(XT)[:, 512 * k:512 * k + 512],
                              start=True, stop=True).then_inc(h_ps, 1)
                for k in range(2):
                    pe.wait_ge(h_in, k + 1)
                    for j in range(4):
                        pe.matmul(PS[:, k, 128 * j:128 * j + 128], QT[:, 4 * k + j, :], w[:, 4, :],
                                  start=True, stop=False)
                        mm = pe.matmul(PS[:, k, 128 * j:128 * j + 128], self.ones[0:1, :], row[0:1, :],
                                       start=False, stop=True)
                    mm.then_inc(y_ps, 1)

            @block.scalar
            def _(act):
                act.wait_ge(fold_ps, 1)
                act.copy(fold[:, :], PS[:, 7, 0:128]).then_inc(fold_in, 1)
                for k in range(2):
                    act.wait_ge(xt_ps, k + 1)
                    act.copy(flat(XT)[:, 512 * k:512 * k + 512], PS[:, k, :]).then_inc(xt_in, 1)
                for k in range(2):
                    act.wait_ge(qt_ps, k + 1)
                    act.copy(flat(QT)[:, 512 * k:512 * k + 512], PS[:, 2 + k, :]).then_inc(qt_in, 1)

                def one(n, u, known):
                    if live(known, 1, PAIRS):
                        if known is None or known >= 3:
                            act.wait_ge(o_ps, n - 2)
                        for b in range(BANKS):
                            act.wait_ge(pt_ps, 3 * n - 2 + b)
                            act.copy(PT[1 - u][:, 512 * b:512 * b + 512], PS[0:CHUNK, 3 * (1 - u) + b, :]
                                     ).then_inc(pt_in, 1)
                    if live(known, 0, PAIRS):
                        act.wait_ge(top_in, n + 1)
                        if known is None or known >= 2:
                            act.wait_ge(o_in, n - 1)
                        act.activation(P[u][:, :], P[u][:, :], ACT.Exp, bias=small[:, BIAS, u:u + 1],
                                       scale=scale, accum_out=small[:, SUM, u:u + 1]).then_inc(p_in, 1)

                run_steps(act, PAIRS, 1, 2, one)
                for k in range(2):
                    act.wait_ge(ot_ps, k + 1)
                    act.copy(flat(QT)[:, 512 * k:512 * k + 512], PS[:, k, :]).then_inc(ot_in, 1)
                for k in range(2):
                    act.wait_ge(xt_ps, k + 3)
                    act.copy(flat(XT)[:, 512 * k:512 * k + 512], PS[:, 4 + k, :]).then_inc(xt_in, 1)
                for k in range(2):
                    act.wait_ge(h_ps, k + 1)
                    act.activation(flat(QT)[:, 512 * k:512 * k + 512], PS[:, 6 + k, :], ACT.Relu,
                                   bias=col[:, 0:1]).then_inc(h_in, 1)

            @block.vector
            def _(v):
                chain = Chain(v, step)

                def one(n, u, known):
                    if live(known, 0, PAIRS):
                        chain.base, chain.n = n, 0
                        E = PS[:, 3 * u:3 * u + 3, 0:BANK_KEYS]
                        Pv = P[u][:, :].rearrange("p (b k) -> p b k", b=BANKS)
                        v.wait_ge(e_ps, n + 1)
                        if known is None or known >= 2:
                            v.wait_ge(pt_ps, 3 * n - 3)
                        v.tensor_scalar(Pv, E, 0.0, None, ALU.not_equal, ALU.add,
                                        accum_out=small[:, COUNT, u:u + 1]).then_inc(cnt_in, 1)
                        v.wait_ge(len_ps, n + 1)
                        v.tensor_copy(small[:, LENGTH, u:u + 1], PS[:, 6 + u, 256:257]).then_inc(len_in, 1)
                        v.wait_ge(len_in, n + 1)
                        if known is None or known >= 1:
                            v.wait_ge(top_in, n)
                        v.tensor_scalar(pad[:, :], kidx[:, :], small[:, LENGTH, u:u + 1], NEG,
                                        ALU.is_ge, ALU.mult).then_inc(pad_in, 1)
                        v.wait_ge(pad_in, n + 1)
                        settle(v, self.passed)
                        chain(v.tensor_tensor_reduce(
                            Pv, E, pad[:, :].rearrange("p (b k) -> p b k", b=BANKS), 1.0, -3.4e38, ALU.add,
                            ALU.max, small[:, TOP, u:u + 1]))
                        v.tensor_scalar(small[:, BIAS, u:u + 1], small[:, TOP, u:u + 1], -scale, None,
                                        ALU.mult).then_inc(top_in, 1)
                    if live(known, 1, PAIRS):
                        v.wait_ge(o_ps, n)
                        v.reciprocal(small[:, INV, 1 - u:2 - u], small[:, SUM, 1 - u:2 - u]).then_inc(inv_in, 1)
                        v.wait_ge(inv_in, n)
                        v.tensor_scalar(ON[:, bass.ds(n - 1, 1), :].rearrange("p a d -> p (a d)"),
                                        PS[:, 7 - u, 0:D], small[:, INV, 1 - u:2 - u], None,
                                        ALU.mult).then_inc(o_in, 1)

                run_steps(v, PAIRS, 1, 2, one)
                chain.base, chain.n = PAIRS, 0
                v.wait_ge(z_ps, 2)
                Z = PS[:, 2:4, :].rearrange("p a (j m) -> p (a j) m", m=128)
                chain(v.tensor_tensor(ON[:, :, :], Z, XN[:, :, :], ALU.add))
                layer_norm(v, chain, XN, ON, ln, 1e-5)
                v.wait_ge(w_in, 16 * 11)
                self.affine(v, chain, XN, gb[:, 0, :, :])
                v.sem_inc(n2_ready, 1)
                v.wait_ge(y_ps, 2)
                Z = PS[:, 0:2, :].rearrange("p a (j m) -> p (a j) m", m=128)
                chain(v.tensor_tensor(ON[:, :, :], Z, XN[:, :, :], ALU.add))
                layer_norm(v, chain, XN, ON, ln, 1e-5)
                self.affine(v, chain, XN, gb[:, 1, :, :])
                chain(v.tensor_tensor(X[:, :, :], X[:, :, :], XN[:, :, :], ALU.add))

    def quantised_ffn(self):
        nc, t = self.nc, self.t
        self.stage = "l1q"
        X, XN, ident, PS = self.X, self.XN, self.ident, self.PS
        BLOCK, ROUND = 32, 12582912.0
        with ExitStack() as ctx:
            XT = self.sb(ctx, "XT", [128, PAIRS * 128])
            W = self.sb(ctx, "W", [128, 3 * FFN1])
            WQ = self.sb(ctx, "WQ", [128, 3 * FFN1])
            WT = self.sb(ctx, "WT", [128, 3 * GCHUNKS, 128])
            wmax = self.sb(ctx, "wmax", [128, 3, 3 * FFN1 // BLOCK])
            U = self.sb(ctx, "U", [128, GCHUNKS * 1024])
            Gt = self.sb(ctx, "G", [128, GCHUNKS * 1024])
            SG = self.sb(ctx, "SG", [128, GCHUNKS * 1024])
            red = self.sb(ctx, "red", [128, 4])
            top1 = self.sb(ctx, "top1", [1, 1])
            ln = self.norm_scratch(ctx)
            (w_in, wq_ready, wt_ps, wt_in, x_ready, xt_ps, xt_in, top_in, top_ps, top1_in, all_ps, u_ps,
             u_in, g_ps, g_in, sig_ready, sig_in, o_ready, z_ps, step) = (self.sem(ctx, n) for n in (
                 "w_in", "wq_ready", "wt_ps", "wt_in", "x_ready", "xt_ps", "xt_in", "top_in", "top_ps",
                 "top1_in", "all_ps", "u_ps", "u_in", "g_ps", "g_in", "sig_ready", "sig_in", "o_ready",
                 "z_ps", "step"))
            block = ctx.enter_context(nc.Block())

            @block.sync
            def _(sp):
                for k, name in enumerate(("up", "gate")):
                    sp.dma_start(W[:, FFN1 * k:FFN1 * k + FFN1].rearrange("p (c i) -> p c i", i=128),
                                 t[f"L1_ffn_w_{name}"].rearrange("(c p) i -> p c i", p=128)).then_inc(w_in, 16)
                sp.dma_start(W[:, 2 * FFN1:3 * FFN1], t["L1_ffn_w_down"]).then_inc(w_in, 16)

            @block.tensor
            def _(pe):
                tops = [0]

                def spread():
                    n = tops[0] = tops[0] + 1
                    pe.wait_ge(top_in, n)
                    pe.transpose(PS[0:1, 7, 0:128], red[:, 0:1], ident[:, :]).then_inc(top_ps, 1)
                    pe.wait_ge(top1_in, n)
                    pe.matmul(PS[:, 7, 256:257], self.ones[0:1, :], top1[0:1, 0:1], start=True,
                              stop=True).then_inc(all_ps, 1)

                pe.wait_ge(wq_ready, 1)
                for k in range(3):
                    for j in range(GCHUNKS):
                        at = FFN1 * k + 128 * j
                        mm = pe.transpose(PS[:, k, 128 * j:128 * j + 128], WQ[:, at:at + 128], ident[:, :])
                    mm.then_inc(wt_ps, 1)
                spread()
                pe.wait_ge(x_ready, 1)
                for k in range(2):
                    for j in range(4):
                        mm = pe.transpose(PS[:, 4 + k, 128 * j:128 * j + 128], XN[:, 4 * k + j, :], ident[:, :])
                    mm.then_inc(xt_ps, 1)
                pe.wait_ge(wt_in, 3)
                pe.wait_ge(xt_in, 2)
                for k, done in ((0, u_ps), (1, g_ps)):
                    for b in range(6):
                        if k:
                            pe.wait_ge(u_in, b + 1)
                        pe.matmul(PS[:, b, :], WT[:, GCHUNKS * k + b // 2, :],
                                  XT[:, 512 * (b % 2):512 * (b % 2) + 512], start=True, stop=True
                                  ).then_inc(done, 1)
                for _ in range(4):
                    spread()
                pe.wait_ge(o_ready, 1)
                for p in range(PAIRS):
                    for j in range(GCHUNKS):
                        mm = pe.matmul(PS[:, p // 4, 128 * (p % 4):128 * (p % 4) + 128],
                                       U[:, 1024 * j + 128 * p:1024 * j + 128 * p + 128],
                                       WT[:, 2 * GCHUNKS + j, :], start=(j == 0), stop=(j == GCHUNKS - 1))
                    if p % 4 == 3:
                        mm.then_inc(z_ps, 1)

            @block.scalar
            def _(act):
                for k in range(3):
                    act.wait_ge(wt_ps, k + 1)
                    act.copy(WT[:, GCHUNKS * k:GCHUNKS * k + GCHUNKS, :].rearrange("p c m -> p (c m)"),
                             PS[:, k, 0:FFN1]).then_inc(wt_in, 1)
                for k in range(2):
                    act.wait_ge(xt_ps, k + 1)
                    act.copy(XT[:, 512 * k:512 * k + 512], PS[:, 4 + k, :]).then_inc(xt_in, 1)
                for dst, ps, done in ((U, u_ps, u_in), (Gt, g_ps, g_in)):
                    for b in range(6):
                        act.wait_ge(ps, b + 1)
                        act.copy(dst[:, 512 * b:512 * b + 512], PS[:, b, :]).then_inc(done, 1)
                act.wait_ge(sig_ready, 1)
                act.activation(SG[:, :], Gt[:, :], ACT.Sigmoid).then_inc(sig_in, 1)

            @block.vector
            def _(v):
                chain = Chain(v, step)
                tops = [0]

                def scale_of(a):
                    n = tops[0] = tops[0] + 1
                    v.tensor_reduce(red[:, 0:1], a, X_AXIS, ALU.max, apply_absolute_value=True).then_inc(top_in, 1)
                    v.wait_ge(top_ps, n)
                    v.tensor_reduce(top1[0:1, 0:1], PS[0:1, 7, 0:128], X_AXIS, ALU.max).then_inc(top1_in, 1)
                    v.wait_ge(all_ps, n)
                    chain(v.tensor_scalar(red[:, 1:2], PS[:, 7, 256:257], 1.0 / 32767.0, 1e-12, ALU.mult, ALU.max))
                    chain(v.reciprocal(red[:, 2:3], red[:, 1:2]))

                def qdq(a):
                    chain(v.tensor_scalar(a, a, red[:, 2:3], ROUND, ALU.mult, ALU.add))
                    chain(v.tensor_scalar(a, a, -ROUND, 32767.0, ALU.add, ALU.min))
                    chain(v.tensor_scalar(a, a, -32768.0, red[:, 1:2], ALU.max, ALU.mult))

                wb = W[:, :].rearrange("p (n k) -> p n k", k=BLOCK)
                wq = WQ[:, :].rearrange("p (n k) -> p n k", k=BLOCK)
                wide = lambda r: r.unsqueeze(2).to_broadcast([128, 3 * FFN1 // BLOCK, BLOCK])
                v.wait_ge(w_in, 48)
                chain(v.tensor_reduce(wmax[:, 0, :], wb, X_AXIS, ALU.max, apply_absolute_value=True))
                chain(v.tensor_scalar(wmax[:, 1, :], wmax[:, 0, :], 1.0 / 7.0, 1e-12, ALU.mult, ALU.max))
                chain(v.reciprocal(wmax[:, 2, :], wmax[:, 1, :]))
                chain(v.tensor_tensor(wq, wb, wide(wmax[:, 2, :]), ALU.mult))
                chain(v.tensor_scalar(WQ[:, :], WQ[:, :], ROUND, -ROUND, ALU.add, ALU.add))
                chain(v.tensor_scalar(WQ[:, :], WQ[:, :], 7.0, -8.0, ALU.min, ALU.max))
                v.tensor_tensor(wq, wq, wide(wmax[:, 1, :]), ALU.mult).then_inc(wq_ready, 1)
                layer_norm(v, chain, XN, X, ln, 1e-5)
                xn = XN[:, :, :].rearrange("p t d -> p (t d)")
                chain(v.tensor_scalar(xn, xn, self.rowmask[:, 0:1], None, ALU.mult))
                scale_of(xn)
                qdq(xn)
                v.sem_inc(x_ready, 1)
                v.wait_ge(u_in, 6)
                scale_of(U[:, :])
                qdq(U[:, :])
                v.wait_ge(g_in, 6)
                scale_of(Gt[:, :])
                qdq(Gt[:, :])
                v.sem_inc(sig_ready, 1)
                v.wait_ge(sig_in, 1)
                chain(v.tensor_scalar(SG[:, :], SG[:, :], 65536.0, ROUND, ALU.mult, ALU.add))
                chain(v.tensor_scalar(SG[:, :], SG[:, :], -ROUND, 0.0, ALU.add, ALU.max))
                chain(v.tensor_scalar(SG[:, :], SG[:, :], 65535.0, 1.0 / 65536.0, ALU.min, ALU.mult))
                chain(v.tensor_tensor(Gt[:, :], Gt[:, :], SG[:, :], ALU.mult))
                scale_of(Gt[:, :])
                qdq(Gt[:, :])
                chain(v.tensor_tensor(U[:, :], Gt[:, :], U[:, :], ALU.mult))
                scale_of(U[:, :])
                qdq(U[:, :])
                v.sem_inc(o_ready, 1)
                v.wait_ge(z_ps, 2)
                chain(v.tensor_tensor(X[:, :, :], PS[:, 0:2, :].rearrange("p a (j m) -> p (a j) m", m=128),
                                      X[:, :, :], ALU.add))

    def unit_ffn(self):
        nc, t = self.nc, self.t
        self.stage = "l2f"
        X, XN, ident, PS = self.X, self.XN, self.ident, self.PS
        JJ = INNER // 2
        with ExitStack() as ctx:
            XT = self.sb(ctx, "XT", [128, PAIRS * 128])
            win = self.sb(ctx, "win", [128, 2, M2])
            bin_ = self.sb(ctx, "bin", [128, 1])
            cols = self.sb(ctx, "cols", [128, 3, JJ])
            wout = self.sb(ctx, "wout", [128, D])
            b2 = self.sb(ctx, "b2", [M2, 1])
            bout = self.sb(ctx, "bout", [1, D])
            crow = self.sb(ctx, "crow", [1, D])
            WO = self.sb(ctx, "WO", [128, JJ, D])
            S = self.sb(ctx, "S", [128, PAIRS * 128])
            H = self.sb(ctx, "H", [128, JJ, PAIRS * 128])
            ln = self.norm_scratch(ctx)
            (w_in, c_ps, c_in, xn_ready, xt_ps, xt_in, s_ps, s_in, h_in, wo_in, z_ps, step) = (
                self.sem(ctx, n) for n in ("w_in", "c_ps", "c_in", "xn_ready", "xt_ps", "xt_in", "s_ps",
                                           "s_in", "h_in", "wo_in", "z_ps", "step"))
            block = ctx.enter_context(nc.Block())
            DMAS = 14

            @block.sync
            def _(sp):
                for par in range(2):
                    rows = slice(M2 * par, M2 * par + M2)
                    sp.dma_start(win[:, par, :], t["L2_ffn_Win"]).then_inc(w_in, 16)
                    sp.dma_start(bin_[rows, :], t["L2_ffn_bin_"].unsqueeze(1)).then_inc(w_in, 16)
                    sp.dma_start(wout[rows, :], t["L2_ffn_Wout"]).then_inc(w_in, 16)
                    for k, name in enumerate(("W1", "b1", "W2")):
                        sp.dma_start(cols[rows, k, :], t[f"L2_ffn_{name}_halves"][par]).then_inc(w_in, 16)
                sp.dma_start(b2[:, :], t["L2_ffn_b2"].unsqueeze(1)).then_inc(w_in, 16)
                sp.dma_start(bout[:, :], t["L2_ffn_bout"].unsqueeze(0)).then_inc(w_in, 16)

            @block.tensor
            def _(pe):
                pe.wait_ge(w_in, 16 * DMAS)
                pe.matmul(PS[0:1, 7, 0:D], b2[:, :], wout[0:M2, :], start=True, stop=True).then_inc(c_ps, 1)
                pe.wait_ge(xn_ready, 1)
                for k in range(2):
                    for j in range(4):
                        mm = pe.transpose(PS[:, k, 128 * j:128 * j + 128], XN[:, 4 * k + j, :], ident[:, :])
                    mm.then_inc(xt_ps, 1)
                for k in range(2):
                    pe.wait_ge(xt_in, k + 1)
                    pe.matmul(PS[:, 2 + k, :], win[:, :, :].rearrange("p a m -> p (a m)"),
                              XT[:, 512 * k:512 * k + 512], start=True, stop=True).then_inc(s_ps, 1)
                pe.wait_ge(wo_in, 1)
                pe.wait_ge(c_in, 1)
                for p in range(PAIRS):
                    z = PS[:, 4 + p // 4, 128 * (p % 4):128 * (p % 4) + 128]
                    pe.matmul(z, self.ones[0:1, :], crow[0:1, :], start=True, stop=False)
                    for j in range(JJ):
                        if p == 0:
                            pe.wait_ge(h_in, j + 1)
                        mm = pe.matmul(z, H[:, j, 128 * p:128 * p + 128], WO[:, j, :], start=False,
                                       stop=(j == JJ - 1))
                    if p % 4 == 3:
                        mm.then_inc(z_ps, 1)

            @block.scalar
            def _(act):
                for k in range(2):
                    act.wait_ge(xt_ps, k + 1)
                    act.copy(XT[:, 512 * k:512 * k + 512], PS[:, k, :]).then_inc(xt_in, 1)
                act.wait_ge(w_in, 16 * DMAS)
                for k in range(2):
                    act.wait_ge(s_ps, k + 1)
                    act.activation(S[:, 512 * k:512 * k + 512], PS[:, 2 + k, :], ACT.Identity,
                                   bias=bin_[:, 0:1]).then_inc(s_in, 1)
                act.wait_ge(s_in, 2)
                for j in range(JJ):
                    act.activation(H[:, j, :], S[:, :], ACT.Relu, bias=cols[:, 1, j:j + 1],
                                   scale=cols[:, 0, j:j + 1]).then_inc(h_in, 1)

            @block.vector
            def _(v):
                chain = Chain(v, step)
                layer_norm(v, chain, XN, X, ln, 1e-5)
                v.sem_inc(xn_ready, 1)
                v.wait_ge(w_in, 16 * DMAS)
                for j in range(JJ):
                    last = v.tensor_scalar(WO[:, j, :], wout[:, :], cols[:, 2, j:j + 1], None, ALU.mult)
                last.then_inc(wo_in, 1)
                v.wait_ge(c_ps, 1)
                v.tensor_tensor(crow[0:1, :], PS[0:1, 7, 0:D], bout[0:1, :], ALU.add).then_inc(c_in, 1)
                v.wait_ge(z_ps, 2)
                chain(v.tensor_tensor(X[:, :, :], PS[:, 4:6, :].rearrange("p a (j m) -> p (a j) m", m=128),
                                      X[:, :, :], ALU.add))

    def head_attention(self, stage, J, weights, padded):
        nc, t = self.nc, self.t
        self.stage = stage
        X, XN, ident, PS = self.X, self.XN, self.ident, self.PS
        scale = 1.0 / float(np.sqrt(float(J)))
        with ExitStack() as whole:
            QP = self.sb(whole, "QP", [128, BATCH * ROWS])
            CH = self.sb(whole, "CH", [128, HEADS, D])
            cout = self.sb(whole, "cout", [128, 1])
            wx = self.sb(whole, "wx", [128, D])
            XT = self.sb(whole, "XT", [128, PAIRS, 128])
            QH = [self.sb(whole, f"QH{s}", [128, 128], F32R) for s in range(2)]
            QL = [self.sb(whole, f"QL{s}", [128, 128], F32R) for s in range(2)]
            heads = lambda g: QP[:, :].rearrange("p (b h q) -> p b h q", b=BATCH, h=HEADS)[
                :, 8 * g:8 * g + 8]
            tokens = lambda g: XT[:, 4 * g:4 * g + 4, :].rearrange("p t (a q) -> p (t a) q", a=2)[
                :, :, 0:TOK]
            cT, c = self.sb(whole, "cT", [128, KEYS]), self.sb(whole, "c", [CHUNK, CHUNKS * D])
            raw_in = self.sem(whole, "raw_in")

            def load_context(sp, b):
                one = bass.ds(b, 1)
                sp.dma_start(cT[:, :], t["ctxT"][one].rearrange("a d k -> d (a k)")).then_inc(raw_in, 16)
                sp.dma_start(c[:, :].rearrange("k (c d) -> k c d", d=D), t["ctx_1024"][one].rearrange(
                    "a (c k) d -> k (a c) d", k=CHUNK)).then_inc(raw_in, 16)

            self.fold_heads(stage, J, scale, QP, CH, cout, wx, XT, heads, tokens, weights, load_context)
            self.attend(stage, QP, QH, QL, padded, cT, c, raw_in, load_context)
            self.combine(stage, QP, CH, cout, wx, XT, heads, tokens, weights)

    def fold_heads(self, stage, J, scale, QP, CH, cout, wx, XT, heads, tokens, weights,
                   load_context):
        nc, t = self.nc, self.t
        self.stage = stage + "fold"
        X, XN, ident, PS = self.X, self.XN, self.ident, self.PS
        query_out = weights.get("query_out")
        with ExitStack() as ctx:
            names = ("wqT", "wkT", "wvT") if weights["wkT"] is not weights["wvT"] else ("wqT", "wkT")
            W = {k: self.sb(ctx, k, [J, HEADS, D]) for k in (*names, "wo")}
            if "wvT" not in W:
                W["wvT"] = W["wkT"]
            wide = self.sb(ctx, "wide", [128, 4, HEADS * J])
            bo = self.sb(ctx, "bo", [128, 1])
            cq = self.sb(ctx, "cq", [128, HEADS])
            BH = self.sb(ctx, "BH", [128, HEADS, D])
            ln = self.norm_scratch(ctx)
            (w_in, b_ps, b_in, wide_in, c_in, xn_ready, xt_ps, xt_in, q_ps, q_in, step, ql_ps) = (
                self.sem(ctx, n) for n in ("w_in", "b_ps", "b_in", "wide_in", "c_in", "xn_ready", "xt_ps",
                                           "xt_in", "q_ps", "q_in", "step", "ql_ps"))
            DMAS = len(names) + 1 + (1 if query_out is not None else 0)
            block = ctx.enter_context(nc.Block())

            @block.sync
            def _(sp):
                for k in names:
                    sp.dma_start(W[k][:, :, :], weights[k].rearrange("(h j) d -> j h d", j=J)).then_inc(w_in, 16)
                sp.dma_start(W["wo"][:, :, :], weights["wo"].rearrange("(h j) d -> j h d", j=J)).then_inc(w_in, 16)
                if query_out is not None:
                    sp.dma_start(wx[:, :], query_out).then_inc(w_in, 16)
                sp.dma_start(bo[:, :], weights["bo"].unsqueeze(1)).then_inc(wide_in, 16)
                for k, name in enumerate(("wk", "woT", "bq", "bv")):
                    src = weights[name] if k < 2 else weights[name].partition_broadcast(128)
                    sp.dma_start(wide[:, k, :], src).then_inc(wide_in, 16)
                load_context(sp, 0)

            @block.tensor
            def _(pe):
                pe.wait_ge(w_in, 16 * DMAS)
                for k, (a, b) in enumerate((("wqT", "wkT"), ("wvT", "wo"))):
                    for g in range(4):
                        for j in range(4):
                            h = 4 * g + j
                            mm = pe.matmul(PS[:, 4 * (k % 2) + g, 128 * j:128 * j + 128], W[a][:, h, :],
                                           W[b][:, h, :], start=True, stop=True)
                        mm.then_inc(b_ps, 1)
                pe.wait_ge(xn_ready, 1)
                pe.wait_ge(b_in, 4)
                for k in range(2):
                    for j in range(4):
                        mm = pe.transpose(PS[:, 2 + k, 128 * j:128 * j + 128], XN[:, 4 * k + j, :], ident[:, :])
                    mm.then_inc(xt_ps, 1)
                pe.wait_ge(xt_in, 2)
                pe.wait_ge(b_in, 8)
                for n in range(2 * HEADS):
                    if n >= 4:
                        pe.wait_ge(q_in if n % 2 == 0 else ql_ps, (n - 4) // 2 + 1)
                    pe.matmul(PS[:, 4 + n % 4, 0:HALF_TOK], BH[:, n // 2, :], tokens(n % 2),
                              start=True, stop=True).then_inc(q_ps, 1)

            def queries(eng, n):
                dst = heads(n % 2)[:, :, n // 2, :]
                src = PS[:, 4 + n % 4, 0:HALF_TOK].rearrange("p (b q) -> p b q", q=TOK)
                return dst, src

            @block.scalar
            def _(act):
                for g in range(8):
                    act.wait_ge(b_ps, g + 1)
                    dst = BH if g < 4 else CH
                    act.copy(dst[:, 4 * (g % 4):4 * (g % 4) + 4, :].rearrange("p h d -> p (h d)"),
                             PS[:, g, :]).then_inc(b_in, 1)
                for k in range(2):
                    act.wait_ge(xt_ps, k + 1)
                    act.copy(XT[:, 4 * k:4 * k + 4, :].rearrange("p t m -> p (t m)"), PS[:, 2 + k, :]
                             ).then_inc(xt_in, 1)
                act.wait_ge(c_in, 1)
                for n in range(0, 2 * HEADS, 2):
                    act.wait_ge(q_ps, n + 1)
                    dst, src = queries(act, n)
                    act.activation(dst, src, ACT.Identity, bias=cq[:, n // 2:n // 2 + 1], scale=scale
                                   ).then_inc(q_in, 1)

            @block.vector
            def _(v):
                chain = Chain(v, step)
                layer_norm(v, chain, XN, X, ln, 1e-5)
                v.sem_inc(xn_ready, 1)
                v.wait_ge(wide_in, 16 * 5)
                for k in range(2):
                    chain(v.tensor_tensor(wide[:, k, :], wide[:, k, :], wide[:, 2 + k, :], ALU.mult))
                chain(v.tensor_reduce(cq[:, :], wide[:, 0, :].rearrange("p (h j) -> p h j", j=J), X_AXIS,
                                      ALU.add))
                chain(v.tensor_scalar(cq[:, :], cq[:, :], scale, None, ALU.mult))
                chain(v.tensor_reduce(cout[:, :], wide[:, 1, :], X_AXIS, ALU.add))
                chain(v.tensor_tensor(cout[:, :], cout[:, :], bo[:, :], ALU.add))
                v.sem_inc(c_in, 1)
                for n in range(1, 2 * HEADS, 2):
                    v.wait_ge(q_ps, n + 1)
                    dst, src = queries(v, n)
                    v.tensor_scalar(dst, src, scale, cq[:, n // 2:n // 2 + 1], ALU.mult, ALU.add
                                    ).then_inc(ql_ps, 1)

    def attend(self, stage, QP, QH, QL, padded, cT, c, raw_in, load_context):
        nc, t = self.nc, self.t
        self.stage = stage + "att"
        ident, PS = self.ident, self.PS
        with ExitStack() as ctx:
            cTh, cTl = (self.sb(ctx, n, [128, 2, KEYS], F32R) for n in ("cTh", "cTl"))
            cc = self.sb(ctx, "cc", [CHUNK, 2, CHUNKS, 2, D], F32R)
            P = [self.sb(ctx, f"P{s}", [128, KEYS]) for s in range(2)]
            PTh = [self.sb(ctx, f"PTh{s}", [CHUNK, CHUNKS * 128], F32R) for s in range(2)]
            PTl = [self.sb(ctx, f"PTl{s}", [CHUNK, CHUNKS * 128], F32R) for s in range(2)]
            O = [self.sb(ctx, f"O{s}", [128, D]) for s in range(2)]
            top = self.sb(ctx, "top", [128, 2])
            neg = self.sb(ctx, "neg", [128, 2])
            total, inv = self.sb(ctx, "total", [128, 4]), self.sb(ctx, "inv", [128, 4])
            (high_first, low_first, split, split_step, q_in, e_ps, top_in, p_in, pt_ps, hi_in, lo_in, o_ps, o_in,
             inv_in, ot_ps, ot_in, mask_in, o_low) = (self.sem(ctx, n) for n in (
                 "high_first", "low_first", "split", "split_step", "q_in", "e_ps", "top_in", "p_in", "pt_ps", "hi_in",
                 "lo_in", "o_ps", "o_in", "inv_in", "ot_ps", "ot_in", "mask_in",
                 "o_low"))
            if padded:
                mask8 = [self.sb(ctx, f"mask8_{s}", [128, KEYS], U8) for s in range(2)]
                maskb = self.sb(ctx, "maskb", [128, KEYS])
                mask_raw, topped = [self.sem(ctx, f"mask_raw{s}") for s in range(2)], self.sem(ctx, "topped")
            block = ctx.enter_context(nc.Block())
            UNROLL, LAG, BT = 4, 3, BATCH_TILES

            @block.sync
            def _(sp):
                def load(b, u, known):
                    if not live(known, 0, BATCH):
                        return
                    if known is None or known >= 1:
                        sp.wait_ge(split, b)
                        load_context(sp, b)
                    if padded:
                        if known is None or known >= 2:
                            sp.wait_ge(mask_in, b - 1)
                            settle(sp, self.passed)
                        sp.dma_start(mask8[u][:, :], t["mask"][bass.ds(b, 1)].to_broadcast([128, KEYS])
                                     ).then_inc(mask_raw[u], 16)

                run_steps(sp, BATCH, 2, 2, load)

            @block.gpsimd
            def _(g):
                chain = Chain(g, split_step)

                def split_part(b, slot, k):
                    if k < 2:
                        src, hi, lo = cT[:, :], cTh[:, slot, :], cTl[:, slot, :]
                    else:
                        src, hi, lo = (c[:, :].rearrange("k (c d) -> k c d", d=D), cc[:, slot, :, 0, :],
                                       cc[:, slot, :, 1, :])
                    if k % 2 == 0:
                        settle(g, self.passed)
                        ins = g.tensor_copy(hi, src)
                    else:
                        ins = g.tensor_tensor(lo, src, hi, ALU.subtract)
                    chain(ins)

                def split_query(n, m):
                    if not (isinstance(n, int) and n < 2):
                        g.wait_ge(e_ps, n - 1)
                    at = bass.ds(n * 128, 128)
                    chain(g.tensor_copy(QH[m % 2][:, :], QP[:, at]))
                    settle(g, self.passed)
                    g.tensor_tensor(QL[m % 2][:, :], QP[:, at], QH[m % 2][:, :], ALU.subtract).then_inc(q_in, 1)

                def batch_pair(i, last):
                    for s in range(2):
                        b = 2 * i + s
                        chain.base = (2 * BT + 8) * i + (BT + 4) * s
                        chain.n = 0
                        more = not (last and s == 1)
                        for j in range(BT):
                            split_query(BT * b + j, BT * s + j)
                            if padded and j == 1:
                                g.wait_ge(mask_raw[s], 16 * i + 16)
                                g.wait_ge(top_in, BT * b)
                                settle(g, self.passed)
                                g.tensor_scalar(maskb[:, :], mask8[s][:, :], NEG, None,
                                                ALU.mult).then_inc(mask_in, 1)
                            if more and 2 <= j <= 5:
                                if j == 2:
                                    g.wait_ge(raw_in, 32 * b + 64)
                                    g.wait_ge(o_ps, BT * b)
                                split_part(b + 1, 1 - s, j - 2)
                                if j == 5:
                                    g.sem_inc(split, 1)

                batch_pair(0, False)
                with g.Fori(1, BATCH // 2 - 1) as i:
                    batch_pair(i, False)
                batch_pair(BATCH // 2 - 1, True)

            @block.tensor
            def _(pe):
                def one(n, u, known):
                    s, s1 = u % 2, (u + 1) % 2
                    if live(known, 0, TILES):
                        b = n // BT
                        pe.wait_ge(split, b + 1)
                        pe.wait_ge(q_in, n + 1)
                        off = pe.snap((b % 2) * KEYS) if known is None else (b % 2) * KEYS
                        th, tl = (x[:, :, :].rearrange("p s k -> p (s k)") for x in (cTh, cTl))
                        for g in range(BANKS):
                            if known is None or known >= 2:
                                pe.wait_ge(lo_in, 3 * n - 5 + g)
                            at = bass.ds(off + BANK_KEYS * g, BANK_KEYS)
                            e = PS[:, 3 * s + g, 0:BANK_KEYS]
                            pe.matmul(e, QH[s][:, :], th[:, at], start=True, stop=False)
                            pe.matmul(e, QH[s][:, :], tl[:, at], start=False, stop=False)
                            mm = pe.matmul(e, QL[s][:, :], th[:, at], start=False, stop=True)
                        mm.then_inc(e_ps, 1)
                    if live(known, 1, TILES):
                        pe.wait_ge(p_in, n)
                        for g in range(BANKS):
                            for j in range(4):
                                at = CHUNK * (4 * g + j)
                                mm = pe.transpose(PS[0:CHUNK, 3 * s1 + g, 128 * j:128 * j + 128],
                                                  P[s1][:, at:at + CHUNK], ident[:, :])
                            mm.then_inc(pt_ps, 1)
                    if live(known, 3, TILES):
                        pe.wait_ge(o_in, n - 2)
                        pe.transpose(PS[:, 6 + s1, 256:384], O[s1][:, :], ident[:, :]).then_inc(ot_ps, 1)
                    if live(known, 2, TILES):
                        pe.wait_ge(lo_in, 3 * n - 3)
                        if known is None or known >= 4:
                            pe.wait_ge(ot_in, n - 3)
                        b2 = (n - 2) // BT
                        SLOT = CHUNKS * 2 * D
                        off2 = pe.snap((b2 % 2) * SLOT) if known is None else (b2 % 2) * SLOT
                        parts = cc[:, :, :, :, :].rearrange("p s c h d -> p (s c h d)")
                        for k in range(CHUNKS):
                            cols = slice(128 * k, 128 * k + 128)
                            at = bass.ds(off2 + 2 * D * k, 2 * D)
                            o = PS[:, 6 + s, 0:2 * D]
                            pe.matmul(o, PTh[s][:, cols], parts[:, at], start=(k == 0), stop=False)
                            mm = pe.matmul(o, PTl[s][:, cols], parts[:, at], start=False,
                                           stop=(k == CHUNKS - 1))
                        mm.then_inc(o_ps, 1)

                run_steps(pe, TILES, LAG, UNROLL, one)

            @block.scalar
            def _(act):
                def one(n, u, known):
                    s, s1 = u % 2, (u + 1) % 2
                    if live(known, 1, TILES):
                        if known is None or known >= 3:
                            act.wait_ge(o_ps, n - 2)
                        for g in range(BANKS):
                            act.wait_ge(pt_ps, 3 * n - 2 + g)
                            act.copy(PTh[s1][:, 512 * g:512 * g + 512], PS[0:CHUNK, 3 * s1 + g, :]
                                     ).then_inc(hi_in, 1)
                    if live(known, 0, TILES):
                        act.wait_ge(top_in, n + 1)
                        if known is None or known >= 2:
                            act.wait_ge(pt_ps, 3 * n - 3)
                        if known is None or known >= 4:
                            act.wait_ge(inv_in, n - 3)
                        Pv = P[s][:, :].rearrange("p (b k) -> p b k", b=BANKS)
                        act.activation(Pv, Pv if padded else PS[:, 3 * s:3 * s + 3, 0:BANK_KEYS], ACT.Exp,
                                       bias=neg[:, s:s + 1], accum_out=total[:, u:u + 1]).then_inc(p_in, 1)
                    if live(known, 3, TILES):
                        act.wait_ge(ot_ps, n - 2)
                        act.copy(QP[:, bass.ds((n - 3) * 128, 128)], PS[:, 6 + s1, 256:384]).then_inc(ot_in, 1)

                act.wait_ge(raw_in, 32)
                act.copy(cTh[:, 0, :], cT[:, :]).then_inc(high_first, 1)
                act.copy(cc[:, 0, :, 0, :], c[:, :].rearrange("k (c d) -> k c d", d=D)).then_inc(high_first, 1)
                run_steps(act, TILES, LAG, UNROLL, one)

            @block.vector
            def _(v):
                def one(n, u, known):
                    s, s1 = u % 2, (u + 1) % 2
                    if live(known, 0, TILES):
                        v.wait_ge(e_ps, n + 1)
                        E = PS[:, 3 * s:3 * s + 3, 0:BANK_KEYS]
                        if padded:
                            v.wait_ge(mask_in, n // BT + 1)
                            if known is None or known >= 2:
                                v.wait_ge(pt_ps, 3 * n - 3)
                            settle(v, self.passed)
                            v.tensor_tensor_reduce(
                                P[s][:, :].rearrange("p (b k) -> p b k", b=BANKS), E,
                                maskb[:, :].rearrange("p (b k) -> p b k", b=BANKS), 1.0, -3.4e38, ALU.add,
                                ALU.max, top[:, s:s + 1]).then_inc(topped, 1)
                            v.wait_ge(topped, n + 1)
                            v.tensor_scalar(neg[:, s:s + 1], top[:, s:s + 1], -1.0, None,
                                            ALU.mult).then_inc(top_in, 1)
                        else:
                            v.tensor_reduce(neg[:, s:s + 1], E, XY_AXES, ALU.max, negate=True
                                            ).then_inc(top_in, 1)
                    if live(known, 1, TILES):
                        for g in range(BANKS):
                            v.wait_ge(hi_in, 3 * n - 2 + g)
                            v.tensor_tensor(PTl[s1][:, 512 * g:512 * g + 512], PS[0:CHUNK, 3 * s1 + g, :],
                                            PTh[s1][:, 512 * g:512 * g + 512], ALU.subtract).then_inc(lo_in, 1)
                        u1 = (u - 1) % 4
                        v.reciprocal(inv[:, u1:u1 + 1], total[:, u1:u1 + 1]).then_inc(inv_in, 1)
                    if live(known, 2, TILES):
                        u2 = (u - 2) % 4
                        v.wait_ge(o_ps, n - 1)
                        v.wait_ge(inv_in, n - 1)
                        if known is None or known >= 4:
                            v.wait_ge(ot_ps, n - 3)
                        v.tensor_scalar(O[s][:, :], PS[:, 6 + s, D:2 * D], inv[:, u2:u2 + 1], None,
                                        ALU.mult).then_inc(o_low, 1)
                        v.wait_ge(o_low, n - 1)
                        v.scalar_tensor_tensor(out=O[s][:, :], in0=PS[:, 6 + s, 0:D],
                                               scalar=inv[:, u2:u2 + 1], in1=O[s][:, :], op0=ALU.mult,
                                               op1=ALU.add).then_inc(o_in, 1)

                v.wait_ge(high_first, 1)
                v.tensor_tensor(cTl[:, 0, :], cT[:, :], cTh[:, 0, :], ALU.subtract).then_inc(low_first, 1)
                v.wait_ge(high_first, 2)
                v.tensor_tensor(cc[:, 0, :, 1, :], c[:, :].rearrange("k (c d) -> k c d", d=D),
                                cc[:, 0, :, 0, :], ALU.subtract).then_inc(low_first, 1)
                v.wait_ge(low_first, 2)
                v.sem_inc(split, 1)
                run_steps(v, TILES, LAG, UNROLL, one)

    def combine(self, stage, QP, CH, cout, wx, XT, heads, tokens, weights):
        nc, t = self.nc, self.t
        self.stage = stage + "comb"
        X, XN, ident, PS = self.X, self.XN, self.ident, self.PS
        query_out, norm = weights.get("query_out"), weights.get("norm")
        with ExitStack() as ctx:
            ZT = self.sb(ctx, "ZT", [128, BATCH, HALF])
            gb = self.sb(ctx, "gb", [128, 2, D])
            Z = self.sb(ctx, "Z", [128, PAIRS, D])
            ln = self.norm_scratch(ctx)
            gb_in, zeroed, zt_ps, zt_in, z_ps, step = (self.sem(ctx, n) for n in (
                "gb_in", "zeroed", "zt_ps", "zt_in", "z_ps", "step"))
            block = ctx.enter_context(nc.Block())

            if norm:
                @block.sync
                def _(sp):
                    for k in range(2):
                        sp.dma_start(gb[:, k, :], norm[k].partition_broadcast(128)).then_inc(gb_in, 16)

            @block.tensor
            def _(pe):
                for g in range(2):
                    z = PS[:, g, 0:HALF_TOK]
                    if query_out is not None:
                        pe.matmul(z, wx[:, :], tokens(g), start=True, stop=False)
                    for h in range(HEADS):
                        mm = pe.matmul(z, CH[:, h, :], heads(g)[:, :, h, :],
                                       start=(h == 0 and query_out is None), stop=(h == HEADS - 1))
                    mm.then_inc(zt_ps, 1)
                for g in range(2):
                    pe.wait_ge(zt_in, g + 1)
                    for j in range(4):
                        mm = pe.transpose(PS[:, 2 + g, 128 * j:128 * j + 128],
                                          ZT[:, 8 * g + 2 * j:8 * g + 2 * j + 2, :].rearrange("p a q -> p (a q)"),
                                          ident[:, :])
                    mm.then_inc(z_ps, 1)

            @block.scalar
            def _(act):
                act.wait_ge(zeroed, 1)
                for g in range(2):
                    act.wait_ge(zt_ps, g + 1)
                    act.activation(ZT[:, 8 * g:8 * g + 8, 0:TOK],
                                   PS[:, g, 0:HALF_TOK].rearrange("p (b q) -> p b q", q=TOK), ACT.Identity,
                                   bias=cout[:, 0:1]).then_inc(zt_in, 1)

            @block.vector
            def _(v):
                chain = Chain(v, step)
                v.memset(ZT[:, :, :], 0.0).then_inc(zeroed, 1)
                v.wait_ge(z_ps, 2)
                zp = PS[:, 2:4, :].rearrange("p a (j m) -> p (a j) m", m=128)
                if norm:
                    chain(v.tensor_copy(Z[:, :, :], zp))
                    layer_norm(v, chain, XN, Z, ln, 1e-5)
                    v.wait_ge(gb_in, 32)
                    self.affine(v, chain, XN, gb)
                    chain(v.tensor_tensor(X[:, :, :], X[:, :, :], XN[:, :, :], ALU.add))
                else:
                    chain(v.tensor_tensor(X[:, :, :], zp, X[:, :, :], ALU.add))

    def store(self):
        nc = self.nc
        self.stage = "store"
        with ExitStack() as ctx:
            stored = self.sem(ctx, "stored")
            block = ctx.enter_context(nc.Block())

            @block.sync
            def _(sp):
                ov = self.out.rearrange("(t two) q d -> two q t d", two=2)
                for par in range(2):
                    sp.dma_start(ov[par], self.X[HALF * par:HALF * par + TOK, :, :]).then_inc(stored, 16)
                sp.wait_ge(stored, 32)


def xattn_ffn_layers(nc, t, out, stages="0123456789"):
    k = Kernel(nc, t, out)
    with ExitStack() as ctx:
        k.stage = "all"
        k.passed = k.sem(ctx, "passed")
        k.X, k.XN = k.sb(ctx, "X", [128, PAIRS, D]), k.sb(ctx, "XN", [128, PAIRS, D])
        k.ident, k.blockm, k.valid, k.pick, k.ones = (
            k.sb(ctx, n, [128, 128]) for n in ("ident", "blockm", "valid", "pick", "ones"))
        k.rowmask, k.kidx = k.sb(ctx, "rowmask", [128, 1]), k.sb(ctx, "kidx", [128, KEYS])
        k.e_idx = k.sb(ctx, "e_idx", [128, PAIRS, EXPERTS])
        k.PS = ctx.enter_context(nc.psum_tensor("PS", [128, 8, 512], F32))
        k.setup()
        if "0" in stages:
            k.local_attention("l0a", False)
        if "1" in stages:
            k.moe("l0f", False)
        if "2" in stages:
            k.local_attention("l1s", True)
            k.cross_attention()
        if "3" in stages:
            k.quantised_ffn()
        k.clear_used()
        if "4" in stages:
            k.head_attention("l2", 64, dict(
                wqT=t["WqT2"], wkT=t["WvT2"], wvT=t["WvT2"], wo=t["L2_xattn_Wfc"][0:HEADS * 64],
                query_out=t["L2_xattn_Wfc"][HEADS * 64:HEADS * 64 + D], wk=t["L2_xattn_Wv"],
                woT=t["WoT2"], bq=t["L2_xattn_bq"], bv=t["L2_xattn_bv"], bo=t["L2_xattn_bfc"], norm=(t["L2_xattn_gamma"], t["L2_xattn_beta"])),
                padded=False)
        if "5" in stages:
            k.unit_ffn()
        k.clear_used()
        if "6" in stages:
            k.head_attention("l3", 8, dict(
                wqT=t["WqT3"], wkT=t["WkT3"], wvT=t["WvT3"], wo=t["L3_xattn_W_O"],
                wk=t["L3_xattn_W_K"], woT=t["WoT3"], bq=t["L3_xattn_b_Q"], bv=t["L3_xattn_b_V"], bo=t["L3_xattn_b_O"]), padded=True)
        if "7" in stages:
            k.moe("l3f", True)
        k.store()


def arrange(inputs):
    a = {k: np.ascontiguousarray(v) for k, v in inputs.items() if k != "mask_BxS2_bk0"}
    a["mask"] = np.ascontiguousarray(inputs["mask_BxS2_bk0"])

    def turned(name, axes=(1, 0)):
        return np.ascontiguousarray(np.transpose(a[name], axes))

    a["ctxT"] = turned("ctx_1024", (0, 2, 1))
    a["WqT0"] = turned("L0_xattn_Wq")
    a["Wq1T"], a["Wk1T"] = turned("L1_xattn_Wq1"), turned("L1_xattn_Wk1")
    a["Wq2T"], a["Wk2T"] = turned("L1_xattn_Wq2"), turned("L1_xattn_Wk2")
    a["WqT2"], a["WvT2"] = turned("L2_xattn_Wq"), turned("L2_xattn_Wv")
    a["WqT3"], a["WkT3"], a["WvT3"] = (turned(f"L3_xattn_W_{x}") for x in "QKV")
    a["WoT2"] = np.ascontiguousarray(a["L2_xattn_Wfc"][0:HEADS * 64].T)
    a["WoT3"] = turned("L3_xattn_W_O")
    for name in ("W1", "b1", "W2"):
        a[f"L2_ffn_{name}_halves"] = np.ascontiguousarray(
            np.transpose(a[f"L2_ffn_{name}"].reshape(M2, INNER // 2, 2), (2, 0, 1)))
    for n, name in ((0, "L0_ffn_b1"), (3, "L3_ffn_b1")):
        a[f"b1T{n}"] = np.ascontiguousarray(
            np.transpose(a[name].reshape(EXPERTS, FCHUNKS, 128), (2, 0, 1)))
    return a


def kernel(**inputs):
    import concourse.bacc as _bacc
    from concourse.bass_utils import run_bass_kernel_spmd as _run

    nc = _bacc.Bacc("TRN2", target_bir_lowering=False, num_devices=1)
    arrays = {f"in_{k}": v for k, v in arrange(inputs).items()}
    t = {k[3:]: nc.dram_tensor(k, v.shape, mybir.dt.from_np(v.dtype), kind="ExternalInput").ap()
         for k, v in arrays.items()}
    out = nc.dram_tensor("out_x", (BATCH, TOK, D), F32, kind="ExternalOutput").ap()
    xattn_ffn_layers(nc, t, out)
    r = _run(nc, [arrays], core_ids=[0])
    return r.results[0]["out_x"]
```

```python
from contextlib import ExitStack

import numpy as np

import concourse.bass as bass
from concourse import mybir

F32 = mybir.dt.float32
F32R = mybir.dt.float32r
I32 = mybir.dt.int32
U8 = mybir.dt.uint8
ALU = mybir.AluOpType
ACT = mybir.ActivationFunctionType
X_AXIS = mybir.AxisListType.X
XY_AXES = mybir.AxisListType.XY

BATCH, TOK, D = 16, 56, 128
PAIRS = BATCH // 2
HALF = 64
KEYS = 1500
CHUNK = 125
CHUNKS = KEYS // CHUNK
BANKS = 3
BANK_KEYS = KEYS // BANKS
HEADS = 16
ROWS = HEADS * TOK
TILES = BATCH * ROWS // 128
BATCH_TILES = ROWS // 128
EXPERTS, FF = 8, 512
FCHUNKS = FF // 128
FFN1 = 384
GCHUNKS = FFN1 // 128
QBLOCK = 32
ROUND = 12582912.0
M2, INNER = 64, 16
NEG = -3.0e38
HALF_TOK = BATCH // 2 * TOK


class Chain:

    def __init__(self, eng, sem):
        self.eng, self.sem, self.n, self.base = eng, sem, 0, 0

    def __call__(self, ins):
        self.n += 1
        ins.then_inc(self.sem, 1)
        self.eng.wait_ge(self.sem, self.base + self.n)


def settle(eng, passed):
    eng.sem_inc(passed, 1)


def wait_for(eng, sem, count):
    if not (isinstance(count, int) and count == 0):
        eng.wait_ge(sem, count)


def expert_pairs(eng, pair):
    pair(0)
    with eng.Fori(1, EXPERTS // 2) as i:
        pair(i)


def run_steps(eng, total, lag, unroll, step, peeled=0):
    first = -(-lag // unroll) * unroll
    loops = (total - first) // unroll - peeled
    for n in range(first):
        step(n, n % unroll, n)
    if loops > 0:
        with eng.Fori(first // unroll, first // unroll + loops) as i:
            for u in range(unroll):
                step(i * unroll + u, u, None)
    for n in range(first + max(loops, 0) * unroll, total + lag):
        step(n, n % unroll, n)


def live(known, lag, total):
    return known is None or lag <= known < total + lag


class Stack:

    def __init__(self, nc, t, out):
        self.nc, self.t, self.out = nc, t, out
        self.used = []

    def sem(self, ctx, name):
        sem = ctx.enter_context(self.nc.semaphore(f"{self.stage}_{name}"))
        if self.stage != "all":
            self.used.append(sem.num)
        return sem

    def clear_used(self):
        runs = []
        for num in sorted(set(self.used)):
            if runs and runs[-1][-1] == num - 1:
                runs[-1].append(num)
            else:
                runs.append([num])
        self.used = []
        with self.nc.Block() as block:

            @block.gpsimd
            def _(g):
                for run in runs:
                    g.sem_clear(range(run[0], run[-1] + 1))

    def sb(self, ctx, name, shape, dt=F32):
        return ctx.enter_context(self.nc.sbuf_tensor(f"{self.stage}_{name}", shape, dt))




def rsqrt(v, chain, out, var, eps, w):
    ve, half, y2, tt = w[0], w[1], w[2], w[3]
    v.tensor_scalar(half, var, eps, -0.5, ALU.add, ALU.mult)
    chain(v.tensor_scalar(ve, var, eps, None, ALU.add))
    chain(v.tensor_scalar(tt.bitcast(I32), ve.bitcast(I32), 1, None, ALU.logical_shift_right))
    chain(v.tensor_scalar(out.bitcast(I32), tt.bitcast(I32), -1.0, float(0x5F3759DF), ALU.mult, ALU.add))
    for _ in range(3):
        chain(v.tensor_tensor(y2, out, out, ALU.mult))
        chain(v.tensor_tensor(tt, y2, half, ALU.mult))
        chain(v.scalar_tensor_tensor(out=out, in0=tt, scalar=1.5, in1=out, op0=ALU.add, op1=ALU.mult))


def layer_norm(v, chain, dst, src, w, eps, ready=None):
    stats, mv, rstd, work = w
    for t in range(PAIRS):
        last = v.bn_stats(stats[:, t, :], src[:, t, :])
    chain(last)
    for t in range(PAIRS):
        last = v.bn_aggr(mv[:, t, :], stats[:, t, :])
    chain(last)
    rsqrt(v, chain, rstd[:, :], mv[:, :, 1], eps, [work[:, k, :] for k in range(4)])
    for t in range(PAIRS):
        last = v.tensor_scalar(dst[:, t, :], src[:, t, :], mv[:, t, 0:1], rstd[:, t:t + 1],
                               ALU.subtract, ALU.mult)
        if ready is not None and t % (PAIRS // 2) == PAIRS // 2 - 1:
            last.then_inc(ready, 1)
    if ready is None:
        chain(last)
    else:
        v.wait_ge(ready, 2)


class Kernel(Stack):
    def norm_scratch(self, ctx):
        return (self.sb(ctx, "stats", [128, PAIRS, 6]), self.sb(ctx, "mv", [128, PAIRS, 2]),
                self.sb(ctx, "rstd", [128, PAIRS]), self.sb(ctx, "nwork", [128, 4, PAIRS]))

    def setup(self):
        nc, t = self.nc, self.t
        self.stage = "init"
        with ExitStack() as ctx:
            zeroed, marked, x_in, step = (self.sem(ctx, n) for n in ("zeroed", "marked", "x_in", "step"))
            X, ident, blockm, valid, pick, rowmask, kidx, e_idx, ones = (
                self.X, self.ident, self.blockm, self.valid, self.pick, self.rowmask, self.kidx,
                self.e_idx, self.ones)
            block = ctx.enter_context(nc.Block())

            @block.vector
            def _(v):
                chain = Chain(v, step)
                v.memset(ident[:, :], 0.0)
                v.memset(blockm[:, :], NEG)
                v.memset(valid[:, :], 0.0)
                v.memset(pick[:, :], 0.0)
                v.memset(ones[:, :], 1.0)
                v.memset(rowmask[:, :], 1.0)
                chain(v.memset(X[:, :, :], 0.0))
                v.memset(blockm[0:HALF, 0:HALF], 0.0)
                v.memset(blockm[HALF:128, HALF:128], 0.0)
                v.memset(valid[0:HALF, 0:TOK], 1.0)
                v.memset(valid[HALF:128, HALF:HALF + TOK], 1.0)
                v.memset(pick[0:1, 0:HALF], 1.0)
                v.memset(pick[HALF:HALF + 1, HALF:128], 1.0).then_inc(zeroed, 1)

            @block.gpsimd
            def _(g):
                chain = Chain(g, marked)
                g.iota(kidx[:, :], [[1, HALF]], base=0, channel_multiplier=0,
                       allow_small_or_imprecise_dtypes=True)
                chain(g.iota(e_idx[:, :, :], [[0, PAIRS], [1, EXPERTS]], base=-EXPERTS, channel_multiplier=0,
                             allow_small_or_imprecise_dtypes=True))
                g.wait_ge(zeroed, 1)
                chain(g.affine_select(out=ident[:, :], in_=ident[:, :], compare_op=ALU.not_equal, fill=1.0,
                                      base=0, pattern=[[-1, 128]], channel_multiplier=1))
                chain(g.affine_select(out=blockm[:, :], in_=blockm[:, :], compare_op=ALU.is_ge, fill=NEG,
                                      base=0, pattern=[[-1, 128]], channel_multiplier=1))
                for p in (0, HALF):
                    chain(g.affine_select(out=rowmask[p:p + HALF, :], in_=rowmask[p:p + HALF, :],
                                          compare_op=ALU.is_ge, fill=0.0, base=TOK - 1, pattern=[[0, 1]],
                                          channel_multiplier=-1))

            @block.sync
            def _(sp):
                xv = t["x"].rearrange("(t two) q d -> two q t d", two=2)
                sp.wait_ge(zeroed, 1)
                for par in range(2):
                    sp.dma_start(X[HALF * par:HALF * par + TOK, :, :], xv[par]).then_inc(x_in, 16)
                sp.wait_ge(x_in, 32)

    def local_attention(self, stage, self_keys, load_ahead=None):
        nc, t = self.nc, self.t
        self.stage = stage
        X, XN, ident, blockm, PS = self.X, self.XN, self.ident, self.blockm, self.PS
        scale = 1.0 / np.sqrt(8.0) if self_keys else 1.0 / np.sqrt(float(D))
        with ExitStack() as ctx:
            XT = self.sb(ctx, "XT", [128, PAIRS, 128])
            QT = self.sb(ctx, "QT", [128, PAIRS, 128])
            KT = XT if self_keys else self.sb(ctx, "KT", [128, PAIRS, 2, HALF])
            C = XN if self_keys else self.sb(ctx, "C", [128, PAIRS, D])
            S = self.sb(ctx, "S", [128, PAIRS, 128])
            PT = self.sb(ctx, "PT", [128, PAIRS, 128])
            OT = self.sb(ctx, "OT", [128, PAIRS, 128])
            w_q = self.sb(ctx, "w_q", [128, 128])
            w_k = self.sb(ctx, "w_k", [128, 128])
            w_v = self.sb(ctx, "w_v", [128, 128])
            fold = self.sb(ctx, "fold", [128, 128])
            red = self.sb(ctx, "red", [128, 4, PAIRS])
            ln = self.norm_scratch(ctx)
            gb = self.sb(ctx, "gb", [128, 2, D])
            (w_in, c_in, c_zero, fold_ps, fold_in, xn_ready, xt_ps, xt_in, qt_ps, qt_in, e_ps, s_ready,
             p_ready, p_done, pt_ps, pt_in, o_ps, o_in, z_ps, step, cnt_in, len_ps) = (
                self.sem(ctx, n) for n in (
                    "w_in", "c_in", "c_zero", "fold_ps", "fold_in", "xn_ready", "xt_ps", "xt_in",
                    "qt_ps", "qt_in", "e_ps", "s_ready", "p_ready", "p_done", "pt_ps", "pt_in", "o_ps",
                    "o_in", "z_ps", "step", "cnt_in", "len_ps"))
            block = ctx.enter_context(nc.Block())
            flat = lambda a: a[:, :, :].rearrange("p t m -> p (t m)")

            @block.sync
            def _(sp):
                if self_keys:
                    sp.dma_start(w_q[:, :], t["Wq1T"]).then_inc(w_in, 16)
                    sp.dma_start(w_k[:, :], t["Wk1T"]).then_inc(w_in, 16)
                    sp.dma_start(w_v[:, :], t["L1_xattn_Wv1"]).then_inc(w_in, 16)
                    sp.dma_start(gb[:, 0, :], t["L1_xattn_ln1_g"].partition_broadcast(128)).then_inc(w_in, 16)
                    sp.dma_start(gb[:, 1, :], t["L1_xattn_ln1_b"].partition_broadcast(128)).then_inc(w_in, 16)
                    load_ahead(sp)
                else:
                    sp.dma_start(w_q[:, :], t["L0_xattn_Wq"]).then_inc(w_in, 16)
                    sp.dma_start(w_v[:, :], t["WqT0"]).then_inc(w_in, 16)
                    sp.wait_ge(c_zero, 1)
                    cv = t["ctx_1024"].rearrange("(t two) k d -> two k t d", two=2)
                    tv = t["ctxT"].rearrange("(t two) d k -> two d t k", two=2)
                    for par in range(2):
                        sp.dma_start(C[HALF * par:HALF * par + TOK, :, :], cv[par, 0:TOK]).then_inc(c_in, 16)
                        sp.dma_start(KT[:, :, par, 0:TOK], tv[par, :, :, 0:TOK]).then_inc(c_in, 16)

            @block.tensor
            def _(pe):
                pe.wait_ge(w_in, 80 if self_keys else 32)
                pe.matmul(PS[:, 7, 0:128], w_q[:, :], w_k[:, :] if self_keys else w_q[:, :],
                          start=True, stop=True).then_inc(fold_ps, 1)
                for k in range(2):
                    pe.wait_ge(xn_ready, k + 1)
                    for j in range(4):
                        mm = pe.transpose(PS[:, k, 128 * j:128 * j + 128], XN[:, 4 * k + j, :], ident[:, :])
                    mm.then_inc(xt_ps, 1)
                pe.wait_ge(fold_in, 1)
                for k in range(2):
                    pe.wait_ge(xt_in, k + 1)
                    pe.matmul(PS[:, 2 + k, :], fold[:, :], flat(XT)[:, 512 * k:512 * k + 512],
                              start=True, stop=True).then_inc(qt_ps, 1)
                if not self_keys:
                    pe.wait_ge(c_in, 64)
                for k in range(2):
                    pe.wait_ge(qt_in, k + 1)
                    for j in range(4):
                        keys = (XT[:, 4 * k + j, :] if self_keys
                                else KT[:, 4 * k + j, :, :].rearrange("p a k -> p (a k)"))
                        mm = pe.matmul(PS[:, 4 + k, 128 * j:128 * j + 128], QT[:, 4 * k + j, :], keys,
                                       start=True, stop=True)
                    mm.then_inc(e_ps, 1)
                if self_keys:
                    pe.wait_ge(cnt_in, 1)
                    pe.matmul(PS[:, 6, 0:PAIRS], self.pick[:, :], red[:, 3, :], start=True,
                              stop=True).then_inc(len_ps, 1)
                pe.wait_ge(p_done, 1)
                for k in range(2):
                    for j in range(4):
                        mm = pe.transpose(PS[:, k, 128 * j:128 * j + 128], S[:, 4 * k + j, :], ident[:, :])
                    mm.then_inc(pt_ps, 1)
                for k in range(2):
                    pe.wait_ge(pt_in, k + 1)
                    for j in range(4):
                        mm = pe.matmul(PS[:, 2 + k, 128 * j:128 * j + 128], C[:, 4 * k + j, :],
                                       PT[:, 4 * k + j, :], start=True, stop=True)
                    mm.then_inc(o_ps, 1)
                for k in range(2):
                    pe.wait_ge(o_in, k + 1)
                    for j in range(4):
                        mm = pe.matmul(PS[:, 4 + k, 128 * j:128 * j + 128], OT[:, 4 * k + j, :], w_v[:, :],
                                       start=True, stop=True)
                    mm.then_inc(z_ps, 1)

            @block.scalar
            def _(act):
                act.wait_ge(fold_ps, 1)
                act.copy(fold[:, :], PS[:, 7, 0:128]).then_inc(fold_in, 1)
                for k in range(2):
                    act.wait_ge(xt_ps, k + 1)
                    act.copy(flat(XT)[:, 512 * k:512 * k + 512], PS[:, k, :]).then_inc(xt_in, 1)
                for k in range(2):
                    act.wait_ge(qt_ps, k + 1)
                    act.mul(flat(QT)[:, 512 * k:512 * k + 512], PS[:, 2 + k, :], 1.0).then_inc(qt_in, 1)
                act.wait_ge(s_ready, 1)
                act.activation(S[:, :, :], S[:, :, :], ACT.Exp, scale=scale).then_inc(p_ready, 1)
                for k in range(2):
                    act.wait_ge(pt_ps, k + 1)
                    act.copy(flat(PT)[:, 512 * k:512 * k + 512], PS[:, k, :]).then_inc(pt_in, 1)
                for k in range(2):
                    act.wait_ge(o_ps, k + 1)
                    act.copy(flat(OT)[:, 512 * k:512 * k + 512], PS[:, 2 + k, :]).then_inc(o_in, 1)

            @block.vector
            def _(v):
                chain = Chain(v, step)
                if not self_keys:
                    chain(v.memset(C[:, :, :], 0.0))
                    v.memset(KT[:, :, :, :], 0.0).then_inc(c_zero, 1)
                layer_norm(v, chain, XN, X, ln, 1e-5, xn_ready)
                E = PS[:, 4:6, :].rearrange("p a (j m) -> p (a j) m", m=128)
                v.wait_ge(e_ps, 2)
                if self_keys:
                    chain(v.tensor_scalar(S[:, :, :], E, 0.0, None, ALU.not_equal))
                    chain(v.tensor_tensor(S[:, :, :], S[:, :, :],
                                          self.valid[:, :].unsqueeze(1).to_broadcast([128, PAIRS, 128]), ALU.mult))
                    v.tensor_reduce(red[:, 3, :], S[:, :, :], X_AXIS, ALU.add).then_inc(cnt_in, 1)
                    v.wait_ge(len_ps, 1)
                    chain(v.tensor_copy(red[:, 3, :], PS[:, 6, 0:PAIRS]))
                    for p in (0, HALF):
                        chain(v.tensor_tensor(
                            S[p:p + HALF, :, p:p + HALF],
                            self.kidx[p:p + HALF, 0:HALF].unsqueeze(1).to_broadcast([HALF, PAIRS, HALF]),
                            red[p:p + HALF, 3, :].unsqueeze(2).to_broadcast([HALF, PAIRS, HALF]), ALU.is_ge))
                        chain(v.memset(S[p:p + HALF, :, HALF - p:128 - p], 0.0))
                    chain(v.tensor_scalar(S[:, :, :], S[:, :, :], NEG, None, ALU.mult))
                    chain(v.tensor_tensor(S[:, :, :], S[:, :, :],
                                          blockm[:, :].unsqueeze(1).to_broadcast([128, PAIRS, 128]), ALU.min))
                    chain(v.tensor_tensor(S[:, :, :], E, S[:, :, :], ALU.add))
                else:
                    chain(v.tensor_tensor(S[:, :, :], E,
                                          blockm[:, :].unsqueeze(1).to_broadcast([128, PAIRS, 128]), ALU.add))
                chain(v.tensor_reduce(red[:, 0, :], S[:, :, :], X_AXIS, ALU.max))
                v.tensor_tensor(S[:, :, :], S[:, :, :], red[:, 0, :].unsqueeze(2).to_broadcast([128, PAIRS, 128]),
                                ALU.subtract).then_inc(s_ready, 1)
                v.wait_ge(p_ready, 1)
                chain(v.tensor_reduce(red[:, 1, :], S[:, :, :], X_AXIS, ALU.add))
                chain(v.reciprocal(red[:, 2, :], red[:, 1, :]))
                v.tensor_tensor(S[:, :, :], S[:, :, :], red[:, 2, :].unsqueeze(2).to_broadcast([128, PAIRS, 128]),
                                ALU.mult).then_inc(p_done, 1)
                v.wait_ge(z_ps, 2)
                Z = PS[:, 4:6, :].rearrange("p a (j m) -> p (a j) m", m=128)
                if self_keys:
                    v.wait_ge(w_in, 80)
                    chain(v.tensor_tensor(S[:, :, :], Z, XN[:, :, :], ALU.add))
                    layer_norm(v, chain, XN, S, ln, 1e-5)
                    self.affine(v, chain, XN, gb)
                else:
                    chain(v.tensor_tensor(X[:, :, :], Z, X[:, :, :], ALU.add))

    def affine(self, v, chain, dst, gb):
        for k, op in ((0, ALU.mult), (1, ALU.add)):
            chain(v.tensor_tensor(dst[:, :, :], dst[:, :, :],
                                  gb[:, k, :].unsqueeze(1).to_broadcast([128, PAIRS, D]), op))

    def moe(self, stage, final):
        nc, t = self.nc, self.t
        self.stage = stage
        X, XN, ident, PS = self.X, self.XN, self.ident, self.PS
        W1, W2 = (t["L3_ffn_w1"], t["L3_ffn_w2"]) if final else (t["L0_ffn_W1"], t["L0_ffn_W2"])
        B1 = t["b1T3"] if final else t["b1T0"]
        with ExitStack() as ctx:
            XT = self.sb(ctx, "XT", [128, PAIRS, 128])
            HT = self.sb(ctx, "HT", [128, FCHUNKS, PAIRS, 2, HALF])
            w1 = [self.sb(ctx, f"w1_{s}", [128, FF]) for s in range(2)]
            w1h, w1l = ([self.sb(ctx, f"{n}_{s}", [128, FF], F32R) for s in range(2)] for n in ("w1h", "w1l"))
            XTh, XTl = (self.sb(ctx, n, [128, PAIRS, 128], F32R) for n in ("XTh", "XTl"))
            w2 = [self.sb(ctx, f"w2_{s}", [128, FCHUNKS, D]) for s in range(2)]
            b1 = self.sb(ctx, "b1", [128, EXPERTS, FCHUNKS])
            wg = self.sb(ctx, "wg", [128, EXPERTS])
            if not final:
                bg = self.sb(ctx, "bg", [128, EXPERTS])
            add = self.sb(ctx, "add", [EXPERTS, D])
            G = self.sb(ctx, "G", [128, PAIRS, EXPERTS])
            GT = self.sb(ctx, "GT", [EXPERTS, PAIRS, 128])
            lg = self.sb(ctx, "lg", [128, 6, PAIRS, EXPERTS])
            red = self.sb(ctx, "red", [128, 6, PAIRS])
            ln = self.norm_scratch(ctx)
            if final:
                b2 = self.sb(ctx, "b2", [128, EXPERTS, D])
                gamma = self.sb(ctx, "gamma", [128, EXPERTS, D])
                XB = [self.sb(ctx, f"XB{s}", [128, PAIRS, D]) for s in range(2)]
                R = self.sb(ctx, "R", [128, PAIRS, D])
                gscale = self.sb(ctx, "gscale", [128, PAIRS])
            (w_in, g_in, h_zero, xn_ready, xt_ps, xt_in, lg_ps, l_ready, p_ready, g_ready, gt_ps, gt_in,
             add_ps, step) = (self.sem(ctx, n) for n in (
                 "w_in", "g_in", "h_zero", "xn_ready", "xt_ps", "xt_in", "lg_ps", "l_ready", "p_ready",
                 "g_ready", "gt_ps", "gt_in", "add_ps", "step"))
            w_slot = [self.sem(ctx, f"w_slot{s}") for s in range(2)]
            w_used = [self.sem(ctx, f"w_used{s}") for s in range(2)]
            w1_high, w1_split = ([self.sem(ctx, f"{n}{s}") for s in range(2)] for n in ("w1_high", "w1_split"))
            xth_in, xtl_in = self.sem(ctx, "xth_in"), self.sem(ctx, "xtl_in")
            h_ps, h_in = self.sem(ctx, "h_ps"), [self.sem(ctx, f"h_in{k}") for k in range(4)]
            y_ps = [self.sem(ctx, f"y_ps{s}") for s in range(2)]
            y_used = [self.sem(ctx, f"y_used{s}") for s in range(2)]
            xb_in = [self.sem(ctx, f"xb_in{s}") for s in range(2)]
            block = ctx.enter_context(nc.Block())
            flat = lambda a: a[:, :, :].rearrange("p t m -> p (t m)")
            SETUP_DMAS = 5 if final else 4

            @block.sync
            def _(sp):
                sp.dma_start(b1[:, :, :], B1).then_inc(w_in, 16)
                if final:
                    sp.dma_start(wg[:, :], t["L3_ffn_router_w"]).then_inc(w_in, 16)
                    sp.dma_start(add[:, :], t["L3_ffn_beta"]).then_inc(w_in, 16)
                    sp.dma_start(b2[:, :, :], t["L3_ffn_b2"].partition_broadcast(128)).then_inc(w_in, 16)
                    sp.dma_start(gamma[:, :, :], t["L3_ffn_gamma"].partition_broadcast(128)).then_inc(w_in, 16)
                else:
                    sp.dma_start(wg[:, :], t["L0_ffn_Wg"]).then_inc(w_in, 16)
                    sp.dma_start(add[:, :], t["L0_ffn_b2"]).then_inc(w_in, 16)
                    sp.dma_start(bg[:, :], t["L0_ffn_bg"].partition_broadcast(128)).then_inc(w_in, 16)

                def load(i):
                    for s in range(2):
                        wait_for(sp, w_used[s], i)
                        sp.dma_start(w1[s][:, :], W1[bass.ds(2 * i + s, 1)].rearrange("a d f -> d (a f)")
                                     ).then_inc(w_slot[s], 16)
                        sp.dma_start(w2[s][:, :, :], W2[bass.ds(2 * i + s, 1)].rearrange(
                            "a (c f) d -> f (a c) d", f=128)).then_inc(w_slot[s], 16)

                expert_pairs(sp, load)

            @block.tensor
            def _(pe):
                pe.wait_ge(w_in, 16 * SETUP_DMAS)
                for k in range(2):
                    pe.wait_ge(xn_ready, k + 1)
                    for j in range(4):
                        mm = pe.transpose(PS[:, k, 128 * j:128 * j + 128], XN[:, 4 * k + j, :], ident[:, :])
                    mm.then_inc(xt_ps, 1)
                pe.wait_ge(xt_in, 2)
                for p in range(PAIRS):
                    mm = pe.matmul(PS[:, 6, 8 * p:8 * p + 8], XT[:, p, :], wg[:, :], start=True, stop=True)
                mm.then_inc(lg_ps, 1)

                def gates_turned():
                    pe.wait_ge(g_ready, 1)
                    for k in range(2):
                        for j in range(4):
                            mm = pe.transpose(PS[0:EXPERTS, 6 + k, 128 * j:128 * j + 128], G[:, 4 * k + j, :],
                                              ident[:, :])
                        mm.then_inc(gt_ps, 1)

                def added():
                    pe.wait_ge(gt_in, 2)
                    for k in range(2):
                        for j in range(4):
                            mm = pe.matmul(PS[:, 6 + k, 128 * j:128 * j + 128], GT[:, 4 * k + j, :], add[:, :],
                                           start=True, stop=True)
                        mm.then_inc(add_ps, 1)

                def experts(i):
                    for s in range(2):
                        first = isinstance(i, int) and s == 0
                        pe.wait_ge(w_slot[s], 32 * i + 32)
                        pe.wait_ge(w1_split[s], i + 1)
                        if first:
                            pe.wait_ge(xtl_in, 2)
                        for half in range(2):
                            for c in range(FCHUNKS):
                                wait_for(pe, h_in[c], 4 * i + (2 * s + half))
                                high, low = (x[:, 4 * half:4 * half + 4, :].rearrange(
                                    "p t (a q) -> p (t a) q", a=2)[:, :, 0:TOK] for x in (XTh, XTl))
                                cols, h = slice(128 * c, 128 * c + 128), PS[:, c, 0:HALF_TOK]
                                pe.matmul(h, w1h[s][:, cols], high, start=True, stop=False)
                                pe.matmul(h, w1h[s][:, cols], low, start=False, stop=False)
                                pe.matmul(h, w1l[s][:, cols], high, start=False, stop=True).then_inc(h_ps, 1)
                        if first:
                            gates_turned()
                        if isinstance(i, int) and s == 1:
                            pe.wait_ge(g_in, 1)
                        wait_for(pe, y_used[s], i)
                        for half in range(2):
                            for c in range(FCHUNKS):
                                pe.wait_ge(h_in[c], 4 * i + 2 * s + half + 1)
                            for j in range(4):
                                p = 4 * half + j
                                for c in range(FCHUNKS):
                                    mm = pe.matmul(PS[:, 4 + 2 * s + half, 128 * j:128 * j + 128],
                                                   HT[:, c, p, :, :].rearrange("p a q -> p (a q)"),
                                                   w2[s][:, c, :], start=(c == 0), stop=(c == FCHUNKS - 1))
                            mm.then_inc(y_ps[s], 1)
                        pe.wait_ge(y_ps[s], 2 * i + 2)
                        pe.nop().then_inc(w_used[s], 1)
                        if first:
                            added()

                expert_pairs(pe, experts)

            @block.scalar
            def _(act):
                for k in range(2):
                    act.wait_ge(xt_ps, k + 1)
                    act.copy(flat(XT)[:, 512 * k:512 * k + 512], PS[:, k, :]).then_inc(xt_in, 1)
                for k in range(2):
                    act.copy(flat(XTh)[:, 512 * k:512 * k + 512], PS[:, k, :]).then_inc(xth_in, 1)
                act.wait_ge(l_ready, 1)
                act.activation(lg[:, 4, :, :], lg[:, 5, :, :], ACT.Exp).then_inc(p_ready, 1)
                act.wait_ge(h_zero, 1)
                act.wait_ge(w_in, 16 * SETUP_DMAS)

                def experts(i):
                    for s in range(2):
                        for half in range(2):
                            if half == 0:
                                wait_for(act, w_used[1 - s], i + s)
                            for c in range(FCHUNKS):
                                act.wait_ge(h_ps, 16 * i + 8 * s + 4 * half + c + 1)
                                settle(act, self.passed)
                                act.activation(
                                    HT[:, c, 4 * half:4 * half + 4, :, 0:TOK].rearrange("p t a q -> p (t a) q"),
                                    PS[:, c, 0:HALF_TOK].rearrange("p (t q) -> p t q", q=TOK), ACT.Gelu,
                                    bias=b1[:, bass.ds(2 * i + s, 1), c]).then_inc(h_in[c], 1)
                        if isinstance(i, int) and s == 0:
                            for k in range(2):
                                act.wait_ge(gt_ps, k + 1)
                                act.copy(GT[:, 4 * k:4 * k + 4, :].rearrange("p t m -> p (t m)"),
                                         PS[0:EXPERTS, 6 + k, :]).then_inc(gt_in, 1)

                expert_pairs(act, experts)

            @block.gpsimd
            def _(g):
                g.memset(HT[:, :, :, :, TOK:HALF], 0.0).then_inc(h_zero, 1)

                def split_w1(i, s):
                    g.wait_ge(w_slot[s], 32 * i + 32)
                    wait_for(g, w_used[s], i)
                    settle(g, self.passed)
                    g.tensor_copy(w1h[s][:, :], w1[s][:, :]).then_inc(w1_high[s], 1)
                    g.wait_ge(w1_high[s], i + 1)
                    g.tensor_tensor(w1l[s][:, :], w1[s][:, :], w1h[s][:, :], ALU.subtract
                                    ).then_inc(w1_split[s], 1)

                if final:
                    def pair(i):
                        for s in range(2):
                            split_w1(i, s)
                            if isinstance(i, int) and s == 0:
                                g.wait_ge(w_in, 16 * SETUP_DMAS)
                                g.wait_ge(xn_ready, 2)
                            wait_for(g, y_used[s], i)
                            g.tensor_tensor(XB[s][:, :, :], XN[:, :, :],
                                            b2[:, bass.ds(2 * i + s, 1), :].to_broadcast([128, PAIRS, D]),
                                            ALU.add).then_inc(xb_in[s], 1)

                    expert_pairs(g, pair)
                else:
                    def pair(i):
                        for s in range(2):
                            split_w1(i, s)

                    expert_pairs(g, pair)

            @block.vector
            def _(v):
                chain = Chain(v, step)
                layer_norm(v, chain, XN, X, ln, 1e-5, xn_ready)
                for k in range(2):
                    v.wait_ge(xth_in, k + 1)
                    v.tensor_tensor(flat(XTl)[:, 512 * k:512 * k + 512], PS[:, k, :],
                                    flat(XTh)[:, 512 * k:512 * k + 512], ALU.subtract).then_inc(xtl_in, 1)
                v.wait_ge(lg_ps, 1)
                if not final:
                    v.wait_ge(w_in, 16 * SETUP_DMAS)
                self.gates(v, chain, PS[:, 6, 0:64].rearrange("p (t e) -> p t e", e=EXPERTS), lg, red, G,
                           l_ready, p_ready, final, None if final else bg)
                v.sem_inc(g_ready, 1)
                per_expert = 19 if final else 1
                done = chain.n
                extra = 1

                def experts(i):
                    for s in range(2):
                        first = isinstance(i, int) and s == 0
                        chain.base = done + 2 * per_expert * i + per_expert * s + extra
                        chain.n = 0
                        if first:
                            chain.base -= extra
                            v.wait_ge(add_ps, 2)
                            chain(v.tensor_tensor(
                                X[:, :, :], PS[:, 6:8, :].rearrange("p a (j m) -> p (a j) m", m=128),
                                X[:, :, :], ALU.add))
                            v.sem_inc(g_in, 1)
                            chain.base, chain.n = chain.base + extra, 0
                        Y = PS[:, 4 + 2 * s:6 + 2 * s, :].rearrange("p a (j m) -> p (a j) m", m=128)
                        v.wait_ge(y_ps[s], 2 * i + 2)
                        if final:
                            v.wait_ge(xb_in[s], i + 1)
                            stats, mv, rstd, work = ln
                            chain(v.tensor_tensor(R[:, :, :], Y, XB[s][:, :, :], ALU.add))
                            v.sem_inc(y_used[s], 1)
                            for p in range(PAIRS):
                                last = v.bn_stats(stats[:, p, :], R[:, p, :])
                            chain(last)
                            settle(v, self.passed)
                            for p in range(PAIRS):
                                last = v.bn_aggr(mv[:, p, :], stats[:, p, :])
                            chain(last)
                            rsqrt(v, chain, rstd[:, :], mv[:, :, 1], 1e-6, [work[:, k, :] for k in range(4)])
                            chain(v.tensor_tensor(gscale[:, :], rstd[:, :],
                                                  G[:, :, bass.ds(2 * i + s, 1)].rearrange("p t a -> p (t a)"),
                                                  ALU.mult))
                            for p in range(PAIRS):
                                last = v.tensor_scalar(R[:, p, :], R[:, p, :], mv[:, p, 0:1],
                                                       gscale[:, p:p + 1], ALU.subtract, ALU.mult)
                            chain(last)
                            chain(v.tensor_tensor(
                                R[:, :, :], R[:, :, :],
                                gamma[:, bass.ds(2 * i + s, 1), :].to_broadcast([128, PAIRS, D]), ALU.mult))
                            chain(v.tensor_tensor(X[:, :, :], X[:, :, :], R[:, :, :], ALU.add))
                        else:
                            for p in range(PAIRS):
                                last = v.scalar_tensor_tensor(
                                    out=X[:, p, :], in0=Y[:, p, :], scalar=G[:, p, bass.ds(2 * i + s, 1)],
                                    in1=X[:, p, :], op0=ALU.mult, op1=ALU.add)
                            chain(last)
                            v.sem_inc(y_used[s], 1)
                        assert chain.n == per_expert, chain.n

                expert_pairs(v, experts)

    def gates(self, v, chain, logits, lg, red, G, l_ready, p_ready, final, bias):
        shape = [128, PAIRS, EXPERTS]
        wide = lambda r: r.unsqueeze(2).to_broadcast(shape)
        L, cand, best, L2, P, less = (lg[:, k, :, :] for k in range(6))
        if bias is None:
            chain(v.tensor_copy(L, logits))
        else:
            chain(v.tensor_tensor(L, logits, bias[:, :].unsqueeze(1).to_broadcast(shape), ALU.add))
        chain(v.tensor_reduce(red[:, 0, :], L, X_AXIS, ALU.max))
        v.tensor_tensor(less, L, wide(red[:, 0, :]), ALU.subtract).then_inc(l_ready, 1)
        for k, (src, hit) in enumerate(((L, best), (L2, cand))):
            if k:
                chain(v.tensor_reduce(red[:, 0, :], src, X_AXIS, ALU.max))
            chain(v.tensor_tensor(cand, src, wide(red[:, 0, :]), ALU.is_equal))
            chain(v.tensor_tensor(cand, cand, self.e_idx[:, :, :], ALU.mult))
            chain(v.tensor_reduce(red[:, 1 + k, :], cand, X_AXIS, ALU.min))
            chain(v.tensor_tensor(hit, self.e_idx[:, :, :], wide(red[:, 1 + k, :]), ALU.is_equal))
            if not k:
                chain(v.scalar_tensor_tensor(out=L2.rearrange("p t e -> p (t e)"),
                                             in0=hit.rearrange("p t e -> p (t e)"), scalar=NEG,
                                             in1=L.rearrange("p t e -> p (t e)"), op0=ALU.mult, op1=ALU.add))
        chain(v.tensor_tensor(best, best, cand, ALU.add))
        v.wait_ge(p_ready, 1)
        chain(v.tensor_tensor(G[:, :, :], P, best, ALU.mult))
        chain(v.tensor_reduce(red[:, 3, :], G[:, :, :] if final else P, X_AXIS, ALU.add))
        chain(v.reciprocal(red[:, 4, :], red[:, 3, :]))
        chain(v.tensor_tensor(G[:, :, :], G[:, :, :], wide(red[:, 4, :]), ALU.mult))

    def layer_one(self):
        t = self.t
        self.stage = "l1"
        with ExitStack() as whole:
            WQ = self.sb(whole, "WQ", [128, 3 * FFN1])
            ctx = whole.enter_context(ExitStack())
            cT = [self.sb(ctx, f"cT{s}", [128, 2, KEYS]) for s in range(2)]
            c = [self.sb(ctx, f"c{s}", [CHUNK, 2 * CHUNKS, D]) for s in range(2)]
            w = self.sb(ctx, "w", [128, 5, 128])
            col = self.sb(ctx, "col", [128, 1])
            row = self.sb(ctx, "row", [1, D])
            gb = self.sb(ctx, "gb", [128, 2, 2, D])
            W = self.sb(ctx, "W", [128, 3 * FFN1])
            cT_in = [self.sem(ctx, f"cT_in{s}") for s in range(2)]
            c_in = [self.sem(ctx, f"c_in{s}") for s in range(2)]
            w_in, ffn_in = self.sem(ctx, "w_in"), self.sem(ctx, "ffn_in")

            def load_features(sp, n, u):
                sp.dma_start(cT[u][:, :, :], t["ctxT"][bass.ds(2 * n, 2)].rearrange("a d k -> d a k")
                             ).then_inc(cT_in[u], 16)

            def load_keys(sp, n, u):
                sp.dma_start(c[u][:, :, :], t["ctx_1024"][bass.ds(2 * n, 2)].rearrange(
                    "a (c k) d -> k (a c) d", k=CHUNK)).then_inc(c_in[u], 16)

            def load_ahead(sp):
                for k, src in enumerate((t["Wq2T"], t["Wk2T"], t["L1_xattn_Wv2"], t["L1_xattn_fc1_w"],
                                         t["L1_xattn_fc2_w"])):
                    sp.dma_start(w[:, k, :], src).then_inc(w_in, 16)
                sp.dma_start(col[:, :], t["L1_xattn_fc1_b"].unsqueeze(1)).then_inc(w_in, 16)
                sp.dma_start(row[:, :], t["L1_xattn_fc2_b"].unsqueeze(0)).then_inc(w_in, 16)
                for k, src in enumerate(("ln2_g", "ln2_b", "ln3_g", "ln3_b")):
                    sp.dma_start(gb[:, k // 2, k % 2, :], t["L1_xattn_" + src].partition_broadcast(128)
                                 ).then_inc(w_in, 16)
                for n in range(2):
                    load_features(sp, n, n)
                    load_keys(sp, n, n)
                for k, name in enumerate(("up", "gate")):
                    sp.dma_start(W[:, FFN1 * k:FFN1 * k + FFN1].rearrange("p (c i) -> p c i", i=128),
                                 t[f"L1_ffn_w_{name}"].rearrange("(c p) i -> p c i", p=128)
                                 ).then_inc(ffn_in, 16)
                sp.dma_start(W[:, 2 * FFN1:3 * FFN1], t["L1_ffn_w_down"]).then_inc(ffn_in, 16)

            self.local_attention("l1s", True, load_ahead)
            self.cross_attention(w, col, row, gb, cT, c, w_in, cT_in, c_in, load_features, load_keys,
                                 W, WQ, ffn_in)
            ctx.close()
            self.quantised_ffn(WQ)

    def cross_attention(self, w, col, row, gb, cT, c, w_in, cT_in, c_in, load_features, load_keys,
                        W, WQ, ffn_in):
        nc, t = self.nc, self.t
        self.stage = "l1c"
        X, XN, ident, PS = self.X, self.XN, self.ident, self.PS
        scale = 1.0 / float(np.sqrt(8.0))
        with ExitStack() as ctx:
            XT = self.sb(ctx, "XT", [128, PAIRS, 128])
            QT = self.sb(ctx, "QT", [128, PAIRS, 128])
            ON = self.sb(ctx, "ON", [128, PAIRS, D])
            fold = self.sb(ctx, "fold", [128, 128])
            q = [self.sb(ctx, f"q{s}", [128, 128]) for s in range(2)]
            P = [self.sb(ctx, f"P{s}", [128, KEYS]) for s in range(2)]
            PT = [self.sb(ctx, f"PT{s}", [CHUNK, CHUNKS * 128]) for s in range(2)]
            wmax = self.sb(ctx, "wmax", [128, 3, 3 * FFN1 // QBLOCK])
            pad, kidx = self.sb(ctx, "pad", [128, KEYS]), self.sb(ctx, "kidx", [128, KEYS])
            small = self.sb(ctx, "small", [128, 6, 2])
            ln = self.norm_scratch(ctx)
            COUNT, LENGTH, TOP, BIAS, SUM, INV = range(6)
            (fold_ps, fold_in, xt_ps, xt_in, qt_ps, qt_in, q_in, e_ps, cnt_in, len_ps, len_in,
             pad_in, top_in, p_in, pt_ps, pt_in, o_ps, o_in, step, ot_ps, ot_in, z_ps,
             n2_ready, h_ps, h_in, y_ps) = (self.sem(ctx, n) for n in (
                 "fold_ps", "fold_in", "xt_ps", "xt_in", "qt_ps", "qt_in", "q_in", "e_ps", "cnt_in",
                 "len_ps", "len_in", "pad_in", "top_in", "p_in", "pt_ps", "pt_in", "o_ps",
                 "o_in", "step", "ot_ps", "ot_in", "z_ps", "n2_ready", "h_ps", "h_in", "y_ps"))
            inv_in, kidx_in = self.sem(ctx, "inv_in"), self.sem(ctx, "kidx_in")
            block = ctx.enter_context(nc.Block())
            flat = lambda a: a[:, :, :].rearrange("p t m -> p (t m)")

            @block.sync
            def _(sp):

                def load(n, u, known):
                    if known is None or known >= 2:
                        sp.wait_ge(e_ps, n - 1)
                        load_features(sp, n, u)
                        sp.wait_ge(o_ps, n - 1)
                        load_keys(sp, n, u)

                run_steps(sp, PAIRS, 2, 2, lambda n, u, known: load(n, u, known) if live(known, 0, PAIRS) else None)

            @block.gpsimd
            def _(g):
                g.iota(kidx[:, :], [[1, KEYS]], base=0, channel_multiplier=0,
                       allow_small_or_imprecise_dtypes=True).then_inc(kidx_in, 1)
                g.wait_ge(qt_in, 2)

                def one(n, u, known):
                    if live(known, 0, PAIRS):
                        if known is None or known >= 2:
                            g.wait_ge(e_ps, n - 1)
                        g.tensor_copy(q[u][:, :], QT[:, bass.ds(n, 1), :].rearrange("p a m -> p (a m)")
                                      ).then_inc(q_in, 1)

                run_steps(g, PAIRS, 1, 2, one)

            @block.tensor
            def _(pe):
                pe.wait_ge(w_in, 16 * 11)
                pe.matmul(PS[:, 7, 0:128], w[:, 0, :], w[:, 1, :], start=True, stop=True).then_inc(fold_ps, 1)
                for k in range(2):
                    for j in range(4):
                        mm = pe.transpose(PS[:, k, 128 * j:128 * j + 128], XN[:, 4 * k + j, :], ident[:, :])
                    mm.then_inc(xt_ps, 1)
                pe.wait_ge(fold_in, 1)
                for k in range(2):
                    pe.wait_ge(xt_in, k + 1)
                    pe.matmul(PS[:, 2 + k, :], fold[:, :], flat(XT)[:, 512 * k:512 * k + 512],
                              start=True, stop=True).then_inc(qt_ps, 1)
                pe.wait_ge(qt_in, 2)

                def one(n, u, known):
                    if live(known, 0, PAIRS):
                        pe.wait_ge(cT_in[u], 8 * (n - u) + 16)
                        pe.wait_ge(q_in, n + 1)
                        for b in range(BANKS):
                            if known is None or known >= 2:
                                pe.wait_ge(pt_in, 3 * n - 5 + b)
                            for par in range(2):
                                mm = pe.matmul(PS[HALF * par:HALF * par + HALF, 3 * u + b, 0:BANK_KEYS],
                                               q[u][:, HALF * par:HALF * par + HALF],
                                               cT[u][:, par, BANK_KEYS * b:BANK_KEYS * b + BANK_KEYS],
                                               start=True, stop=True)
                        mm.then_inc(e_ps, 1)
                    if live(known, 1, PAIRS):
                        pe.wait_ge(p_in, n)
                        for b in range(BANKS):
                            for j in range(4):
                                at = CHUNK * (4 * b + j)
                                mm = pe.transpose(PS[0:CHUNK, 3 * (1 - u) + b, 128 * j:128 * j + 128],
                                                  P[1 - u][:, at:at + CHUNK], ident[:, :])
                            mm.then_inc(pt_ps, 1)
                    if live(known, 0, PAIRS):
                        pe.wait_ge(cnt_in, n + 1)
                        if known is None or known >= 2:
                            pe.wait_ge(o_in, n - 1)
                        pe.matmul(PS[:, 6 + u, 256:257], self.pick[:, :], small[:, COUNT, u:u + 1],
                                  start=True, stop=True).then_inc(len_ps, 1)
                    if live(known, 1, PAIRS):
                        pe.wait_ge(pt_in, 3 * n)
                        pe.wait_ge(c_in[1 - u], 8 * (n - 1 - (1 - u)) + 16)
                        for par in range(2):
                            for k in range(CHUNKS):
                                mm = pe.matmul(PS[HALF * par:HALF * par + HALF, 7 - u, 0:D],
                                               PT[1 - u][:, 128 * k + HALF * par:128 * k + HALF * par + HALF],
                                               c[1 - u][:, CHUNKS * par + k, :],
                                               start=(k == 0), stop=(k == CHUNKS - 1))
                        mm.then_inc(o_ps, 1)

                run_steps(pe, PAIRS, 1, 2, one)
                pe.wait_ge(o_in, PAIRS)
                for k in range(2):
                    for j in range(4):
                        mm = pe.transpose(PS[:, k, 128 * j:128 * j + 128], ON[:, 4 * k + j, :], ident[:, :])
                    mm.then_inc(ot_ps, 1)
                for k in range(2):
                    pe.wait_ge(ot_in, k + 1)
                    for j in range(4):
                        mm = pe.matmul(PS[:, 2 + k, 128 * j:128 * j + 128], QT[:, 4 * k + j, :], w[:, 2, :],
                                       start=True, stop=True)
                    mm.then_inc(z_ps, 1)
                pe.wait_ge(n2_ready, 1)
                for k in range(2):
                    for j in range(4):
                        mm = pe.transpose(PS[:, 4 + k, 128 * j:128 * j + 128], XN[:, 4 * k + j, :], ident[:, :])
                    mm.then_inc(xt_ps, 1)
                for k in range(2):
                    pe.wait_ge(xt_in, k + 3)
                    pe.matmul(PS[:, 6 + k, :], w[:, 3, :], flat(XT)[:, 512 * k:512 * k + 512],
                              start=True, stop=True).then_inc(h_ps, 1)
                for k in range(2):
                    pe.wait_ge(h_in, k + 1)
                    for j in range(4):
                        pe.matmul(PS[:, k, 128 * j:128 * j + 128], QT[:, 4 * k + j, :], w[:, 4, :],
                                  start=True, stop=False)
                        mm = pe.matmul(PS[:, k, 128 * j:128 * j + 128], self.ones[0:1, :], row[0:1, :],
                                       start=False, stop=True)
                    mm.then_inc(y_ps, 1)

            @block.scalar
            def _(act):
                act.wait_ge(fold_ps, 1)
                act.copy(fold[:, :], PS[:, 7, 0:128]).then_inc(fold_in, 1)
                for k in range(2):
                    act.wait_ge(xt_ps, k + 1)
                    act.copy(flat(XT)[:, 512 * k:512 * k + 512], PS[:, k, :]).then_inc(xt_in, 1)
                for k in range(2):
                    act.wait_ge(qt_ps, k + 1)
                    act.copy(flat(QT)[:, 512 * k:512 * k + 512], PS[:, 2 + k, :]).then_inc(qt_in, 1)

                def one(n, u, known):
                    if live(known, 1, PAIRS):
                        if known is None or known >= 3:
                            act.wait_ge(o_ps, n - 2)
                        for b in range(BANKS):
                            act.wait_ge(pt_ps, 3 * n - 2 + b)
                            act.copy(PT[1 - u][:, 512 * b:512 * b + 512], PS[0:CHUNK, 3 * (1 - u) + b, :]
                                     ).then_inc(pt_in, 1)
                    if live(known, 0, PAIRS):
                        act.wait_ge(top_in, n + 1)
                        if known is None or known >= 2:
                            act.wait_ge(o_in, n - 1)
                        act.activation(P[u][:, :], P[u][:, :], ACT.Exp, bias=small[:, BIAS, u:u + 1],
                                       scale=scale, accum_out=small[:, SUM, u:u + 1]).then_inc(p_in, 1)

                run_steps(act, PAIRS, 1, 2, one)
                for k in range(2):
                    act.wait_ge(ot_ps, k + 1)
                    act.copy(flat(QT)[:, 512 * k:512 * k + 512], PS[:, k, :]).then_inc(ot_in, 1)
                for k in range(2):
                    act.wait_ge(xt_ps, k + 3)
                    act.copy(flat(XT)[:, 512 * k:512 * k + 512], PS[:, 4 + k, :]).then_inc(xt_in, 1)
                for k in range(2):
                    act.wait_ge(h_ps, k + 1)
                    act.activation(flat(QT)[:, 512 * k:512 * k + 512], PS[:, 6 + k, :], ACT.Relu,
                                   bias=col[:, 0:1]).then_inc(h_in, 1)

            @block.vector
            def _(v):
                chain = Chain(v, step)
                v.wait_ge(ffn_in, 48)
                self.dequantised_weights(v, chain, W, WQ, wmax)
                before = chain.n
                v.wait_ge(kidx_in, 1)

                def one(n, u, known):
                    if live(known, 0, PAIRS):
                        chain.base, chain.n = n + before, 0
                        E = PS[:, 3 * u:3 * u + 3, 0:BANK_KEYS]
                        Pv = P[u][:, :].rearrange("p (b k) -> p b k", b=BANKS)
                        v.wait_ge(e_ps, n + 1)
                        if known is None or known >= 2:
                            v.wait_ge(pt_ps, 3 * n - 3)
                        v.tensor_scalar(Pv, E, 0.0, None, ALU.not_equal, ALU.add,
                                        accum_out=small[:, COUNT, u:u + 1]).then_inc(cnt_in, 1)
                        v.wait_ge(len_ps, n + 1)
                        v.tensor_copy(small[:, LENGTH, u:u + 1], PS[:, 6 + u, 256:257]).then_inc(len_in, 1)
                        v.wait_ge(len_in, n + 1)
                        if known is None or known >= 1:
                            v.wait_ge(top_in, n)
                        v.tensor_scalar(pad[:, :], kidx[:, :], small[:, LENGTH, u:u + 1], NEG,
                                        ALU.is_ge, ALU.mult).then_inc(pad_in, 1)
                        v.wait_ge(pad_in, n + 1)
                        settle(v, self.passed)
                        chain(v.tensor_tensor_reduce(
                            Pv, E, pad[:, :].rearrange("p (b k) -> p b k", b=BANKS), 1.0, -3.4e38, ALU.add,
                            ALU.max, small[:, TOP, u:u + 1]))
                        v.tensor_scalar(small[:, BIAS, u:u + 1], small[:, TOP, u:u + 1], -scale, None,
                                        ALU.mult).then_inc(top_in, 1)
                    if live(known, 1, PAIRS):
                        v.wait_ge(o_ps, n)
                        v.reciprocal(small[:, INV, 1 - u:2 - u], small[:, SUM, 1 - u:2 - u]).then_inc(inv_in, 1)
                        v.wait_ge(inv_in, n)
                        v.tensor_scalar(ON[:, bass.ds(n - 1, 1), :].rearrange("p a d -> p (a d)"),
                                        PS[:, 7 - u, 0:D], small[:, INV, 1 - u:2 - u], None,
                                        ALU.mult).then_inc(o_in, 1)

                run_steps(v, PAIRS, 1, 2, one)
                chain.base, chain.n = PAIRS + before, 0
                v.wait_ge(z_ps, 2)
                Z = PS[:, 2:4, :].rearrange("p a (j m) -> p (a j) m", m=128)
                chain(v.tensor_tensor(ON[:, :, :], Z, XN[:, :, :], ALU.add))
                layer_norm(v, chain, XN, ON, ln, 1e-5)
                v.wait_ge(w_in, 16 * 11)
                self.affine(v, chain, XN, gb[:, 0, :, :])
                v.sem_inc(n2_ready, 1)
                v.wait_ge(y_ps, 2)
                Z = PS[:, 0:2, :].rearrange("p a (j m) -> p (a j) m", m=128)
                chain(v.tensor_tensor(ON[:, :, :], Z, XN[:, :, :], ALU.add))
                layer_norm(v, chain, XN, ON, ln, 1e-5)
                self.affine(v, chain, XN, gb[:, 1, :, :])
                chain(v.tensor_tensor(X[:, :, :], X[:, :, :], XN[:, :, :], ALU.add))

    def dequantised_weights(self, v, chain, W, WQ, wmax):
        wb = W[:, :].rearrange("p (n k) -> p n k", k=QBLOCK)
        wq = WQ[:, :].rearrange("p (n k) -> p n k", k=QBLOCK)
        wide = lambda r: r.unsqueeze(2).to_broadcast([128, 3 * FFN1 // QBLOCK, QBLOCK])
        chain(v.tensor_reduce(wmax[:, 0, :], wb, X_AXIS, ALU.max, apply_absolute_value=True))
        chain(v.tensor_scalar(wmax[:, 1, :], wmax[:, 0, :], 1.0 / 7.0, 1e-12, ALU.mult, ALU.max))
        chain(v.reciprocal(wmax[:, 2, :], wmax[:, 1, :]))
        chain(v.tensor_tensor(wq, wb, wide(wmax[:, 2, :]), ALU.mult))
        chain(v.tensor_scalar(WQ[:, :], WQ[:, :], ROUND, -ROUND, ALU.add, ALU.add))
        chain(v.tensor_tensor(wq, wq, wide(wmax[:, 1, :]), ALU.mult))

    def quantised_ffn(self, WQ):
        nc, t = self.nc, self.t
        self.stage = "l1q"
        X, XN, ident, PS = self.X, self.XN, self.ident, self.PS
        with ExitStack() as ctx:
            XT = self.sb(ctx, "XT", [128, PAIRS * 128])
            WT = self.sb(ctx, "WT", [128, 3 * GCHUNKS, 128])
            U = self.sb(ctx, "U", [128, GCHUNKS * 1024])
            Gt = self.sb(ctx, "G", [128, GCHUNKS * 1024])
            SG = self.sb(ctx, "SG", [128, GCHUNKS * 1024])
            red = self.sb(ctx, "red", [128, 4])
            top1 = self.sb(ctx, "top1", [1, 1])
            ln = self.norm_scratch(ctx)
            (wt_ps, wt_in, x_ready, xt_ps, xt_in, top_in, top_ps, top1_in, all_ps, u_ps,
             u_in, g_ps, g_in, sig_ready, sig_in, o_ready, z_ps, step) = (self.sem(ctx, n) for n in (
                 "wt_ps", "wt_in", "x_ready", "xt_ps", "xt_in", "top_in", "top_ps",
                 "top1_in", "all_ps", "u_ps", "u_in", "g_ps", "g_in", "sig_ready", "sig_in", "o_ready",
                 "z_ps", "step"))
            block = ctx.enter_context(nc.Block())

            @block.tensor
            def _(pe):
                tops = [0]

                def spread():
                    n = tops[0] = tops[0] + 1
                    pe.wait_ge(top_in, n)
                    pe.transpose(PS[0:1, 7, 0:128], red[:, 0:1], ident[:, :]).then_inc(top_ps, 1)
                    pe.wait_ge(top1_in, n)
                    pe.matmul(PS[:, 7, 256:257], self.ones[0:1, :], top1[0:1, 0:1], start=True,
                              stop=True).then_inc(all_ps, 1)

                for k in range(3):
                    for j in range(GCHUNKS):
                        at = FFN1 * k + 128 * j
                        mm = pe.transpose(PS[:, k, 128 * j:128 * j + 128], WQ[:, at:at + 128], ident[:, :])
                    mm.then_inc(wt_ps, 1)
                spread()
                pe.wait_ge(x_ready, 1)
                for k in range(2):
                    for j in range(4):
                        mm = pe.transpose(PS[:, 4 + k, 128 * j:128 * j + 128], XN[:, 4 * k + j, :], ident[:, :])
                    mm.then_inc(xt_ps, 1)
                pe.wait_ge(wt_in, 3)
                pe.wait_ge(xt_in, 2)
                for k, done in ((1, g_ps), (0, u_ps)):
                    for b in range(6):
                        if done is u_ps:
                            pe.wait_ge(g_in, b + 1)
                        pe.matmul(PS[:, b, :], WT[:, GCHUNKS * k + b // 2, :],
                                  XT[:, 512 * (b % 2):512 * (b % 2) + 512], start=True, stop=True
                                  ).then_inc(done, 1)
                for _ in range(4):
                    spread()
                pe.wait_ge(o_ready, 1)
                for p in range(PAIRS):
                    for j in range(GCHUNKS):
                        mm = pe.matmul(PS[:, p // 4, 128 * (p % 4):128 * (p % 4) + 128],
                                       U[:, 1024 * j + 128 * p:1024 * j + 128 * p + 128],
                                       WT[:, 2 * GCHUNKS + j, :], start=(j == 0), stop=(j == GCHUNKS - 1))
                    if p % 4 == 3:
                        mm.then_inc(z_ps, 1)

            @block.scalar
            def _(act):
                for k in range(3):
                    act.wait_ge(wt_ps, k + 1)
                    act.copy(WT[:, GCHUNKS * k:GCHUNKS * k + GCHUNKS, :].rearrange("p c m -> p (c m)"),
                             PS[:, k, 0:FFN1]).then_inc(wt_in, 1)
                for k in range(2):
                    act.wait_ge(xt_ps, k + 1)
                    act.copy(XT[:, 512 * k:512 * k + 512], PS[:, 4 + k, :]).then_inc(xt_in, 1)
                for dst, ps, done in ((Gt, g_ps, g_in), (U, u_ps, u_in)):
                    for b in range(6):
                        act.wait_ge(ps, b + 1)
                        act.copy(dst[:, 512 * b:512 * b + 512], PS[:, b, :]).then_inc(done, 1)
                act.wait_ge(sig_ready, 1)
                act.activation(SG[:, :], Gt[:, :], ACT.Sigmoid).then_inc(sig_in, 1)

            @block.vector
            def _(v):
                chain = Chain(v, step)
                tops = [0]

                def scale_of(a):
                    n = tops[0] = tops[0] + 1
                    v.tensor_reduce(red[:, 0:1], a, X_AXIS, ALU.max, apply_absolute_value=True).then_inc(top_in, 1)
                    v.wait_ge(top_ps, n)
                    v.tensor_reduce(top1[0:1, 0:1], PS[0:1, 7, 0:128], X_AXIS, ALU.max).then_inc(top1_in, 1)
                    v.wait_ge(all_ps, n)
                    chain(v.tensor_scalar(red[:, 1:2], PS[:, 7, 256:257], 1.0 / 32767.0, 1e-12, ALU.mult, ALU.max))
                    chain(v.reciprocal(red[:, 2:3], red[:, 1:2]))

                def qdq(a):
                    chain(v.tensor_scalar(a, a, red[:, 2:3], ROUND, ALU.mult, ALU.add))
                    chain(v.tensor_scalar(a, a, -ROUND, red[:, 1:2], ALU.add, ALU.mult))

                layer_norm(v, chain, XN, X, ln, 1e-5)
                xn = XN[:, :, :].rearrange("p t d -> p (t d)")
                chain(v.tensor_scalar(xn, xn, self.rowmask[:, 0:1], None, ALU.mult))
                scale_of(xn)
                qdq(xn)
                v.sem_inc(x_ready, 1)
                v.wait_ge(g_in, 6)
                scale_of(Gt[:, :])
                qdq(Gt[:, :])
                v.sem_inc(sig_ready, 1)
                v.wait_ge(u_in, 6)
                scale_of(U[:, :])
                qdq(U[:, :])
                v.wait_ge(sig_in, 1)
                chain(v.tensor_scalar(SG[:, :], SG[:, :], 65536.0, ROUND, ALU.mult, ALU.add))
                chain(v.tensor_scalar(SG[:, :], SG[:, :], -ROUND, 65535.0, ALU.add, ALU.min))
                chain(v.scalar_tensor_tensor(out=Gt[:, :], in0=SG[:, :], scalar=1.0 / 65536.0, in1=Gt[:, :],
                                             op0=ALU.mult, op1=ALU.mult))
                scale_of(Gt[:, :])
                qdq(Gt[:, :])
                chain(v.tensor_tensor(U[:, :], Gt[:, :], U[:, :], ALU.mult))
                scale_of(U[:, :])
                qdq(U[:, :])
                v.sem_inc(o_ready, 1)
                v.wait_ge(z_ps, 2)
                chain(v.tensor_tensor(X[:, :, :], PS[:, 0:2, :].rearrange("p a (j m) -> p (a j) m", m=128),
                                      X[:, :, :], ALU.add))

    def unit_ffn(self):
        nc, t = self.nc, self.t
        self.stage = "l2f"
        X, XN, ident, PS = self.X, self.XN, self.ident, self.PS
        JJ = INNER // 2
        with ExitStack() as ctx:
            XT = self.sb(ctx, "XT", [128, PAIRS * 128])
            win = self.sb(ctx, "win", [128, 2, M2])
            bin_ = self.sb(ctx, "bin", [128, 1])
            cols = self.sb(ctx, "cols", [128, 3, JJ])
            wout = self.sb(ctx, "wout", [128, D])
            b2 = self.sb(ctx, "b2", [M2, 1])
            bout = self.sb(ctx, "bout", [D, 1])
            ccol = self.sb(ctx, "ccol", [D, 1])
            ZT = self.sb(ctx, "ZT", [128, PAIRS * 128])
            WO = self.sb(ctx, "WO", [128, JJ, D])
            S = self.sb(ctx, "S", [128, PAIRS * 128])
            H = self.sb(ctx, "H", [128, JJ, PAIRS * 128])
            ln = self.norm_scratch(ctx)
            zt_ps, zt_in = self.sem(ctx, "zt_ps"), self.sem(ctx, "zt_in")
            (w_in, c_ps, c_in, xn_ready, xt_ps, xt_in, s_ps, s_in, h_in, wo_in, z_ps, step) = (
                self.sem(ctx, n) for n in ("w_in", "c_ps", "c_in", "xn_ready", "xt_ps", "xt_in", "s_ps",
                                           "s_in", "h_in", "wo_in", "z_ps", "step"))
            block = ctx.enter_context(nc.Block())
            DMAS = 14

            @block.sync
            def _(sp):
                for par in range(2):
                    rows = slice(M2 * par, M2 * par + M2)
                    sp.dma_start(win[:, par, :], t["L2_ffn_Win"]).then_inc(w_in, 16)
                    sp.dma_start(bin_[rows, :], t["L2_ffn_bin_"].unsqueeze(1)).then_inc(w_in, 16)
                    sp.dma_start(wout[rows, :], t["L2_ffn_Wout"]).then_inc(w_in, 16)
                    for k, name in enumerate(("W1", "b1", "W2")):
                        sp.dma_start(cols[rows, k, :], t[f"L2_ffn_{name}_halves"][par]).then_inc(w_in, 16)
                sp.dma_start(b2[:, :], t["L2_ffn_b2"].unsqueeze(1)).then_inc(w_in, 16)
                sp.dma_start(bout[:, :], t["L2_ffn_bout"].unsqueeze(1)).then_inc(w_in, 16)

            @block.tensor
            def _(pe):
                pe.wait_ge(w_in, 16 * DMAS)
                pe.matmul(PS[:, 7, 0:1], wout[0:M2, :], b2[:, :], start=True, stop=True).then_inc(c_ps, 1)
                for k in range(2):
                    pe.wait_ge(xn_ready, k + 1)
                    for j in range(4):
                        mm = pe.transpose(PS[:, k, 128 * j:128 * j + 128], XN[:, 4 * k + j, :], ident[:, :])
                    mm.then_inc(xt_ps, 1)
                for k in range(2):
                    pe.wait_ge(xt_in, k + 1)
                    pe.matmul(PS[:, 2 + k, :], win[:, :, :].rearrange("p a m -> p (a m)"),
                              XT[:, 512 * k:512 * k + 512], start=True, stop=True).then_inc(s_ps, 1)
                pe.wait_ge(wo_in, 1)
                for j in range(JJ):
                    pe.wait_ge(h_in, j + 1)
                    for k in range(2):
                        mm = pe.matmul(PS[:, 4 + k, :], WO[:, j, :], H[:, j, 512 * k:512 * k + 512],
                                       start=(j == 0), stop=(j == JJ - 1))
                        if j == JJ - 1:
                            mm.then_inc(zt_ps, 1)
                for k in range(2):
                    pe.wait_ge(zt_in, k + 1)
                    for j in range(4):
                        at = 512 * k + 128 * j
                        mm = pe.transpose(PS[:, k, 128 * j:128 * j + 128], ZT[:, at:at + 128], ident[:, :])
                    mm.then_inc(z_ps, 1)

            @block.scalar
            def _(act):
                for k in range(2):
                    act.wait_ge(xt_ps, k + 1)
                    act.copy(XT[:, 512 * k:512 * k + 512], PS[:, k, :]).then_inc(xt_in, 1)
                act.wait_ge(w_in, 16 * DMAS)
                for k in range(2):
                    act.wait_ge(s_ps, k + 1)
                    act.activation(S[:, 512 * k:512 * k + 512], PS[:, 2 + k, :], ACT.Identity,
                                   bias=bin_[:, 0:1]).then_inc(s_in, 1)
                act.wait_ge(s_in, 2)
                for j in range(JJ):
                    act.activation(H[:, j, :], S[:, :], ACT.Relu, bias=cols[:, 1, j:j + 1],
                                   scale=cols[:, 0, j:j + 1]).then_inc(h_in, 1)
                act.wait_ge(c_in, 1)
                for k in range(2):
                    act.wait_ge(zt_ps, k + 1)
                    act.activation(ZT[:, 512 * k:512 * k + 512], PS[:, 4 + k, :], ACT.Identity,
                                   bias=ccol[:, 0:1]).then_inc(zt_in, 1)

            @block.vector
            def _(v):
                chain = Chain(v, step)
                layer_norm(v, chain, XN, X, ln, 1e-5, xn_ready)
                v.wait_ge(w_in, 16 * DMAS)
                for j in range(JJ):
                    last = v.tensor_scalar(WO[:, j, :], wout[:, :], cols[:, 2, j:j + 1], None, ALU.mult)
                last.then_inc(wo_in, 1)
                v.wait_ge(c_ps, 1)
                v.tensor_tensor(ccol[:, :], PS[:, 7, 0:1], bout[:, :], ALU.add).then_inc(c_in, 1)
                v.wait_ge(z_ps, 2)
                chain(v.tensor_tensor(X[:, :, :], PS[:, 0:2, :].rearrange("p a (j m) -> p (a j) m", m=128),
                                      X[:, :, :], ALU.add))

    def head_attention(self, stage, J, weights, padded):
        t = self.t
        self.stage = stage
        scale = 1.0 / float(np.sqrt(float(J)))
        with ExitStack() as whole:
            QP = self.sb(whole, "QP", [128, BATCH * ROWS])
            CH = self.sb(whole, "CH", [128, HEADS, D])
            cout = self.sb(whole, "cout", [128, 1])
            wx = self.sb(whole, "wx", [128, D])
            QH = [self.sb(whole, f"QH{s}", [128, 128], F32R) for s in range(2)]
            QL = [self.sb(whole, f"QL{s}", [128, 128], F32R) for s in range(2)]
            heads = lambda g: QP[:, :].rearrange("p (b h q) -> p b h q", b=BATCH, h=HEADS)[
                :, 8 * g:8 * g + 8]
            cT, c = self.sb(whole, "cT", [128, KEYS]), self.sb(whole, "c", [CHUNK, CHUNKS * D])
            raw_in = self.sem(whole, "raw_in")

            def load_context(sp, b):
                one = bass.ds(b, 1)
                sp.dma_start(cT[:, :], t["ctxT"][one].rearrange("a d k -> d (a k)")).then_inc(raw_in, 16)
                sp.dma_start(c[:, :].rearrange("k (c d) -> k c d", d=D), t["ctx_1024"][one].rearrange(
                    "a (c k) d -> k (a c) d", k=CHUNK)).then_inc(raw_in, 16)

            early = whole.enter_context(ExitStack())
            XT = self.sb(early, "XT", [128, PAIRS, 128])
            tokens = lambda g: XT[:, 4 * g:4 * g + 4, :].rearrange("p t (a q) -> p (t a) q", a=2)[
                :, :, 0:TOK]
            self.fold_heads(stage, J, scale, QP, CH, cout, wx, XT, heads, tokens, weights, load_context)
            if weights.get("query_out") is None:
                early.close()
            self.attend(stage, QP, QH, QL, padded, cT, c, raw_in, load_context)
            self.combine(stage, QP, CH, cout, wx, XT, heads, tokens, weights)

    def fold_heads(self, stage, J, scale, QP, CH, cout, wx, XT, heads, tokens, weights,
                   load_context):
        nc, t = self.nc, self.t
        self.stage = stage + "fold"
        X, XN, ident, PS = self.X, self.XN, self.ident, self.PS
        query_out = weights.get("query_out")
        with ExitStack() as ctx:
            names = ("wqT", "wkT", "wvT") if weights["wkT"] is not weights["wvT"] else ("wqT", "wkT")
            W = {k: self.sb(ctx, k, [J, HEADS, D]) for k in (*names, "wo")}
            if "wvT" not in W:
                W["wvT"] = W["wkT"]
            wide = self.sb(ctx, "wide", [128, 4, HEADS * J])
            bo = self.sb(ctx, "bo", [128, 1])
            cq = self.sb(ctx, "cq", [128, HEADS])
            BHh, BHl = (self.sb(ctx, n, [128, HEADS * D], F32R) for n in ("BHh", "BHl"))
            XTh, XTl = (self.sb(ctx, n, [128, PAIRS, 128], F32R) for n in ("XTh", "XTl"))
            ln = self.norm_scratch(ctx)
            (w_in, b_ps, b_in, wide_in, c_in, xn_ready, xt_ps, xt_in, q_ps, q_in, step, ql_ps) = (
                self.sem(ctx, n) for n in ("w_in", "b_ps", "b_in", "wide_in", "c_in", "xn_ready", "xt_ps",
                                           "xt_in", "q_ps", "q_in", "step", "ql_ps"))
            bl_in, xtl_in = self.sem(ctx, "bl_in"), self.sem(ctx, "xtl_in")
            flat = lambda a: a[:, :, :].rearrange("p t m -> p (t m)")
            DMAS = len(names) + 1 + (1 if query_out is not None else 0)
            block = ctx.enter_context(nc.Block())

            @block.sync
            def _(sp):
                for k in names:
                    sp.dma_start(W[k][:, :, :], weights[k].rearrange("(h j) d -> j h d", j=J)).then_inc(w_in, 16)
                sp.dma_start(W["wo"][:, :, :], weights["wo"].rearrange("(h j) d -> j h d", j=J)).then_inc(w_in, 16)
                if query_out is not None:
                    sp.dma_start(wx[:, :], query_out).then_inc(w_in, 16)
                sp.dma_start(bo[:, :], weights["bo"].unsqueeze(1)).then_inc(wide_in, 16)
                for k, name in enumerate(("wk", "woT", "bq", "bv")):
                    src = weights[name] if k < 2 else weights[name].partition_broadcast(128)
                    sp.dma_start(wide[:, k, :], src).then_inc(wide_in, 16)
                load_context(sp, 0)

            @block.tensor
            def _(pe):
                pe.wait_ge(w_in, 16 * DMAS)
                for k, (a, b) in enumerate((("wqT", "wkT"), ("wvT", "wo"))):
                    for g in range(4):
                        for j in range(4):
                            h = 4 * g + j
                            mm = pe.matmul(PS[:, 4 * (k % 2) + g, 128 * j:128 * j + 128], W[a][:, h, :],
                                           W[b][:, h, :], start=True, stop=True)
                        mm.then_inc(b_ps, 1)
                pe.wait_ge(bl_in, 4)
                for k in range(2):
                    pe.wait_ge(xn_ready, k + 1)
                    for j in range(4):
                        mm = pe.transpose(PS[:, 2 + k, 128 * j:128 * j + 128], XN[:, 4 * k + j, :], ident[:, :])
                    mm.then_inc(xt_ps, 1)
                pe.wait_ge(xtl_in, 2)
                pe.wait_ge(bl_in, 4)
                pe.wait_ge(b_in, 8)
                for n in range(2 * HEADS):
                    if n >= 4:
                        pe.wait_ge(q_in if n % 2 == 0 else ql_ps, (n - 4) // 2 + 1)
                    cols, q = slice(D * (n // 2), D * (n // 2) + D), PS[:, 4 + n % 4, 0:HALF_TOK]
                    high, low = (x[:, 4 * (n % 2):4 * (n % 2) + 4, :].rearrange("p t (a q) -> p (t a) q", a=2)[
                        :, :, 0:TOK] for x in (XTh, XTl))
                    pe.matmul(q, BHh[:, cols], high, start=True, stop=False)
                    pe.matmul(q, BHh[:, cols], low, start=False, stop=False)
                    pe.matmul(q, BHl[:, cols], high, start=False, stop=True).then_inc(q_ps, 1)

            def queries(eng, n):
                dst = heads(n % 2)[:, :, n // 2, :]
                src = PS[:, 4 + n % 4, 0:HALF_TOK].rearrange("p (b q) -> p b q", q=TOK)
                return dst, src

            @block.scalar
            def _(act):
                for g in range(8):
                    act.wait_ge(b_ps, g + 1)
                    dst = (BHh[:, 512 * g:512 * g + 512] if g < 4
                           else CH[:, 4 * (g - 4):4 * (g - 4) + 4, :].rearrange("p h d -> p (h d)"))
                    act.copy(dst, PS[:, g, :]).then_inc(b_in, 1)
                for k in range(2):
                    act.wait_ge(xt_ps, k + 1)
                    if query_out is not None:
                        act.copy(flat(XT)[:, 512 * k:512 * k + 512], PS[:, 2 + k, :])
                    act.copy(flat(XTh)[:, 512 * k:512 * k + 512], PS[:, 2 + k, :]).then_inc(xt_in, 1)
                act.wait_ge(c_in, 1)
                for n in range(0, 2 * HEADS, 2):
                    act.wait_ge(q_ps, n + 1)
                    dst, src = queries(act, n)
                    act.activation(dst, src, ACT.Identity, bias=cq[:, n // 2:n // 2 + 1], scale=scale
                                   ).then_inc(q_in, 1)

            @block.vector
            def _(v):
                chain = Chain(v, step)
                layer_norm(v, chain, XN, X, ln, 1e-5, xn_ready)
                v.wait_ge(wide_in, 16 * 5)
                for k in range(2):
                    chain(v.tensor_tensor(wide[:, k, :], wide[:, k, :], wide[:, 2 + k, :], ALU.mult))
                chain(v.tensor_reduce(cq[:, :], wide[:, 0, :].rearrange("p (h j) -> p h j", j=J), X_AXIS,
                                      ALU.add))
                chain(v.tensor_scalar(cq[:, :], cq[:, :], scale, None, ALU.mult))
                chain(v.tensor_reduce(cout[:, :], wide[:, 1, :], X_AXIS, ALU.add))
                chain(v.tensor_tensor(cout[:, :], cout[:, :], bo[:, :], ALU.add))
                v.sem_inc(c_in, 1)
                for g in range(4):
                    v.wait_ge(b_in, g + 1)
                    v.tensor_tensor(BHl[:, 512 * g:512 * g + 512], PS[:, g, :],
                                    BHh[:, 512 * g:512 * g + 512], ALU.subtract).then_inc(bl_in, 1)
                for k in range(2):
                    v.wait_ge(xt_in, k + 1)
                    v.tensor_tensor(flat(XTl)[:, 512 * k:512 * k + 512], PS[:, 2 + k, :],
                                    flat(XTh)[:, 512 * k:512 * k + 512], ALU.subtract).then_inc(xtl_in, 1)
                for n in range(1, 2 * HEADS, 2):
                    v.wait_ge(q_ps, n + 1)
                    dst, src = queries(v, n)
                    v.tensor_scalar(dst, src, scale, cq[:, n // 2:n // 2 + 1], ALU.mult, ALU.add
                                    ).then_inc(ql_ps, 1)

    def attend(self, stage, QP, QH, QL, padded, cT, c, raw_in, load_context):
        nc, t = self.nc, self.t
        self.stage = stage + "att"
        ident, PS = self.ident, self.PS
        with ExitStack() as ctx:
            cTh, cTl = (self.sb(ctx, n, [128, 2, KEYS], F32R) for n in ("cTh", "cTl"))
            cc = self.sb(ctx, "cc", [CHUNK, 2, CHUNKS, 2, D], F32R)
            P = [self.sb(ctx, f"P{s}", [128, KEYS]) for s in range(2)]
            PT = self.sb(ctx, "PT", [CHUNK, CHUNKS, 4, 2, 128], F32R)
            PLACE = (0, 1, 2, 3, 0, 1, 2, 3, 1, 0, 2, 1, 3, 2)
            O = self.sb(ctx, "O", [128, D])
            o_low = self.sem(ctx, "o_low")
            top = self.sb(ctx, "top", [128, 2])
            neg = self.sb(ctx, "neg", [128, 2])
            total, inv = self.sb(ctx, "total", [128, 2]), self.sb(ctx, "inv", [128, 2])
            (high_in, split, split_step, q_in, e_ps, top_in, p_in, pn_in, pt_ps, hi_in, lo_in,
             o_ps, pair_in, single_in, inv_in, mask_in) = (self.sem(ctx, n) for n in (
                 "high_in", "split", "split_step", "q_in", "e_ps", "top_in", "p_in",
                 "pn_in", "pt_ps", "hi_in", "lo_in", "o_ps", "pair_in", "single_in", "inv_in", "mask_in"))
            if padded:
                mask8 = [self.sb(ctx, f"mask8_{s}", [128, KEYS], U8) for s in range(2)]
                maskb = self.sb(ctx, "maskb", [128, KEYS])
                mask_raw, topped = [self.sem(ctx, f"mask_raw{s}") for s in range(2)], self.sem(ctx, "topped")
            block = ctx.enter_context(nc.Block())
            LAG, BT = 4, BATCH_TILES
            UNROLL = 2 * BT

            def group_end(j):
                return j if j % BT == BT - 1 else j + 1 - (j % BT) % 2

            def place_free(j):
                before = next(m for m in range(j - 1, -2 * UNROLL, -1) if PLACE[m % UNROLL] == PLACE[j])
                turn = before // UNROLL * UNROLL
                return j - (group_end(before - turn) + turn)

            def piece(u):
                r = (u - 3) % BT
                if r == BT - 1:
                    return 3, 1, range(CHUNKS)
                return (3, 2, range(CHUNKS // 2)) if r % 2 == 0 else (4, 2, range(CHUNKS // 2, CHUNKS))

            def bank(j):
                return 6 + (j % BT) // 2 % 2

            @block.sync
            def _(sp):
                def load(b, u, known):
                    if not live(known, 0, BATCH):
                        return
                    if known is None or known >= 1:
                        sp.wait_ge(split, 4 * b)
                        load_context(sp, b)
                    if padded:
                        if known is None or known >= 2:
                            sp.wait_ge(mask_in, b - 1)
                            settle(sp, self.passed)
                        sp.dma_start(mask8[u][:, :], t["mask"][bass.ds(b, 1)].to_broadcast([128, KEYS])
                                     ).then_inc(mask_raw[u], 16)

                run_steps(sp, BATCH, 2, 2, load)

            @block.gpsimd
            def _(g):
                chain = Chain(g, split_step)

                def low_part(slot, k):
                    half = slice(k % 2 * (KEYS // 2), (k % 2 + 1) * (KEYS // 2))
                    some = slice(k % 2 * (CHUNKS // 2), (k % 2 + 1) * (CHUNKS // 2))
                    if k < 2:
                        ins = g.tensor_tensor(cTl[:, slot, half], cT[:, half], cTh[:, slot, half], ALU.subtract)
                    else:
                        ins = g.tensor_tensor(cc[:, slot, some, 1, :],
                                              c[:, :].rearrange("k (c d) -> k c d", d=D)[:, some, :],
                                              cc[:, slot, some, 0, :], ALU.subtract)
                    ins.then_inc(split, 1)

                def split_query(n, m):
                    if not (isinstance(n, int) and n < 2):
                        g.wait_ge(e_ps, n - 1)
                    at = bass.ds(n * 128, 128)
                    chain(g.tensor_copy(QH[m % 2][:, :], QP[:, at]))
                    settle(g, self.passed)
                    g.tensor_tensor(QL[m % 2][:, :], QP[:, at], QH[m % 2][:, :], ALU.subtract).then_inc(q_in, 1)

                def batch_pair(i, last):
                    for s in range(2):
                        b = 2 * i + s
                        chain.base = BT * b
                        chain.n = 0
                        more = not (last and s == 1)
                        for j in range(BT):
                            split_query(BT * b + j, BT * s + j)
                            if more and 2 <= j <= 5:
                                g.wait_ge(high_in, 2 * b + (3 if j < 4 else 4))
                                settle(g, self.passed)
                                low_part(1 - s, j - 2)

                batch_pair(0, False)
                with g.Fori(1, BATCH // 2 - 1) as i:
                    batch_pair(i, False)
                batch_pair(BATCH // 2 - 1, True)

            @block.tensor
            def _(pe):
                def one(n, u, known):
                    s, s1 = u % 2, (u + 1) % 2
                    if live(known, 0, TILES):
                        pe.wait_ge(split, n // BT * 4 + 2)
                        pe.wait_ge(q_in, n + 1)
                        slot = u // BT
                        for g in range(BANKS):
                            if known is None or known >= 2:
                                pe.wait_ge(lo_in, 3 * n - 5 + g)
                            keys = slice(BANK_KEYS * g, BANK_KEYS * g + BANK_KEYS)
                            e = PS[:, 3 * s + g, 0:BANK_KEYS]
                            pe.matmul(e, QH[s][:, :], cTh[:, slot, keys], start=True, stop=False)
                            pe.matmul(e, QH[s][:, :], cTl[:, slot, keys], start=False, stop=False)
                            mm = pe.matmul(e, QL[s][:, :], cTh[:, slot, keys], start=False, stop=True)
                        mm.then_inc(e_ps, 1)
                    if live(known, 1, TILES):
                        pe.wait_ge(pn_in, n)
                        for g in range(BANKS):
                            for j in range(4):
                                at = CHUNK * (4 * g + j)
                                mm = pe.transpose(PS[0:CHUNK, 3 * s1 + g, 128 * j:128 * j + 128],
                                                  P[s1][:, at:at + CHUNK], ident[:, :])
                            mm.then_inc(pt_ps, 1)
                    back, size, chunks = piece(u)
                    if live(known, back, TILES):
                        a = (u - back) % UNROLL
                        slot = a // BT
                        if chunks[0] == 0:
                            pe.wait_ge(split, (n - back) // BT * 4 + 4)
                            pe.wait_ge(lo_in, 3 * (n - back + size))
                            if a % BT == 2:
                                if known is None or known - back >= BT:
                                    pe.wait_ge(single_in, (n - back) // BT)
                            elif a % BT > 2:
                                pe.wait_ge(pair_in, (n - back) // BT * (BT - 1) + a % BT - 2)
                            elif known is None or known - back >= BT:
                                pe.wait_ge(pair_in, (n - back) // BT * (BT - 1))
                        out = PS[:, bank(a), 0:256]
                        for k in chunks:
                            first, last = k == 0, k == CHUNKS - 1
                            if size == 1:
                                at = PLACE[a]
                                pe.matmul(out, cc[:, slot, k, 0, :],
                                          PT[:, k, at, :, :].rearrange("k h r -> k (h r)"),
                                          start=first, stop=False)
                                mm = pe.matmul(out[:, 0:128], cc[:, slot, k, 1, :], PT[:, k, at, 0, :],
                                               start=False, stop=last)
                            else:
                                lo, hi = sorted((PLACE[a], PLACE[a + 1]))
                                two = slice(lo, hi + 1, hi - lo)
                                out2 = out.rearrange("p (a r) -> p a r", a=2)
                                pe.matmul(out2, cc[:, slot, k, 0, :], PT[:, k, two, 0, :], start=first,
                                          stop=False)
                                pe.matmul(out2, cc[:, slot, k, 1, :], PT[:, k, two, 0, :], start=False,
                                          stop=False)
                                mm = pe.matmul(out2, cc[:, slot, k, 0, :], PT[:, k, two, 1, :], start=False,
                                               stop=last)
                        if chunks[-1] == CHUNKS - 1:
                            mm.then_inc(o_ps, size)

                run_steps(pe, TILES, LAG, UNROLL, one)

            @block.scalar
            def _(act):
                def high_part(slot, k):
                    if k == 0:
                        act.copy(cTh[:, slot, :], cT[:, :]).then_inc(high_in, 1)
                    else:
                        act.copy(cc[:, slot, :, 0, :], c[:, :].rearrange("k (c d) -> k c d", d=D)
                                 ).then_inc(high_in, 1)

                def mask_part(slot):
                    act.activation(maskb[:, :], mask8[slot][:, :], ACT.Copy, scale=NEG).then_inc(mask_in, 1)

                def one(n, u, known):
                    s, s1 = u % 2, (u + 1) % 2
                    if live(known, 1, TILES):
                        u1 = (u - 1) % UNROLL
                        if known is None or known - 1 - place_free(u1) >= 0:
                            act.wait_ge(o_ps, n - place_free(u1))
                        for g in range(BANKS):
                            act.wait_ge(pt_ps, 3 * n - 2 + g)
                            act.copy(PT[:, 4 * g:4 * g + 4, PLACE[u1], 0, :],
                                     PS[0:CHUNK, 3 * s1 + g, :].rearrange("k (c r) -> k c r", r=128)
                                     ).then_inc(hi_in, 1)
                    if live(known, 0, TILES):
                        act.wait_ge(top_in, n + 1)
                        if known is None or known >= 2:
                            act.wait_ge(pt_ps, 3 * n - 3)
                            act.wait_ge(inv_in, n - 1)
                        Pv = P[s][:, :].rearrange("p (b k) -> p b k", b=BANKS)
                        act.activation(Pv, Pv if padded else PS[:, 3 * s:3 * s + 3, 0:BANK_KEYS], ACT.Exp,
                                       bias=neg[:, s:s + 1], accum_out=total[:, s:s + 1]).then_inc(p_in, 1)
                    back, size, chunks = piece(u)
                    if size == 2 and chunks[0] > 0 and live(known, back, TILES):
                        a = (u - back) % UNROLL
                        act.wait_ge(o_ps, n - back + 2)
                        if PLACE[a] < PLACE[a + 1]:
                            act.copy(QP[:, bass.ds((n - back) * 128, 256)], PS[:, bank(a), 0:256]
                                     ).then_inc(pair_in, 2)
                        else:
                            for j in range(2):
                                act.copy(QP[:, bass.ds((n - back + j) * 128, 128)],
                                         PS[:, bank(a), 128 - 128 * j:256 - 128 * j]).then_inc(pair_in, 1)

                    if padded and u % BT == BT - 1 and (known is None or known < TILES - BT):
                        act.wait_ge(mask_raw[1 - u // BT], n // UNROLL * 16 + 16 + 16 * (u // BT))
                        settle(act, self.passed)
                        mask_part(1 - u // BT)
                    if u % BT in (1, 3) and (known is None or known < TILES - BT):
                        b = n // BT
                        act.wait_ge(raw_in, 32 * b + 64)
                        if known is None or known >= BT:
                            act.wait_ge(e_ps if u % BT == 1 else o_ps, BT * b)
                        high_part(1 - u // BT, u % BT // 2)

                act.wait_ge(raw_in, 32)
                if padded:
                    act.wait_ge(mask_raw[0], 16)
                    mask_part(0)
                high_part(0, 0)
                high_part(0, 1)
                run_steps(act, TILES, LAG, UNROLL, one, peeled=1)

            @block.vector
            def _(v):
                def one(n, u, known):
                    s, s1 = u % 2, (u + 1) % 2
                    if live(known, 0, TILES):
                        v.wait_ge(e_ps, n + 1)
                        E = PS[:, 3 * s:3 * s + 3, 0:BANK_KEYS]
                        if padded:
                            v.wait_ge(mask_in, n // BT + 1)
                            if known is None or known >= 2:
                                v.wait_ge(pt_ps, 3 * n - 3)
                            settle(v, self.passed)
                            v.tensor_tensor_reduce(
                                P[s][:, :].rearrange("p (b k) -> p b k", b=BANKS), E,
                                maskb[:, :].rearrange("p (b k) -> p b k", b=BANKS), 1.0, -3.4e38, ALU.add,
                                ALU.max, top[:, s:s + 1]).then_inc(topped, 1)
                            v.wait_ge(topped, n + 1)
                            v.tensor_scalar(neg[:, s:s + 1], top[:, s:s + 1], -1.0, None,
                                            ALU.mult).then_inc(top_in, 1)
                        else:
                            v.tensor_reduce(neg[:, s:s + 1], E, XY_AXES, ALU.max, negate=True
                                            ).then_inc(top_in, 1)
                    if live(known, 1, TILES):
                        at = PLACE[(u - 1) % UNROLL]
                        for g in range(BANKS):
                            v.wait_ge(hi_in, 3 * n - 2 + g)
                            v.tensor_tensor(PT[:, 4 * g:4 * g + 4, at, 1, :],
                                            PS[0:CHUNK, 3 * s1 + g, :].rearrange("k (c r) -> k c r", r=128),
                                            PT[:, 4 * g:4 * g + 4, at, 0, :], ALU.subtract
                                            ).then_inc(lo_in, 1)
                    if live(known, 0, TILES):
                        v.wait_ge(p_in, n + 1)
                        v.reciprocal(inv[:, s:s + 1], total[:, s:s + 1]).then_inc(inv_in, 1)
                        v.wait_ge(inv_in, n + 1)
                        v.tensor_scalar(P[s][:, :], P[s][:, :], inv[:, s:s + 1], None, ALU.mult
                                        ).then_inc(pn_in, 1)
                    back, size, chunks = piece(u)
                    if size == 1 and live(known, back, TILES):
                        v.wait_ge(o_ps, n - back + 1)
                        low = PS[:, bank((u - back) % UNROLL), 128:256]
                        v.tensor_copy(O[:, :], low).then_inc(o_low, 1)
                        v.wait_ge(o_low, (n - back + 1) // BT)
                        v.tensor_tensor(QP[:, bass.ds((n - back) * 128, 128)],
                                        PS[:, bank((u - back) % UNROLL), 0:128], O[:, :], ALU.add
                                        ).then_inc(single_in, 1)

                v.wait_ge(high_in, 1)
                v.tensor_tensor(cTl[:, 0, :], cT[:, :], cTh[:, 0, :], ALU.subtract).then_inc(split, 2)
                v.wait_ge(high_in, 2)
                v.tensor_tensor(cc[:, 0, :, 1, :], c[:, :].rearrange("k (c d) -> k c d", d=D),
                                cc[:, 0, :, 0, :], ALU.subtract).then_inc(split, 2)
                run_steps(v, TILES, LAG, UNROLL, one)

    def combine(self, stage, QP, CH, cout, wx, XT, heads, tokens, weights):
        nc, t = self.nc, self.t
        self.stage = stage + "comb"
        X, XN, ident, PS = self.X, self.XN, self.ident, self.PS
        query_out, norm = weights.get("query_out"), weights.get("norm")
        with ExitStack() as ctx:
            ZT = self.sb(ctx, "ZT", [128, BATCH, HALF])
            gb = self.sb(ctx, "gb", [128, 2, D])
            Z = self.sb(ctx, "Z", [128, PAIRS, D])
            ln = self.norm_scratch(ctx)
            gb_in, zeroed, zt_ps, zt_in, z_ps, step = (self.sem(ctx, n) for n in (
                "gb_in", "zeroed", "zt_ps", "zt_in", "z_ps", "step"))
            block = ctx.enter_context(nc.Block())

            if norm:
                @block.sync
                def _(sp):
                    for k in range(2):
                        sp.dma_start(gb[:, k, :], norm[k].partition_broadcast(128)).then_inc(gb_in, 16)

            @block.tensor
            def _(pe):
                for g in range(2):
                    z = PS[:, g, 0:HALF_TOK]
                    if query_out is not None:
                        pe.matmul(z, wx[:, :], tokens(g), start=True, stop=False)
                    for h in range(HEADS):
                        mm = pe.matmul(z, CH[:, h, :], heads(g)[:, :, h, :],
                                       start=(h == 0 and query_out is None), stop=(h == HEADS - 1))
                    mm.then_inc(zt_ps, 1)
                for g in range(2):
                    pe.wait_ge(zt_in, g + 1)
                    for j in range(4):
                        mm = pe.transpose(PS[:, 2 + g, 128 * j:128 * j + 128],
                                          ZT[:, 8 * g + 2 * j:8 * g + 2 * j + 2, :].rearrange("p a q -> p (a q)"),
                                          ident[:, :])
                    mm.then_inc(z_ps, 1)

            @block.scalar
            def _(act):
                act.wait_ge(zeroed, 1)
                for g in range(2):
                    act.wait_ge(zt_ps, g + 1)
                    act.activation(ZT[:, 8 * g:8 * g + 8, 0:TOK],
                                   PS[:, g, 0:HALF_TOK].rearrange("p (b q) -> p b q", q=TOK), ACT.Identity,
                                   bias=cout[:, 0:1]).then_inc(zt_in, 1)

            @block.vector
            def _(v):
                chain = Chain(v, step)
                v.memset(ZT[:, :, :], 0.0).then_inc(zeroed, 1)
                v.wait_ge(z_ps, 2)
                zp = PS[:, 2:4, :].rearrange("p a (j m) -> p (a j) m", m=128)
                if norm:
                    chain(v.tensor_copy(Z[:, :, :], zp))
                    layer_norm(v, chain, XN, Z, ln, 1e-5)
                    v.wait_ge(gb_in, 32)
                    self.affine(v, chain, XN, gb)
                    chain(v.tensor_tensor(X[:, :, :], X[:, :, :], XN[:, :, :], ALU.add))
                else:
                    chain(v.tensor_tensor(X[:, :, :], zp, X[:, :, :], ALU.add))

    def store(self):
        nc = self.nc
        self.stage = "store"
        with ExitStack() as ctx:
            stored = self.sem(ctx, "stored")
            block = ctx.enter_context(nc.Block())

            @block.sync
            def _(sp):
                ov = self.out.rearrange("(t two) q d -> two q t d", two=2)
                for par in range(2):
                    sp.dma_start(ov[par], self.X[HALF * par:HALF * par + TOK, :, :]).then_inc(stored, 16)
                sp.wait_ge(stored, 32)


def xattn_ffn_layers(nc, t, out):
    k = Kernel(nc, t, out)
    with ExitStack() as ctx:
        k.stage = "all"
        k.passed = k.sem(ctx, "passed")
        k.X, k.XN = k.sb(ctx, "X", [128, PAIRS, D]), k.sb(ctx, "XN", [128, PAIRS, D])
        k.ident, k.blockm, k.valid, k.pick, k.ones = (
            k.sb(ctx, n, [128, 128]) for n in ("ident", "blockm", "valid", "pick", "ones"))
        k.rowmask, k.kidx = k.sb(ctx, "rowmask", [128, 1]), k.sb(ctx, "kidx", [128, HALF])
        k.e_idx = k.sb(ctx, "e_idx", [128, PAIRS, EXPERTS])
        k.PS = ctx.enter_context(nc.psum_tensor("PS", [128, 8, 512], F32))
        k.setup()
        k.local_attention("l0a", False)
        k.moe("l0f", False)
        k.layer_one()
        k.clear_used()
        k.head_attention("l2", 64, dict(
            wqT=t["WqT2"], wkT=t["WvT2"], wvT=t["WvT2"], wo=t["L2_xattn_Wfc"][0:HEADS * 64],
            query_out=t["L2_xattn_Wfc"][HEADS * 64:HEADS * 64 + D], wk=t["L2_xattn_Wv"],
            woT=t["WoT2"], bq=t["L2_xattn_bq"], bv=t["L2_xattn_bv"], bo=t["L2_xattn_bfc"],
            norm=(t["L2_xattn_gamma"], t["L2_xattn_beta"])),
            padded=False)
        k.unit_ffn()
        k.clear_used()
        k.head_attention("l3", 8, dict(
            wqT=t["WqT3"], wkT=t["WkT3"], wvT=t["WvT3"], wo=t["L3_xattn_W_O"],
            wk=t["L3_xattn_W_K"], woT=t["WoT3"], bq=t["L3_xattn_b_Q"], bv=t["L3_xattn_b_V"],
            bo=t["L3_xattn_b_O"]), padded=True)
        k.moe("l3f", True)
        k.store()


def arrange(inputs):
    a = {k: np.ascontiguousarray(v) for k, v in inputs.items() if k != "mask_BxS2_bk0"}
    a["mask"] = np.ascontiguousarray(inputs["mask_BxS2_bk0"])

    def turned(name, axes=(1, 0)):
        return np.ascontiguousarray(np.transpose(a[name], axes))

    a["ctxT"] = turned("ctx_1024", (0, 2, 1))
    a["WqT0"] = turned("L0_xattn_Wq")
    a["Wq1T"], a["Wk1T"] = turned("L1_xattn_Wq1"), turned("L1_xattn_Wk1")
    a["Wq2T"], a["Wk2T"] = turned("L1_xattn_Wq2"), turned("L1_xattn_Wk2")
    a["WqT2"], a["WvT2"] = turned("L2_xattn_Wq"), turned("L2_xattn_Wv")
    a["WqT3"], a["WkT3"], a["WvT3"] = (turned(f"L3_xattn_W_{x}") for x in "QKV")
    a["WoT2"] = np.ascontiguousarray(a["L2_xattn_Wfc"][0:HEADS * 64].T)
    a["WoT3"] = turned("L3_xattn_W_O")
    for name in ("W1", "b1", "W2"):
        a[f"L2_ffn_{name}_halves"] = np.ascontiguousarray(
            np.transpose(a[f"L2_ffn_{name}"].reshape(M2, INNER // 2, 2), (2, 0, 1)))
    for n, name in ((0, "L0_ffn_b1"), (3, "L3_ffn_b1")):
        a[f"b1T{n}"] = np.ascontiguousarray(
            np.transpose(a[name].reshape(EXPERTS, FCHUNKS, 128), (2, 0, 1)))
    return a


def kernel(**inputs):
    import concourse.bacc as _bacc
    from concourse.bass_utils import run_bass_kernel_spmd as _run

    nc = _bacc.Bacc("TRN2", target_bir_lowering=False, num_devices=1)
    arrays = {f"in_{k}": v for k, v in arrange(inputs).items()}
    t = {k[3:]: nc.dram_tensor(k, v.shape, mybir.dt.from_np(v.dtype), kind="ExternalInput").ap()
         for k, v in arrays.items()}
    out = nc.dram_tensor("out_x", (BATCH, TOK, D), F32, kind="ExternalOutput").ap()
    xattn_ffn_layers(nc, t, out)
    r = _run(nc, [arrays], core_ids=[0])
    return r.results[0]["out_x"]
```
